# Optimizing a Trainium2 kernel written in Bass

```python
import numpy as np
import jax
import jax.numpy as jnp

def _softmax(x, axis=-1):
    return jax.nn.softmax(x, axis=axis)

def _gelu(x):
    return jax.nn.gelu(x, approximate=True)

def _silu(x):
    return jax.nn.silu(x)

def _sigmoid(x):
    return jax.nn.sigmoid(x)

def _layernorm(x, axis=-1, eps=1e-05):
    m = jnp.mean(x, axis=axis, keepdims=True)
    v = jnp.var(x, axis=axis, keepdims=True)
    return (x - m) / jnp.sqrt(v + eps)

def _scatter_add(tgt, idx, src, axis=0):
    return tgt.at[idx].add(src)

def _segment_sum(src, seg, n):
    return jax.ops.segment_sum(src, seg, n)
kernel_name = 'mk_recurrent_d2_jaxref_r8_210c05'

def setup_inputs(seed: int=0):
    np.random.seed(seed)
    _w = jnp.asarray

    def _L0_attn_setup():
        import jax, jax.numpy as jnp
        import numpy as np
        B, S, D = (2, 256, 256)
        H, HD = (16, 128)
        RD = 64
        ND = HD - RD
        KVR, QR = (64, 128)
        BASE = 10000.0
        NEG = -1e+30

        def _apply_rope(t):
            half = RD // 2
            seq = t.shape[2]
            inv_freq = 1.0 / BASE ** (jnp.arange(half, dtype=jnp.float32) / half)
            ang = jnp.arange(seq, dtype=jnp.float32)[:, None] * inv_freq
            cos, sin = (jnp.cos(ang), jnp.sin(ang))
            t1, t2 = (t[..., :half], t[..., half:])
            return jnp.concatenate([t1 * cos - t2 * sin, t1 * sin + t2 * cos], axis=-1)
        key = jax.random.key(seed)
        ks = jax.random.split(key, 9)

        def w(k, shape):
            return jax.random.normal(k, shape, jnp.float32) * shape[0] ** (-0.5)
        return {'x': jax.random.normal(ks[0], (B, S, D), jnp.float32), 'Wq_down': w(ks[1], (D, QR)), 'Wq_up': w(ks[2], (QR, H * ND)), 'Wq_rope': w(ks[3], (QR, H * RD)), 'Wkv_down': w(ks[4], (D, KVR)), 'Wk_up': w(ks[5], (KVR, H * ND)), 'Wk_rope': w(ks[6], (D, H * RD)), 'Wv_up': w(ks[7], (KVR, H * HD)), 'Wo': w(ks[8], (H * HD, D))}
    _L0_attn_in = _L0_attn_setup()

    def _L0_ffn_setup():
        import jax, jax.numpy as jnp
        import numpy as np
        H = 256
        I = 256
        E_ROUTED = 7
        NS = 1
        TOPK = 2
        TEMP = 1.0

        def _moe_forward(x, Wr, br, gate_bias, Wup, bup, Wgate, bgate, Wdown, bdown, Wsu, bsu, Wsg, bsg, Wsd, bsd):
            B, S, _ = x.shape
            xt = x.reshape(-1, H)
            N = xt.shape[0]
            gate = (xt @ Wr + br) / TEMP
            bias_gate = gate + gate_bias
            _, ids = jax.lax.top_k(bias_gate, TOPK)
            sel_logits = jnp.take_along_axis(gate, ids, axis=-1)
            masked = jnp.full_like(gate, -jnp.inf)
            masked = masked.at[jnp.arange(N)[:, None], ids].set(sel_logits)
            probs = jax.nn.softmax(masked, axis=-1)
            u = jnp.einsum('nh,ehi->eni', xt, Wup) + bup[:, None, :]
            g = jax.nn.silu(jnp.einsum('eni,eij->enj', u, Wgate) + bgate[:, None, :]) * u
            eo = jnp.einsum('enj,ejh->enh', g, Wdown) + bdown[:, None, :]
            out = jnp.einsum('ne,enh->nh', probs, eo)
            su = (xt @ Wsu + bsu).reshape(N, NS, I)
            sg = jax.nn.silu(su @ Wsg + bsg) * su
            so = (sg @ Wsd + bsd).sum(axis=1)
            out = out + so
            return out.reshape(B, S, H)
        key = jax.random.key(seed)
        ks = jax.random.split(key, 20)
        s = lambda fan_in: 1.0 / np.sqrt(fan_in)
        inp = {'x': jax.random.normal(ks[0], (4, 128, H), dtype=jnp.float32), 'Wr': jax.random.normal(ks[1], (H, E_ROUTED), jnp.float32) * s(H), 'br': jax.random.normal(ks[2], (E_ROUTED,), jnp.float32) * s(H), 'gate_bias': jnp.zeros((E_ROUTED,), jnp.float32), 'Wup': jax.random.normal(ks[3], (E_ROUTED, H, I), jnp.float32) * s(H), 'bup': jax.random.normal(ks[4], (E_ROUTED, I), jnp.float32) * s(H), 'Wgate': jax.random.normal(ks[5], (E_ROUTED, I, I), jnp.float32) * s(I), 'bgate': jax.random.normal(ks[6], (E_ROUTED, I), jnp.float32) * s(I), 'Wdown': jax.random.normal(ks[7], (E_ROUTED, I, H), jnp.float32) * s(I), 'bdown': jax.random.normal(ks[8], (E_ROUTED, H), jnp.float32) * s(I), 'Wsu': jax.random.normal(ks[9], (H, NS * I), jnp.float32) * s(H), 'bsu': jax.random.normal(ks[10], (NS * I,), jnp.float32) * s(H), 'Wsg': jax.random.normal(ks[11], (I, I), jnp.float32) * s(I), 'bsg': jax.random.normal(ks[12], (I,), jnp.float32) * s(I), 'Wsd': jax.random.normal(ks[13], (I, H), jnp.float32) * s(I), 'bsd': jax.random.normal(ks[14], (H,), jnp.float32) * s(I)}
        return inp
    _L0_ffn_in = _L0_ffn_setup()

    def _L1_attn_setup():
        import jax, jax.numpy as jnp
        import numpy as np
        DIM = 256
        H = 16
        KV_RANK = 64
        Q_RANK = 192
        ROPE = 64
        NOPE = 128
        VD = 128
        THETA = 500000.0
        EPS = 1e-06
        B, T = (1, 256)
        QK_HEAD = NOPE + ROPE

        def _rmsnorm(x, w):
            rms = jax.lax.rsqrt(jnp.mean(x * x, axis=-1, keepdims=True) + EPS)
            return x * rms * w

        def _rope_tables(t):
            inv_freq = 1.0 / THETA ** (jnp.arange(0, ROPE, 2, dtype=jnp.float32) / ROPE)
            pos = jnp.arange(t, dtype=jnp.float32)
            angles = jnp.outer(pos, inv_freq)
            return (jnp.cos(angles), jnp.sin(angles))

        def _apply_rope(x, cos, sin):
            b, t, h, d = x.shape
            xp = x.reshape(b, t, h, d // 2, 2)
            even, odd = (xp[..., 0], xp[..., 1])
            c = cos.reshape(1, t, 1, d // 2)
            s = sin.reshape(1, t, 1, d // 2)
            out = jnp.stack((even * c - odd * s, odd * c + even * s), axis=-1)
            return out.reshape(b, t, h, d)
        key = jax.random.key(seed)
        ks = jax.random.split(key, 7)
        s = 0.02
        x = jax.random.normal(ks[0], (B, T, DIM), dtype=jnp.float32)
        w_q_down = jax.random.normal(ks[1], (Q_RANK, DIM), dtype=jnp.float32) * s
        q_norm_w = jnp.ones((Q_RANK,), dtype=jnp.float32)
        w_q_up = jax.random.normal(ks[2], (H * (NOPE + ROPE), Q_RANK), dtype=jnp.float32) * s
        w_kv_down = jax.random.normal(ks[3], (KV_RANK + ROPE, DIM), dtype=jnp.float32) * s
        kv_norm_w = jnp.ones((KV_RANK,), dtype=jnp.float32)
        w_kv_up = jax.random.normal(ks[4], (H * (NOPE + VD), KV_RANK), dtype=jnp.float32) * s
        w_o = jax.random.normal(ks[5], (DIM, H * VD), dtype=jnp.float32) * s
        return {'x': x, 'w_q_down': w_q_down, 'q_norm_w': q_norm_w, 'w_q_up': w_q_up, 'w_kv_down': w_kv_down, 'kv_norm_w': kv_norm_w, 'w_kv_up': w_kv_up, 'w_o': w_o}
    _L1_attn_in = _L1_attn_setup()

    def _L1_ffn_setup():
        import jax, jax.numpy as jnp
        import numpy as np
        HIDDEN = 256
        INTER = 688
        LUT_SIZE = 16

        def _ghost_linear(x, idx, lut):
            w = lut[idx]
            return jnp.einsum('bsh,oh->bso', x, w)
        key = jax.random.key(seed)
        k_x, k_lut, k_g, k_u, k_d = jax.random.split(key, 5)
        x = jax.random.normal(k_x, (2, 512, HIDDEN), dtype=jnp.float32)
        lut = jax.random.normal(k_lut, (LUT_SIZE,), dtype=jnp.float32) * 0.02
        gate_idx = jax.random.randint(k_g, (INTER, HIDDEN), 0, LUT_SIZE, dtype=jnp.int32)
        up_idx = jax.random.randint(k_u, (INTER, HIDDEN), 0, LUT_SIZE, dtype=jnp.int32)
        down_idx = jax.random.randint(k_d, (HIDDEN, INTER), 0, LUT_SIZE, dtype=jnp.int32)
        return {'x': x, 'lut': lut, 'gate_idx': gate_idx, 'up_idx': up_idx, 'down_idx': down_idx}
    _L1_ffn_in = _L1_ffn_setup()
    _d = {'L0_attn_x': _L0_attn_in['x'], 'L0_attn_Wq_down': _L0_attn_in['Wq_down'], 'L0_attn_Wq_up': _L0_attn_in['Wq_up'], 'L0_attn_Wq_rope': _L0_attn_in['Wq_rope'], 'L0_attn_Wkv_down': _L0_attn_in['Wkv_down'], 'L0_attn_Wk_up': _L0_attn_in['Wk_up'], 'L0_attn_Wk_rope': _L0_attn_in['Wk_rope'], 'L0_attn_Wv_up': _L0_attn_in['Wv_up'], 'L0_attn_Wo': _L0_attn_in['Wo'], 'L0_ffn_Wr': _L0_ffn_in['Wr'], 'L0_ffn_br': _L0_ffn_in['br'], 'L0_ffn_gate_bias': _L0_ffn_in['gate_bias'], 'L0_ffn_Wup': _L0_ffn_in['Wup'], 'L0_ffn_bup': _L0_ffn_in['bup'], 'L0_ffn_Wgate': _L0_ffn_in['Wgate'], 'L0_ffn_bgate': _L0_ffn_in['bgate'], 'L0_ffn_Wdown': _L0_ffn_in['Wdown'], 'L0_ffn_bdown': _L0_ffn_in['bdown'], 'L0_ffn_Wsu': _L0_ffn_in['Wsu'], 'L0_ffn_bsu': _L0_ffn_in['bsu'], 'L0_ffn_Wsg': _L0_ffn_in['Wsg'], 'L0_ffn_bsg': _L0_ffn_in['bsg'], 'L0_ffn_Wsd': _L0_ffn_in['Wsd'], 'L0_ffn_bsd': _L0_ffn_in['bsd'], 'L1_attn_w_q_down': _L1_attn_in['w_q_down'], 'L1_attn_q_norm_w': _L1_attn_in['q_norm_w'], 'L1_attn_w_q_up': _L1_attn_in['w_q_up'], 'L1_attn_w_kv_down': _L1_attn_in['w_kv_down'], 'L1_attn_kv_norm_w': _L1_attn_in['kv_norm_w'], 'L1_attn_w_kv_up': _L1_attn_in['w_kv_up'], 'L1_attn_w_o': _L1_attn_in['w_o'], 'L1_ffn_lut': _L1_ffn_in['lut'], 'L1_ffn_gate_idx': _L1_ffn_in['gate_idx'], 'L1_ffn_up_idx': _L1_ffn_in['up_idx'], 'L1_ffn_down_idx': _L1_ffn_in['down_idx']}
    _x0 = _d['L0_attn_x']
    _d['L0_attn_x'] = jax.random.normal(jax.random.fold_in(jax.random.key(seed), 1), (4, 512, 256), dtype=_x0.dtype)
    del _x0
    return _d

def reference(L0_attn_x, L0_attn_Wq_down, L0_attn_Wq_up, L0_attn_Wq_rope, L0_attn_Wkv_down, L0_attn_Wk_up, L0_attn_Wk_rope, L0_attn_Wv_up, L0_attn_Wo, L0_ffn_Wr, L0_ffn_br, L0_ffn_gate_bias, L0_ffn_Wup, L0_ffn_bup, L0_ffn_Wgate, L0_ffn_bgate, L0_ffn_Wdown, L0_ffn_bdown, L0_ffn_Wsu, L0_ffn_bsu, L0_ffn_Wsg, L0_ffn_bsg, L0_ffn_Wsd, L0_ffn_bsd, L1_attn_w_q_down, L1_attn_q_norm_w, L1_attn_w_q_up, L1_attn_w_kv_down, L1_attn_kv_norm_w, L1_attn_w_kv_up, L1_attn_w_o, L1_ffn_lut, L1_ffn_gate_idx, L1_ffn_up_idx, L1_ffn_down_idx):

    def _L0_attn_ref(x, Wq_down, Wq_up, Wq_rope, Wkv_down, Wk_up, Wk_rope, Wv_up, Wo):
        import jax, jax.numpy as jnp
        import numpy as np
        B, S, D = (2, 256, 256)
        H, HD = (16, 128)
        RD = 64
        ND = HD - RD
        KVR, QR = (64, 128)
        BASE = 10000.0
        NEG = -1e+30

        def _apply_rope(t):
            half = RD // 2
            seq = t.shape[2]
            inv_freq = 1.0 / BASE ** (jnp.arange(half, dtype=jnp.float32) / half)
            ang = jnp.arange(seq, dtype=jnp.float32)[:, None] * inv_freq
            cos, sin = (jnp.cos(ang), jnp.sin(ang))
            t1, t2 = (t[..., :half], t[..., half:])
            return jnp.concatenate([t1 * cos - t2 * sin, t1 * sin + t2 * cos], axis=-1)
        b, s, _ = x.shape
        q_lat = x @ Wq_down
        q_nope = (q_lat @ Wq_up).reshape(b, s, H, ND).transpose(0, 2, 1, 3)
        q_pe = (q_lat @ Wq_rope).reshape(b, s, H, RD).transpose(0, 2, 1, 3)
        kv_lat = x @ Wkv_down
        k_nope = (kv_lat @ Wk_up).reshape(b, s, H, ND).transpose(0, 2, 1, 3)
        k_pe = (x @ Wk_rope).reshape(b, s, H, RD).transpose(0, 2, 1, 3)
        v = (kv_lat @ Wv_up).reshape(b, s, H, HD).transpose(0, 2, 1, 3)
        q_pe = _apply_rope(q_pe)
        k_pe = _apply_rope(k_pe)
        q = jnp.concatenate([q_nope, q_pe], axis=-1)
        k = jnp.concatenate([k_nope, k_pe], axis=-1)
        scale = HD ** (-0.5)
        scores = jnp.einsum('bhqd,bhkd->bhqk', q, k) * scale
        causal = jnp.tril(jnp.ones((s, s), dtype=bool))
        scores = jnp.where(causal, scores, NEG)
        attn = jax.nn.softmax(scores, axis=-1)
        out = jnp.einsum('bhqk,bhkd->bhqd', attn, v)
        out = out.transpose(0, 2, 1, 3).reshape(b, s, H * HD)
        return out @ Wo

    def _L0_ffn_ref(x, Wr, br, gate_bias, Wup, bup, Wgate, bgate, Wdown, bdown, Wsu, bsu, Wsg, bsg, Wsd, bsd):
        import jax, jax.numpy as jnp
        import numpy as np
        H = 256
        I = 256
        E_ROUTED = 7
        NS = 1
        TOPK = 2
        TEMP = 1.0

        def _moe_forward(x, Wr, br, gate_bias, Wup, bup, Wgate, bgate, Wdown, bdown, Wsu, bsu, Wsg, bsg, Wsd, bsd):
            B, S, _ = x.shape
            xt = x.reshape(-1, H)
            N = xt.shape[0]
            gate = (xt @ Wr + br) / TEMP
            bias_gate = gate + gate_bias
            _, ids = jax.lax.top_k(bias_gate, TOPK)
            sel_logits = jnp.take_along_axis(gate, ids, axis=-1)
            masked = jnp.full_like(gate, -jnp.inf)
            masked = masked.at[jnp.arange(N)[:, None], ids].set(sel_logits)
            probs = jax.nn.softmax(masked, axis=-1)
            u = jnp.einsum('nh,ehi->eni', xt, Wup) + bup[:, None, :]
            g = jax.nn.silu(jnp.einsum('eni,eij->enj', u, Wgate) + bgate[:, None, :]) * u
            eo = jnp.einsum('enj,ejh->enh', g, Wdown) + bdown[:, None, :]
            out = jnp.einsum('ne,enh->nh', probs, eo)
            su = (xt @ Wsu + bsu).reshape(N, NS, I)
            sg = jax.nn.silu(su @ Wsg + bsg) * su
            so = (sg @ Wsd + bsd).sum(axis=1)
            out = out + so
            return out.reshape(B, S, H)
        return _moe_forward(x, Wr, br, gate_bias, Wup, bup, Wgate, bgate, Wdown, bdown, Wsu, bsu, Wsg, bsg, Wsd, bsd)

    def _L1_attn_ref(x, w_q_down, q_norm_w, w_q_up, w_kv_down, kv_norm_w, w_kv_up, w_o):
        import jax, jax.numpy as jnp
        import numpy as np
        DIM = 256
        H = 16
        KV_RANK = 64
        Q_RANK = 192
        ROPE = 64
        NOPE = 128
        VD = 128
        THETA = 500000.0
        EPS = 1e-06
        B, T = (1, 256)
        QK_HEAD = NOPE + ROPE

        def _rmsnorm(x, w):
            rms = jax.lax.rsqrt(jnp.mean(x * x, axis=-1, keepdims=True) + EPS)
            return x * rms * w

        def _rope_tables(t):
            inv_freq = 1.0 / THETA ** (jnp.arange(0, ROPE, 2, dtype=jnp.float32) / ROPE)
            pos = jnp.arange(t, dtype=jnp.float32)
            angles = jnp.outer(pos, inv_freq)
            return (jnp.cos(angles), jnp.sin(angles))

        def _apply_rope(x, cos, sin):
            b, t, h, d = x.shape
            xp = x.reshape(b, t, h, d // 2, 2)
            even, odd = (xp[..., 0], xp[..., 1])
            c = cos.reshape(1, t, 1, d // 2)
            s = sin.reshape(1, t, 1, d // 2)
            out = jnp.stack((even * c - odd * s, odd * c + even * s), axis=-1)
            return out.reshape(b, t, h, d)
        b, t, _ = x.shape
        c_q = _rmsnorm(x @ w_q_down.T, q_norm_w)
        q = (c_q @ w_q_up.T).reshape(b, t, H, NOPE + ROPE)
        q_nope, q_rope = (q[..., :NOPE], q[..., NOPE:])
        kv = x @ w_kv_down.T
        c_kv = kv[..., :KV_RANK]
        k_rope_raw = kv[..., KV_RANK:].reshape(b, t, 1, ROPE)
        cos, sin = _rope_tables(t)
        q_rope = _apply_rope(q_rope, cos, sin)
        k_rope = _apply_rope(k_rope_raw, cos, sin)
        kv_up = (_rmsnorm(c_kv, kv_norm_w) @ w_kv_up.T).reshape(b, t, H, NOPE + VD)
        k_nope, v = (kv_up[..., :NOPE], kv_up[..., NOPE:])
        q_full = jnp.concatenate((q_nope, q_rope), axis=-1)
        k_full = jnp.concatenate((k_nope, jnp.broadcast_to(k_rope, (b, t, H, ROPE))), axis=-1)
        scale = 1.0 / np.sqrt(QK_HEAD)
        scores = jnp.einsum('bqhd,bkhd->bhqk', q_full, k_full) * scale
        causal = jnp.tril(jnp.ones((t, t), dtype=bool))
        scores = jnp.where(causal[None, None], scores, -jnp.inf)
        attn = jax.nn.softmax(scores, axis=-1)
        out = jnp.einsum('bhqk,bkhd->bqhd', attn, v).reshape(b, t, H * VD)
        return out @ w_o.T

    def _L1_ffn_ref(x, lut, gate_idx, up_idx, down_idx):
        import jax, jax.numpy as jnp
        import numpy as np
        HIDDEN = 256
        INTER = 688
        LUT_SIZE = 16

        def _ghost_linear(x, idx, lut):
            w = lut[idx]
            return jnp.einsum('bsh,oh->bso', x, w)
        gate = _ghost_linear(x, gate_idx, lut)
        up = _ghost_linear(x, up_idx, lut)
        h = jax.nn.silu(gate) * up
        return _ghost_linear(h, down_idx, lut)
    x = L0_attn_x
    xn = _layernorm(x, axis=-1)
    s = _L0_attn_ref(xn, L0_attn_Wq_down, L0_attn_Wq_up, L0_attn_Wq_rope, L0_attn_Wkv_down, L0_attn_Wk_up, L0_attn_Wk_rope, L0_attn_Wv_up, L0_attn_Wo)
    g = _silu(_L0_ffn_ref(xn, L0_ffn_Wr, L0_ffn_br, L0_ffn_gate_bias, L0_ffn_Wup, L0_ffn_bup, L0_ffn_Wgate, L0_ffn_bgate, L0_ffn_Wdown, L0_ffn_bdown, L0_ffn_Wsu, L0_ffn_bsu, L0_ffn_Wsg, L0_ffn_bsg, L0_ffn_Wsd, L0_ffn_bsd))
    x = x + s * g
    xn = _layernorm(x, axis=-1)
    s = _L1_attn_ref(xn, L1_attn_w_q_down, L1_attn_q_norm_w, L1_attn_w_q_up, L1_attn_w_kv_down, L1_attn_kv_norm_w, L1_attn_w_kv_up, L1_attn_w_o)
    g = _silu(_L1_ffn_ref(xn, L1_ffn_lut, L1_ffn_gate_idx, L1_ffn_up_idx, L1_ffn_down_idx))
    x = x + s * g
    return x

_drawn_inputs = setup_inputs


def setup_inputs(seed=0):
    import zlib

    import numpy as np

    out = dict(_drawn_inputs(seed))
    spreads = {'L0_ffn_gate_bias': (0.0, 0.749),
     'L1_attn_q_norm_w': (1.0, 0.6),
     'L1_attn_kv_norm_w': (1.0, 0.6)}
    factors = {'L0_ffn_br': 8.0,
     'L0_ffn_bup': 8.0,
     'L0_ffn_bgate': 8.0,
     'L0_ffn_bdown': 8.0,
     'L0_ffn_bsu': 8.0,
     'L0_ffn_bsg': 8.0,
     'L0_ffn_bsd': 8.0,
     'L1_attn_w_q_down': 8.0,
     'L1_attn_w_q_up': 8.0,
     'L1_attn_w_kv_down': 8.0,
     'L1_attn_w_kv_up': 8.0,
     'L1_attn_w_o': 8.0,
     'L1_ffn_lut': 8.0}
    for name, (base, spread) in spreads.items():
        noise = np.random.default_rng([zlib.crc32(name.encode()), seed]).standard_normal(out[name].shape)
        drawn = base * np.exp(spread * noise) if base else spread * noise
        out[name] = jnp.asarray(drawn.astype(out[name].dtype))
    for name, factor in factors.items():
        out[name] = (out[name] * factor).astype(out[name].dtype)
    return out
```

```python
from contextlib import ExitStack

import numpy as np

import concourse.bass as bass
from concourse import mybir

F32 = mybir.dt.float32
BF16 = mybir.dt.bfloat16
I32 = mybir.dt.int32
ALU = mybir.AluOpType
ACT = mybir.ActivationFunctionType
AX = mybir.AxisListType

P = 128
D = 256
DC = D // P
BATCH, SEQ = 4, 512
T = BATCH * SEQ
QT = SEQ // P
HEADS = 16
PAIRS = HEADS // 2
LAT = 64
ROPE = 64
ND0, QR0, HD0 = 64, 128, 128
Q_RANK1, QK1, NOPE1, VD1 = 192, 192, 128, 128
EXPERTS = 8
ROUTED = 7
INTER, INTER_PAD = 688, 768
IT = INTER_PAD // P
LUT = 16
NEG = -1e30
BIG = 3e38
LN_EPS, RMS_EPS = 1e-5, 1e-6
SWAP = [i ^ 1 for i in range(32)]

STAGE0 = {"qn": 128, "kn": 128, "rope": 128, "key": 256, "v": 128, "o": 512}
STAGE1 = {"qn": 512, "kn": 128, "rope": 256, "v": 128, "o": 512}
LUT_COLS = 2 * 2 * INTER_PAD + IT * D
LUT_CHUNK = 512


def at(i, n):
    return bass.ds(i * n, n)


def only(i):
    return i if isinstance(i, int) else bass.ds(i, 1)


def wait(eng, sem, value):
    if isinstance(value, int) and value <= 0:
        return
    eng.wait_ge(sem, value)


def build(nc, a, out):
    with ExitStack() as top:
        def keep(name, shape, dt=F32):
            return top.enter_context(nc.sbuf_tensor(name, shape, dt))

        XN = keep("normed", [P, DC, T])
        lut_w = keep("lut_weights", [P, LUT_COLS])
        ident = keep("identity", [P, P])
        ident_b = keep("identity_bf16", [P, P], BF16)
        mask_b = keep("causal_mask_bf16", [P, P], BF16)
        ones = keep("ones", [P, P])
        x1_dram = nc.dram_tensor("x_after_layer0", [D, T], F32, kind="Internal").ap()
        gate_dram = nc.dram_tensor("gate", [D, T], F32, kind="Internal").ap()
        prob_dram = nc.dram_tensor("probs", [EXPERTS, T], F32, kind="Internal").ap()
        chunked = lambda t: t.rearrange("(c p) t -> p c t", p=P)

        constants(nc, a, ident, ident_b, mask_b, ones)
        layernorm(nc, XN, ones, chunked(a["xT"]), "ln0")
        mixture(nc, a, XN, ident, lut_w, prob_dram, chunked(gate_dram))
        attention(nc, a, 0, XN, ident, ident_b, mask_b, ones, chunked(a["xT"]), chunked(gate_dram), chunked(x1_dram))
        layernorm(nc, XN, ones, None, "ln1")
        lut_ffn(nc, XN, lut_w, chunked(gate_dram))
        attention(nc, a, 1, XN, ident, ident_b, mask_b, ones, chunked(x1_dram), chunked(gate_dram), chunked(out))


def constants(nc, a, ident, ident_b, mask_b, ones):
    with ExitStack() as k:
        zeroed, made = k.enter_context(nc.semaphore("const_zeroed")), k.enter_context(nc.semaphore("const_made"))
        block = k.enter_context(nc.Block())

        @block.gpsimd
        def _(pool):
            nc.gpsimd.memset(ident[:], 0.0).then_inc(zeroed, 1)
            nc.gpsimd.memset(mask_b[:], 0.0).then_inc(zeroed, 1)
            nc.gpsimd.memset(ones[:], 1.0).then_inc(zeroed, 1)
            pool.wait_ge(zeroed, 3)
            nc.gpsimd.affine_select(out=ident[:], in_=ident[:], compare_op=ALU.not_equal, fill=1.0, base=0,
                                    pattern=[[-1, P]], channel_multiplier=1).then_inc(made, 1)
            nc.gpsimd.affine_select(out=mask_b[:], in_=mask_b[:], compare_op=ALU.is_ge, fill=NEG, base=0,
                                    pattern=[[-1, P]], channel_multiplier=1).then_inc(made, 1)

        @block.vector
        def _(dve):
            dve.wait_ge(made, 2)
            nc.vector.tensor_copy(ident_b[:], ident[:]).then_inc(made, 1)


def layernorm(nc, XN, ones, src, name):
    with ExitStack() as k:
        def sem(n):
            return k.enter_context(nc.semaphore(f"{name}_{n}"))

        def sb(n, shape):
            return k.enter_context(nc.sbuf_tensor(f"{name}_{n}", shape, F32))
        squares = sb("squares", [P, DC, SEQ])
        dev, rstd, eps = sb("dev", [P, SEQ]), sb("rstd", [P, SEQ]), sb("eps", [P, 1])
        mean_ps = k.enter_context(nc.psum_tensor(f"{name}_mean_ps", [P, SEQ], F32))
        var_ps = k.enter_context(nc.psum_tensor(f"{name}_var_ps", [P, SEQ], F32))
        loaded, has_eps, mean_ready, centred, squared, var_ready, dev_ready, rstd_ready, normed = map(
            sem, "loaded has_eps mean_ready centred squared var_ready dev_ready rstd_ready normed".split())
        block = k.enter_context(nc.Block())

        if src is not None:
            @block.sync
            def _(sp):
                for b in range(BATCH):
                    sp.dma_start(XN[:, :, b * SEQ:(b + 1) * SEQ], src[:, :, b * SEQ:(b + 1) * SEQ]).then_inc(loaded, 16)

        @block.tensor
        def _(pe):
            if src is not None:
                pe.wait_ge(loaded, 16 * BATCH)
            with pe.Fori(0, BATCH) as b:
                for c in range(DC):
                    mm = nc.tensor.matmul(mean_ps[:], ones[:], XN[:, c, at(b, SEQ)], start=c == 0, stop=c == DC - 1)
                mm.then_inc(mean_ready, 1)
                pe.wait_ge(squared, b + 1)
                for c in range(DC):
                    mm = nc.tensor.matmul(var_ps[:], ones[:], squares[:, c, :], start=c == 0, stop=c == DC - 1)
                mm.then_inc(var_ready, 1)

        @block.vector
        def _(dve):
            nc.vector.memset(eps[:], LN_EPS).then_inc(has_eps, 1)
            with dve.Fori(0, BATCH) as b:
                x = XN[:, :, at(b, SEQ)]
                dve.wait_ge(mean_ready, b + 1)
                for c in range(DC):
                    xc = XN[:, c, at(b, SEQ)]
                    ins = nc.vector.scalar_tensor_tensor(out=xc, in0=mean_ps[:], scalar=-1.0 / D, in1=xc,
                                                         op0=ALU.mult, op1=ALU.add)
                ins.then_inc(centred, 1)
                dve.wait_ge(dev_ready, b + 1)
                nc.vector.reciprocal(rstd[:], dev[:]).then_inc(rstd_ready, 1)
                dve.wait_ge(rstd_ready, b + 1)
                nc.vector.tensor_tensor(x, x, rstd[:].unsqueeze(1).to_broadcast([P, DC, SEQ]),
                                        ALU.mult).then_inc(normed, 1)

        @block.scalar
        def _(act):
            act.wait_ge(has_eps, 1)
            with act.Fori(0, BATCH) as b:
                act.wait_ge(centred, b + 1)
                nc.scalar.activation(squares[:], XN[:, :, at(b, SEQ)], ACT.Square).then_inc(squared, 1)
                act.wait_ge(var_ready, b + 1)
                nc.scalar.activation(dev[:], var_ps[:], ACT.Sqrt, bias=eps[:, 0:1], scale=1.0 / D).then_inc(dev_ready, 1)


def mixture(nc, a, XN, ident, lut_w, prob_dram, gate):
    TT = T // P
    with ExitStack() as k:
        def sem(n):
            return k.enter_context(nc.semaphore(f"moe_{n}"))

        def sb(n, shape, dt=F32):
            return k.enter_context(nc.sbuf_tensor(f"moe_{n}", shape, dt))

        def ps(n, shape):
            return k.enter_context(nc.psum_tensor(f"moe_{n}", shape, F32))
        w_up, w_gate = (sb(n, [P, DC, D + 1]) for n in ("w_up", "w_gate"))
        w_down = sb("w_down", [P, DC, D])
        b_down = sb("b_down", [P, D])
        w_route, b_route, b_select = sb("w_route", [P, DC, EXPERTS]), sb("b_route", [P, ROUTED]), sb("b_select", [P, ROUTED])
        index, table = sb("index", [P, LUT_COLS], I32), sb("table", [P, LUT])
        hit = sb("hit", [P, 2, LUT_CHUNK])
        acc = sb("acc", [P, DC, T])
        probT = sb("probT", [P, T])
        prob_b = sb("prob_b", [P, BATCH, SEQ])
        U, G = sb("U", [P, 2, DC, SEQ]), sb("G", [P, 2, DC, SEQ])
        SG, UP = sb("SG", [P, DC, SEQ]), sb("UP", [P, DC, SEQ])
        rt = [sb(f"route{i}", [P, TT, EXPERTS]) for i in range(6)]
        r1 = [sb(f"route_row{i}", [P, TT]) for i in range(8)]
        lane = sb("lane", [P, EXPERTS])
        up_ps, gate_ps, down_ps = (ps(n, [P, DC, SEQ]) for n in ("up_ps", "gate_ps", "down_ps"))
        route_ps = ps("route_ps", [P, TT, EXPERTS])
        turn_ps = ps("turn_ps", [EXPERTS, SEQ])
        (loaded, zeroed, lanes, routed, chain, expd, prob_ready, turned, turn_copied, prob_stored,
         up_loaded, gate_loaded, down_loaded, bias_ready, acc_ready, up_ready, up_copied, gate_ready, silu_done,
         scaled, glu_done, down_ready, added, lut_hit, lut_added, gated, stored) = map(sem, (
             "loaded zeroed lanes routed chain expd prob_ready turned turn_copied prob_stored "
             "up_loaded gate_loaded down_loaded bias_ready acc_ready up_ready up_copied gate_ready silu_done "
             "scaled glu_done down_ready added lut_hit lut_added gated stored").split())
        prob_bcast = [sem(f"prob_bcast{b}") for b in range(BATCH)]
        LOADS = 16 * 7

        def a_row(dram, e, b):
            return dram[bass.ds(e, 1), b * SEQ:(b + 1) * SEQ].to_broadcast([P, SEQ])
        block = k.enter_context(nc.Block())

        @block.sync
        def _(sp):
            sp.dma_start(w_route[:], a["w_route"]).then_inc(loaded, 16)
            sp.dma_start(b_route[:], a["b_route"].partition_broadcast(P)).then_inc(loaded, 16)
            sp.dma_start(b_select[:], a["b_select"].partition_broadcast(P)).then_inc(loaded, 16)
            sp.dma_start(table[:], a["lut"].partition_broadcast(P)).then_inc(loaded, 16)
            sp.wait_ge(zeroed, 2)
            sp.dma_start(b_down[0:EXPERTS, :], a["b_down"]).then_inc(loaded, 16)
            sp.dma_start(index[:], a["index"]).then_inc(loaded, 16)
            sp.dma_start(lane[:], a["lane"].partition_broadcast(P)).then_inc(loaded, 16)

            def load(e):
                wait(sp, up_copied, BATCH * e)
                sp.dma_start(w_up[:], a["w_up"][e]).then_inc(up_loaded, 16)
                for b in range(BATCH):
                    if b == 1:
                        wait(sp, silu_done, BATCH * e)
                        sp.dma_start(w_gate[:], a["w_gate"][e]).then_inc(gate_loaded, 16)
                    if b == 2:
                        wait(sp, down_ready, BATCH * e)
                        sp.dma_start(w_down[:], a["w_down"][e]).then_inc(down_loaded, 16)
                    if isinstance(e, int) and b == 0:
                        sp.wait_ge(prob_stored, 16)
                    wait(sp, scaled, BATCH * (e - 1) + b + 1)
                    sp.dma_start(prob_b[:, b, :], a_row(prob_dram, e, b)).then_inc(prob_bcast[b], 16)
            load(0)
            with sp.Fori(1, EXPERTS) as e:
                load(e)
            for b in range(BATCH):
                sp.wait_ge(gated, b + 1)
                sp.dma_start(gate[:, :, b * SEQ:(b + 1) * SEQ], acc[:, :, b * SEQ:(b + 1) * SEQ]).then_inc(stored, 16)
            sp.wait_ge(stored, 16 * BATCH)

        @block.gpsimd
        def _(pool):
            pool.memset(probT[:], 0.0).then_inc(zeroed, 1)
            pool.memset(b_down[:], 0.0).then_inc(zeroed, 1)
            pool.wait_ge(turn_copied, BATCH)
            pool.dma_start(prob_dram, probT[0:EXPERTS, :]).then_inc(prob_stored, 16)
            pool.wait_ge(prob_stored, 16)

        @block.tensor
        def _(pe):
            pe.wait_ge(loaded, LOADS)
            for t in range(TT):
                for c in range(DC):
                    mm = nc.tensor.matmul(route_ps[:, t, :], XN[:, c, t * P:(t + 1) * P], w_route[:, c, :],
                                          start=c == 0, stop=c == DC - 1)
            mm.then_inc(routed, 1)

            def up(e, b):
                if b == 0:
                    pe.wait_ge(up_loaded, 16 * (e + 1))
                wait(pe, up_copied, BATCH * e + b)
                for m in range(DC):
                    for c in range(DC):
                        mm = nc.tensor.matmul(up_ps[:, m, :], w_up[:, c, m * P:(m + 1) * P],
                                              XN[:, c, b * SEQ:(b + 1) * SEQ], start=c == 0, stop=c == DC - 1)
                mm.then_inc(up_ready, 1)

            def gating(e, b):
                if b == 0:
                    pe.wait_ge(gate_loaded, 16 * (e + 1))
                wait(pe, silu_done, BATCH * e + b)
                pe.wait_ge(up_copied, BATCH * e + b + 1)
                for m in range(DC):
                    for c in range(DC):
                        mm = nc.tensor.matmul(gate_ps[:, m, :], w_gate[:, c, m * P:(m + 1) * P],
                                              U[:, b % 2, c, :], start=c == 0, stop=c == DC - 1)
                mm.then_inc(gate_ready, 1)

            def down(e, b):
                if b == 0:
                    pe.wait_ge(down_loaded, 16 * (e + 1))
                wait(pe, added, BATCH * e + b)
                pe.wait_ge(glu_done, BATCH * e + b + 1)
                for m in range(DC):
                    for c in range(DC):
                        mm = nc.tensor.matmul(down_ps[:, m, :], w_down[:, c, m * P:(m + 1) * P],
                                              G[:, b % 2, c, :], start=c == 0, stop=c == DC - 1)
                mm.then_inc(down_ready, 1)

            def steps(e, first):
                for b in range(BATCH):
                    up(e, b)
                    if b >= 1 or not first:
                        gating(*((e, b - 1) if b >= 1 else (e - 1, BATCH - 1)))
                    if b >= 2 or not first:
                        down(*((e, b - 2) if b >= 2 else (e - 1, b + BATCH - 2)))
                    if first and b == 0:
                        turn()

            def turn():
                pe.wait_ge(prob_ready, 1)
                for b in range(BATCH):
                    wait(pe, turn_copied, b)
                    for t in range(QT):
                        mm = nc.tensor.transpose(turn_ps[:, t * P:(t + 1) * P], rt[5][:, b * QT + t, :], ident[:])
                    mm.then_inc(turned, 1)
                for b in range(BATCH):
                    pe.wait_ge(turn_copied, BATCH)
                    wait(pe, acc_ready, b)
                    for m in range(DC):
                        mm = nc.tensor.matmul(down_ps[:, m, :], b_down[:, m * P:(m + 1) * P],
                                              probT[:, b * SEQ:(b + 1) * SEQ], start=True, stop=True)
                    mm.then_inc(bias_ready, 1)
                pe.wait_ge(acc_ready, BATCH)

            steps(0, True)
            with pe.Fori(1, EXPERTS) as e:
                steps(e, False)
            gating(EXPERTS - 1, BATCH - 1)
            down(EXPERTS - 1, BATCH - 2)
            down(EXPERTS - 1, BATCH - 1)

        @block.scalar
        def _(act):
            act.wait_ge(loaded, LOADS)
            for i, n in enumerate((4, 5)):
                act.wait_ge(expd, i + 1)
                nc.scalar.activation(r1[n][:], r1[n][:], ACT.Exp).then_inc(chain, 1)

            def copy_up(e, b):
                act.wait_ge(up_ready, BATCH * e + b + 1)
                if b >= 2 or not isinstance(e, int):
                    act.wait_ge(scaled, BATCH * e + b - 1)
                for m in range(DC):
                    ins = nc.scalar.activation(U[:, b % 2, m, :], up_ps[:, m, :], ACT.Identity,
                                               bias=w_up[:, m, D:D + 1])
                ins.then_inc(up_copied, 1)

            def silu(e, b):
                act.wait_ge(gate_ready, BATCH * e + b + 1)
                wait(act, glu_done, BATCH * e + b)
                for m in range(DC):
                    ins = nc.scalar.activation(SG[:, m, :], gate_ps[:, m, :], ACT.Silu,
                                               bias=w_gate[:, m, D:D + 1])
                ins.then_inc(silu_done, 1)

            def steps(e, first):
                for b in range(BATCH):
                    copy_up(e, b)
                    if b >= 1 or not first:
                        silu(*((e, b - 1) if b >= 1 else (e - 1, BATCH - 1)))
            steps(0, True)
            with act.Fori(1, EXPERTS) as e:
                steps(e, False)
            silu(EXPERTS - 1, BATCH - 1)
            for b in range(BATCH):
                act.wait_ge(added, BATCH * (EXPERTS - 1) + b + 1)
                sl = acc[:, :, b * SEQ:(b + 1) * SEQ]
                nc.scalar.activation(sl, sl, ACT.Silu).then_inc(gated, 1)

        @block.vector
        def _(dve):
            V = nc.vector
            links = [0]

            def link(ins):
                links[0] += 1
                ins.then_inc(lanes, 1)
                dve.wait_ge(lanes, links[0])
            wide = lambda row: row[:].unsqueeze(2).to_broadcast([P, TT, EXPERTS])
            every = lambda v: v[:].unsqueeze(1).to_broadcast([P, TT, v.shape[1]])
            logits, select, pick1, pick2, tmp, probs = rt
            top, place, g1, g2, e1, e2, both, inv = r1
            dve.wait_ge(loaded, LOADS)
            dve.wait_ge(routed, 1)
            link(V.memset(select[:], -BIG))
            link(V.memset(logits[:], 0.0))
            link(V.tensor_tensor(logits[:, :, 0:ROUTED], route_ps[:, :, 0:ROUTED], every(b_route), ALU.add))
            link(V.tensor_tensor(select[:, :, 0:ROUTED], logits[:, :, 0:ROUTED], every(b_select), ALU.add))
            for pick in (pick1, pick2):
                link(V.tensor_reduce(top[:], select[:], AX.X, ALU.max))
                link(V.tensor_tensor(tmp[:], select[:], wide(top), ALU.is_equal))
                link(V.tensor_tensor(tmp[:], tmp[:], every(lane), ALU.mult))
                link(V.tensor_reduce(place[:], tmp[:], AX.X, ALU.max))
                link(V.tensor_tensor(pick[:], tmp[:], wide(place), ALU.is_equal))
                link(V.scalar_tensor_tensor(out=select[:], in0=pick[:], scalar=-BIG, in1=select[:],
                                            op0=ALU.mult, op1=ALU.add))
            for pick, g in ((pick1, g1), (pick2, g2)):
                link(V.tensor_tensor(tmp[:], pick[:], logits[:], ALU.mult))
                link(V.tensor_reduce(g[:], tmp[:], AX.X, ALU.add))
            link(V.tensor_tensor(both[:], g1[:], g2[:], ALU.max))
            V.tensor_tensor(e1[:], g1[:], both[:], ALU.subtract).then_inc(expd, 1)
            V.tensor_tensor(e2[:], g2[:], both[:], ALU.subtract).then_inc(expd, 1)
            dve.wait_ge(chain, 2)
            link(V.tensor_tensor(both[:], e1[:], e2[:], ALU.add))
            link(V.reciprocal(inv[:], both[:]))
            for pick, e in ((pick1, e1), (pick2, e2)):
                link(V.tensor_tensor(e[:], e[:], inv[:], ALU.mult))
                link(V.tensor_tensor(pick[:], pick[:], wide(e), ALU.mult))
            link(V.tensor_tensor(probs[:], pick1[:], pick2[:], ALU.add))
            V.memset(probs[:, :, ROUTED:EXPERTS], 1.0).then_inc(prob_ready, 1)
            dve.wait_ge(zeroed, 1)
            for b in range(BATCH):
                dve.wait_ge(turned, b + 1)
                V.tensor_copy(probT[0:EXPERTS, b * SEQ:(b + 1) * SEQ], turn_ps[:]).then_inc(turn_copied, 1)
            for b in range(BATCH):
                dve.wait_ge(bias_ready, b + 1)
                V.tensor_copy(acc[:, :, b * SEQ:(b + 1) * SEQ], down_ps[:]).then_inc(acc_ready, 1)

            def glu(e, b):
                dve.wait_ge(up_copied, BATCH * e + b + 1)
                dve.wait_ge(prob_bcast[b], 16 * (e + 1))
                V.tensor_tensor(UP[:], U[:, b % 2, :, :], prob_b[:, b, :].unsqueeze(1).to_broadcast([P, DC, SEQ]),
                                ALU.mult).then_inc(scaled, 1)
                dve.wait_ge(scaled, BATCH * e + b + 1)
                dve.wait_ge(silu_done, BATCH * e + b + 1)
                wait(dve, down_ready, BATCH * e + b - 1)
                V.tensor_tensor(G[:, b % 2, :, :], UP[:], SG[:], ALU.mult).then_inc(glu_done, 1)

            def accumulate(e, b):
                dve.wait_ge(down_ready, BATCH * e + b + 1)
                sl = acc[:, :, b * SEQ:(b + 1) * SEQ]
                V.tensor_tensor(sl, sl, down_ps[:], ALU.add).then_inc(added, 1)

            def look_up(chunk, q):
                cols = at(chunk, LUT_CHUNK)
                for v in range(q * LUT // 4, (q + 1) * LUT // 4):
                    n = chunk * LUT + v
                    V.tensor_scalar(hit[:, v % 2, :], index[:, cols], float(v), table[:, v:v + 1],
                                    ALU.is_equal, ALU.mult).then_inc(lut_hit, 1)
                    dve.wait_ge(lut_hit, n + 1)
                    if v == 0:
                        V.tensor_copy(lut_w[:, cols], hit[:, v % 2, :]).then_inc(lut_added, 1)
                    else:
                        dve.wait_ge(lut_added, n)
                        V.tensor_tensor(lut_w[:, cols], lut_w[:, cols], hit[:, v % 2, :], ALU.add).then_inc(lut_added, 1)

            def steps(e, first):
                for b in range(BATCH):
                    if b >= 1 or not first:
                        glu(*((e, b - 1) if b >= 1 else (e - 1, BATCH - 1)))
                    if b >= 2 or not first:
                        accumulate(*((e, b - 2) if b >= 2 else (e - 1, b + BATCH - 2)))
                    look_up(e, b)
            steps(0, True)
            with dve.Fori(1, EXPERTS) as e:
                steps(e, False)
            glu(EXPERTS - 1, BATCH - 1)
            accumulate(EXPERTS - 1, BATCH - 2)
            accumulate(EXPERTS - 1, BATCH - 1)
            for chunk in range(EXPERTS, LUT_COLS // LUT_CHUNK):
                for q in range(4):
                    look_up(chunk, q)


def lut_ffn(nc, XN, lut_w, gate):
    wg = lut_w[:, 0:DC * INTER_PAD].rearrange("p (c n) -> p c n", c=DC)
    wu = lut_w[:, DC * INTER_PAD:2 * DC * INTER_PAD].rearrange("p (c n) -> p c n", c=DC)
    wd = lut_w[:, 2 * DC * INTER_PAD:].rearrange("p (c n) -> p c n", c=IT)
    with ExitStack() as k:
        def sem(n):
            return k.enter_context(nc.semaphore(f"ffn_{n}"))
        H = k.enter_context(nc.sbuf_tensor("ffn_H", [P, IT, SEQ], F32))
        SG = k.enter_context(nc.sbuf_tensor("ffn_SG", [P, 2, SEQ], F32))
        GO = k.enter_context(nc.sbuf_tensor("ffn_out", [P, DC, SEQ], F32))
        g_ps = k.enter_context(nc.psum_tensor("ffn_g_ps", [P, 2, SEQ], F32))
        u_ps = k.enter_context(nc.psum_tensor("ffn_u_ps", [P, 2, SEQ], F32))
        d_ps = k.enter_context(nc.psum_tensor("ffn_d_ps", [P, DC, SEQ], F32))
        g_ready, u_ready, silu_done, h_done, d_ready, gated, stored = map(
            sem, "g_ready u_ready silu_done h_done d_ready gated stored".split())
        block = k.enter_context(nc.Block())

        @block.tensor
        def _(pe):
            def up(b, m):
                i = IT * b + m
                wait(pe, h_done, i - 1)
                for w, o, s in ((wg, g_ps, g_ready), (wu, u_ps, u_ready)):
                    for c in range(DC):
                        mm = nc.tensor.matmul(o[:, m % 2, :], w[:, c, m * P:(m + 1) * P], XN[:, c, at(b, SEQ)],
                                              start=c == 0, stop=c == DC - 1)
                    mm.then_inc(s, 1)

            def batch(b, first):
                for m in range(IT):
                    up(b, m)
                pe.wait_ge(h_done, IT * (b + 1))
                wait(pe, gated, b)
                for m in range(DC):
                    for c in range(IT):
                        mm = nc.tensor.matmul(d_ps[:, m, :], wd[:, c, m * P:(m + 1) * P], H[:, c, :],
                                              start=c == 0, stop=c == IT - 1)
                mm.then_inc(d_ready, 1)
            batch(0, True)
            with pe.Fori(1, BATCH) as b:
                batch(b, False)

        @block.scalar
        def _(act):
            def batch(b):
                for m in range(IT):
                    i = IT * b + m
                    act.wait_ge(g_ready, i + 1)
                    wait(act, h_done, i - 1)
                    nc.scalar.activation(SG[:, m % 2, :], g_ps[:, m % 2, :], ACT.Silu).then_inc(silu_done, 1)
                act.wait_ge(d_ready, b + 1)
                wait(act, stored, 16 * b)
                nc.scalar.activation(GO[:], d_ps[:], ACT.Silu).then_inc(gated, 1)
            batch(0)
            with act.Fori(1, BATCH) as b:
                batch(b)

        @block.vector
        def _(dve):
            def batch(b):
                wait(dve, d_ready, b)
                for m in range(IT):
                    i = IT * b + m
                    dve.wait_ge(silu_done, i + 1)
                    dve.wait_ge(u_ready, i + 1)
                    nc.vector.tensor_tensor(H[:, m, :], SG[:, m % 2, :], u_ps[:, m % 2, :], ALU.mult).then_inc(h_done, 1)
            batch(0)
            with dve.Fori(1, BATCH) as b:
                batch(b)

        @block.sync
        def _(sp):
            with sp.Fori(0, BATCH) as b:
                sp.wait_ge(gated, b + 1)
                sp.dma_start(gate[:, :, at(b, SEQ)], GO[:]).then_inc(stored, 16)
            sp.wait_ge(stored, 16 * BATCH)


def attention(nc, a, layer, XN, ident, ident_b, mask_b, ones, x_src, gate, x_dst):
    with ExitStack() as k:
        def sb(n, shape, dt=F32):
            return k.enter_context(nc.sbuf_tensor(f"at{layer}_{n}", shape, dt))
        st = {
            "latent_q": sb("latent_q", [P, layer + 1, T]),
            "KE": sb("KE", [P, BATCH, SEQ]), "KO": sb("KO", [P, BATCH, SEQ]),
            "V": sb("V", [P, BATCH * QT, P]),
            "OL": sb("OL", [P, PAIRS, T]),
            "WVO": sb("WVO", [P, PAIRS, D]),
            "cos": sb("cos", [P, SEQ]), "sin": sb("sin", [P, SEQ]),
        }
        latents(nc, a, layer, XN, ident, ones, st)
        heads(nc, a, layer, XN, ident, ident_b, mask_b, st)
        project(nc, layer, XN, st, x_src, gate, x_dst)


def latents(nc, a, layer, XN, ident, ones, st):
    n = f"lat{layer}"
    KQ = layer + 1
    with ExitStack() as k:
        def sem(x):
            return k.enter_context(nc.semaphore(f"{n}_{x}"))

        def sb(x, shape, dt=F32):
            return k.enter_context(nc.sbuf_tensor(f"{n}_{x}", shape, dt))

        def ps(x, shape):
            return k.enter_context(nc.psum_tensor(f"{n}_{x}", shape, F32))
        wq = sb("wq", [P, DC, KQ * P])
        wkv = sb("wkv", [P, DC, KQ * P])
        normw = sb("normw", [P, KQ + 1])
        KV, RM, RS = sb("KV", [P, SEQ]), sb("RM", [P, SEQ]), sb("RS", [P, SEQ])
        SQ, dev, rstd = sb("SQ", [P, 3, SEQ]), sb("dev", [P, 2, SEQ]), sb("rstd", [P, 2, SEQ])
        eps = sb("eps", [P, 2])
        q_ps, k_ps, v_ps = ps("q_ps", [P, KQ, SEQ]), ps("k_ps", [P, KQ, SEQ]), ps("v_ps", [P, SEQ])
        m_ps = ps("m_ps", [P, 2, SEQ])
        (loaded, has_eps, q_ready, k_ready, q_done, squared, sums_ready, dev_ready, rstd_ready, kv_ready, k_done,
         roped, rope_done, v_ready, v_done) = map(sem, (
             "loaded has_eps q_ready k_ready q_done squared sums_ready dev_ready rstd_ready kv_ready k_done "
             "roped rope_done v_ready v_done").split())
        KE, KO, CQ, V = st["KE"], st["KO"], st["latent_q"], st["V"]
        LOADS = 16 * (4 + layer)
        block = k.enter_context(nc.Block())

        @block.sync
        def _(sp):
            sp.dma_start(wq[:], a[f"wq_down{layer}"]).then_inc(loaded, 16)
            sp.dma_start(wkv[:], a[f"wkv_down{layer}"]).then_inc(loaded, 16)
            sp.dma_start(st["cos"][:], a[f"cos{layer}"]).then_inc(loaded, 16)
            sp.dma_start(st["sin"][:], a[f"sin{layer}"]).then_inc(loaded, 16)
            if layer == 1:
                sp.dma_start(normw[:], a["norm_w1"]).then_inc(loaded, 16)

        @block.tensor
        def _(pe):
            pe.wait_ge(loaded, LOADS)

            def batch(b):
                wait(pe, q_done, b)
                for m in range(KQ):
                    for c in range(DC):
                        mm = nc.tensor.matmul(q_ps[:, m, :], wq[:, c, m * P:(m + 1) * P], XN[:, c, at(b, SEQ)],
                                              start=c == 0, stop=c == DC - 1)
                mm.then_inc(q_ready, 1)
                wait(pe, kv_ready, b)
                wait(pe, roped, 2 * b * layer)
                for m in range(KQ):
                    for c in range(DC):
                        mm = nc.tensor.matmul(k_ps[:, m, :], wkv[:, c, m * P:(m + 1) * P], XN[:, c, at(b, SEQ)],
                                              start=c == 0, stop=c == DC - 1)
                mm.then_inc(k_ready, 1)
                if layer == 1:
                    pe.wait_ge(squared, 2 * b + 1)
                    for c in range(KQ):
                        mm = nc.tensor.matmul(m_ps[:, 0, :], ones[:], SQ[:, c, :], start=c == 0, stop=c == KQ - 1)
                    mm.then_inc(sums_ready, 1)
                    pe.wait_ge(squared, 2 * b + 2)
                    nc.tensor.matmul(m_ps[:, 1, :], ones[:], SQ[:, 2, :], start=True, stop=True).then_inc(sums_ready, 1)
                pe.wait_ge(kv_ready, b + 1)
                wait(pe, v_done, b)
                for t in range(QT):
                    mm = nc.tensor.transpose(v_ps[:, t * P:(t + 1) * P], KV[:, t * P:(t + 1) * P], ident[:])
                mm.then_inc(v_ready, 1)
            batch(0)
            with pe.Fori(1, BATCH) as b:
                batch(b)

        @block.scalar
        def _(act):
            act.wait_ge(has_eps, 1)

            def batch(b):
                act.wait_ge(q_ready, b + 1)
                if layer == 0:
                    nc.scalar.activation(CQ[:, 0, at(b, SEQ)], q_ps[:, 0, :], ACT.Copy, scale=HD0 ** -0.5).then_inc(q_done, 1)
                else:
                    wait(act, sums_ready, 2 * b)
                    nc.scalar.activation(SQ[:, 0:KQ, :], q_ps[:], ACT.Square).then_inc(squared, 1)
                    act.wait_ge(k_ready, b + 1)
                    nc.scalar.activation(SQ[:, 2, :], k_ps[:, 0, :], ACT.Square).then_inc(squared, 1)
                    act.wait_ge(sums_ready, 2 * b + 2)
                    wait(act, rstd_ready, b)
                    nc.scalar.activation(dev[:, 0, :], m_ps[:, 0, :], ACT.Sqrt, bias=eps[:, 0:1]).then_inc(dev_ready, 1)
                    nc.scalar.activation(dev[:, 1, :], m_ps[:, 1, :], ACT.Sqrt, bias=eps[:, 1:2],
                                         scale=1.0 / P).then_inc(dev_ready, 1)
                act.wait_ge(kv_ready, b + 1)
                nc.scalar.activation(KE[0:LAT, only(b), :], KV[0:LAT, :], ACT.Copy)
                nc.scalar.activation(KO[LAT:P, only(b), :], KV[LAT:P, :], ACT.Copy).then_inc(k_done, 1)
                act.wait_ge(v_ready, b + 1)
                nc.scalar.activation(V[:, at(b, QT), :], v_ps[:].rearrange("p (t n) -> p t n", t=QT), ACT.Copy).then_inc(v_done, 1)
            batch(0)
            with act.Fori(1, BATCH) as b:
                batch(b)

        @block.vector
        def _(dve):
            nc.vector.memset(eps[:, 0:1], Q_RANK1 * RMS_EPS)
            nc.vector.memset(eps[:, 1:2], RMS_EPS).then_inc(has_eps, 1)
            dve.wait_ge(loaded, LOADS)

            def batch(b):
                wait(dve, v_ready, b)
                wait(dve, k_done, b)
                if layer == 0:
                    dve.wait_ge(k_ready, b + 1)
                    nc.vector.tensor_copy(KV[:], k_ps[:, 0, :]).then_inc(kv_ready, 1)
                else:
                    dve.wait_ge(dev_ready, 2 * b + 2)
                    nc.vector.reciprocal(rstd[:], dev[:]).then_inc(rstd_ready, 1)
                    dve.wait_ge(rstd_ready, b + 1)
                    for c in range(KQ):
                        ins = nc.vector.scalar_tensor_tensor(out=CQ[:, c, at(b, SEQ)], in0=q_ps[:, c, :], scalar=normw[:, c:c + 1],
                                                             in1=rstd[:, 0, :], op0=ALU.mult, op1=ALU.mult)
                    ins.then_inc(q_done, 1)
                    nc.vector.scalar_tensor_tensor(out=KV[:], in0=k_ps[:, 0, :], scalar=normw[:, KQ:KQ + 1],
                                                   in1=rstd[:, 1, :], op0=ALU.mult, op1=ALU.mult).then_inc(kv_ready, 1)
                    wait(dve, rope_done, 2 * b)
                    nc.vector.tensor_tensor(RM[:], k_ps[:, 1, :], st["cos"][:], ALU.mult).then_inc(roped, 1)
                    nc.vector.stream_shuffle(RS[:], k_ps[:, 1, :], SWAP).then_inc(roped, 1)
            batch(0)
            with dve.Fori(1, BATCH) as b:
                batch(b)

        if layer == 1:
            @block.gpsimd
            def _(pool):
                pool.wait_ge(loaded, LOADS)
                turned = sem("turned")

                def batch(b):
                    pool.wait_ge(roped, 2 * b + 2)
                    wait(pool, rope_done, 2 * b)
                    nc.gpsimd.tensor_tensor(RS[:], RS[:], st["sin"][:], ALU.mult).then_inc(turned, 1)
                    pool.wait_ge(turned, b + 1)
                    nc.gpsimd.tensor_tensor(KE[LAT:P, only(b), :], RM[LAT:P, :], RS[LAT:P, :], ALU.add).then_inc(rope_done, 1)
                    nc.gpsimd.tensor_tensor(KO[0:LAT, only(b), :], RM[0:LAT, :], RS[0:LAT, :], ALU.add).then_inc(rope_done, 1)
                batch(0)
                with pool.Fori(1, BATCH) as b:
                    batch(b)


def heads(nc, a, layer, XN, ident, ident_b, mask_b, st):
    n = f"hd{layer}"
    KQ = layer + 1
    stage = (STAGE0, STAGE1)[layer]
    offset, width = {}, 0
    for key, cols in stage.items():
        offset[key], width = width, width + cols
    STEPS = 2 * BATCH
    KINDS = ("rope", "key") if layer == 0 else ("rope",)
    NK = len(KINDS)
    KE, KO, CQ, V, OL, WVO = (st[x] for x in ("KE", "KO", "latent_q", "V", "OL", "WVO"))
    with ExitStack() as k:
        def sem(x):
            return k.enter_context(nc.semaphore(f"{n}_{x}"))

        def sb(x, shape, dt=F32):
            return k.enter_context(nc.sbuf_tensor(f"{n}_{x}", shape, dt))

        def ps(x, shape):
            return k.enter_context(nc.psum_tensor(f"{n}_{x}", shape, F32))
        ST = sb("stage", [P, width])
        WN = sb("w_latent", [P, KQ, P])
        QE, QO = sb("QE", [P, 2, SEQ]), sb("QO", [P, 2, SEQ])
        RM, RS = sb("RM", [P, 2, SEQ]), sb("RS", [P, 2, SEQ])
        PR = sb("probs", [P, 2, QT * (QT + 1) // 2, P])
        PT = sb("probsT", [P, 2, QT, SEQ])
        NM, SM, RC = sb("negmax", [P, 2, QT]), sb("sums", [P, 2, QT]), sb("inv_sums", [P, 2, QT])
        s_ps = [ps(f"s_ps{i}", [P, SEQ]) for i in range(3)]
        t_ps = [ps(f"t_ps{i}", [P, SEQ]) for i in range(2)]
        o_ps = ps("o_ps", [P, SEQ])
        pj_ps = [ps(f"pj_ps{i}", [P, SEQ]) for i in range(2)]
        (staged, wabs_ready, wvo_ready, wabs_copied, wvo_copied, qn_ready, qn_copied, rp_ready, rp_read, rp_mult,
         rp_done, s_ready, max_done, exp_done, inv_done, norm_done, t_ready, t_copied, o_ready, o_copied) = map(sem, (
             "staged wabs_ready wvo_ready wabs_copied wvo_copied qn_ready qn_copied rp_ready rp_read rp_mult "
             "rp_done s_ready max_done exp_done inv_done norm_done t_ready t_copied o_ready o_copied").split())

        def part(key, parts=1):
            v = ST[:, offset[key]:offset[key] + stage[key]]
            return v.rearrange("p (k n) -> p k n", k=parts) if parts > 1 else v
        tri = lambda i: i * (i + 1) // 2

        def bank_before(p, g, i):
            t, l = QT * (STEPS * p + g) + i, (QT * (g % 2) + i)
            return t - 3 + 1 if l >= 3 else t + (-2, -2, -5)[l] + 1

        def drive(eng, prologue, body, epilogue):
            prologue()
            body(0, True, False)
            with eng.Fori(1, PAIRS - 1) as p:
                body(p, False, False)
            body(PAIRS - 1, False, True)
            epilogue()

        def back(p, g, lag):
            return (p, g - lag) if g >= lag else (p - 1, g - lag + STEPS)
        block = k.enter_context(nc.Block())

        @block.sync
        def _(sp):
            def load(p):
                wait(sp, rp_ready, NK * BATCH * p)
                wait(sp, qn_ready, BATCH * p)
                sp.dma_start(ST[:], a[f"stage{layer}"][p]).then_inc(staged, 16)
            for p in range(PAIRS):
                load(p)

        @block.tensor
        def _(pe):
            def weights(p):
                pe.wait_ge(staged, 16 * (p + 1))
                wait(pe, qn_copied, BATCH * p)
                wait(pe, rp_read, 2 * NK * BATCH * p)
                if layer == 0:
                    mm = nc.tensor.matmul(pj_ps[0][:, 0:P], part("qn"), part("kn"), start=True, stop=True)
                else:
                    qn, kn = part("qn", 2 * KQ), part("kn", 2)
                    for c in range(KQ):
                        for e in range(2):
                            mm = nc.tensor.matmul(pj_ps[0][:, c * P + e * LAT:c * P + (e + 1) * LAT], qn[:, KQ * e + c, :],
                                                  kn[:, e, :], start=True, stop=True)
                mm.then_inc(wabs_ready, 1)
                v, o = part("v", 2), part("o", 2)
                for e in range(2):
                    mm = nc.tensor.matmul(pj_ps[1][e * LAT:(e + 1) * LAT, 0:D], v[:, e, :], o[:, e, :], start=True, stop=True)
                mm.then_inc(wvo_ready, 1)

            def queries(p, b):
                m = BATCH * p + b
                if b == 0:
                    pe.wait_ge(wabs_copied, p + 1)
                wait(pe, rp_read, 2 * NK * m)
                wait(pe, qn_copied, m)
                for c in range(KQ):
                    mm = nc.tensor.matmul(pj_ps[0][:], WN[:, c, :], CQ[:, c, b * SEQ:(b + 1) * SEQ], start=c == 0, stop=c == KQ - 1)
                mm.then_inc(qn_ready, 1)
                if b == 0:
                    pe.wait_ge(wvo_copied, p + 1)
                wr = part("rope", KQ) if KQ > 1 else part("rope").unsqueeze(1)
                for c in range(KQ):
                    mm = nc.tensor.matmul(pj_ps[1][:], wr[:, c, :], CQ[:, c, b * SEQ:(b + 1) * SEQ], start=c == 0, stop=c == KQ - 1)
                mm.then_inc(rp_ready, 1)
                if layer == 0:
                    pe.wait_ge(qn_copied, m + 1)
                    wk = part("key", DC)
                    for c in range(DC):
                        mm = nc.tensor.matmul(pj_ps[0][:], wk[:, c, :], XN[:, c, b * SEQ:(b + 1) * SEQ], start=c == 0, stop=c == DC - 1)
                    mm.then_inc(rp_ready, 1)

            def scores(p, g, i):
                b, e = g // 2, g % 2
                if i == 0 and e == 0:
                    pe.wait_ge(qn_copied, BATCH * p + b + 1)
                    pe.wait_ge(rp_done, 2 * NK * (BATCH * p + b + 1))
                wait(pe, exp_done, bank_before(p, g, i))
                q, kk = (QO, KO) if e else (QE, KE)
                s = s_ps[(QT * e + i) % 3]
                nc.tensor.matmul(s[:, 0:(i + 1) * P], q[:, b % 2, i * P:(i + 1) * P], kk[:, b, 0:(i + 1) * P], start=True, stop=False)
                nc.tensor.matmul(s[:, i * P:(i + 1) * P], ident_b[:], mask_b[:], start=False, stop=True).then_inc(s_ready, 1)

            def turn(p, g, i):
                h = STEPS * p + g
                pe.wait_ge(norm_done, QT * h + i + 1)
                wait(pe, t_copied, QT * h + i - 1)
                for j in range(i + 1):
                    mm = nc.tensor.transpose(t_ps[i % 2][:, j * P:(j + 1) * P], PR[:, g % 2, tri(i) + j, :], ident[:])
                mm.then_inc(t_ready, 1)

            def values(p, g):
                h = STEPS * p + g
                pe.wait_ge(t_copied, QT * (h + 1))
                wait(pe, o_copied, h)
                for j in range(QT):
                    mm = nc.tensor.matmul(o_ps[:, j * P:SEQ], V[:, (g // 2) * QT + j, :], PT[:, g % 2, j, j * P:SEQ],
                                          start=j == 0, stop=j == QT - 1)
                mm.then_inc(o_ready, 1)

            def body(p, first, last):
                for g in range(STEPS):
                    scores(p, g, 0)
                    scores(p, g, 1)
                    if not (first and g < 1):
                        turn(*back(p, g, 1), 0)
                    scores(p, g, 2)
                    if not (first and g < 1):
                        turn(*back(p, g, 1), 1)
                    scores(p, g, 3)
                    if not (first and g < 2):
                        values(*back(p, g, 2))
                    if not (first and g < 1):
                        turn(*back(p, g, 1), 2)
                        turn(*back(p, g, 1), 3)
                    if g == 5 and not last:
                        weights(p + 1)
                    if g % 2 == 0 and not (last and g == STEPS - 2):
                        queries(p if g < STEPS - 2 else p + 1, (g // 2 + 1) % BATCH)

            def prologue():
                weights(0)
                queries(0, 0)

            def epilogue():
                for i in range(QT):
                    turn(PAIRS - 1, STEPS - 1, i)
                values(PAIRS - 1, STEPS - 2)
                values(PAIRS - 1, STEPS - 1)
            drive(pe, prologue, body, epilogue)

        @block.scalar
        def _(act):
            def weights(p):
                act.wait_ge(wabs_ready, p + 1)
                nc.scalar.activation(WN[:], pj_ps[0][:, 0:KQ * P].rearrange("p (c n) -> p c n", c=KQ), ACT.Copy).then_inc(wabs_copied, 1)

            def queries(p, b):
                act.wait_ge(qn_ready, BATCH * p + b + 1)
                nc.scalar.activation(QE[0:LAT, b % 2, :], pj_ps[0][0:LAT, :], ACT.Copy)
                nc.scalar.activation(QO[LAT:P, b % 2, :], pj_ps[0][LAT:P, :], ACT.Copy).then_inc(qn_copied, 1)

            def exps(p, g, i):
                h = STEPS * p + g
                act.wait_ge(max_done, QT * h + i + 1)
                wait(act, t_ready, QT * (h - 1))
                nc.scalar.activation(PR[:, g % 2, tri(i):tri(i + 1), :], s_ps[(QT * (g % 2) + i) % 3][:, 0:(i + 1) * P]
                                     .rearrange("p (j n) -> p j n", j=i + 1), ACT.Exp,
                                     bias=NM[:, g % 2, i:i + 1], accum_out=SM[:, g % 2, i:i + 1]).then_inc(exp_done, 1)

            def copy_turned(p, g, i):
                h = STEPS * p + g
                act.wait_ge(t_ready, QT * h + i + 1)
                wait(act, o_ready, h - 1)
                nc.scalar.activation(PT[:, g % 2, 0:i + 1, i * P:(i + 1) * P],
                                     t_ps[i % 2][:, 0:(i + 1) * P].rearrange("p (j n) -> p j n", j=i + 1), ACT.Copy).then_inc(t_copied, 1)

            def body(p, first, last):
                for g in range(STEPS):
                    exps(p, g, 0)
                    exps(p, g, 1)
                    if not (first and g < 1):
                        copy_turned(*back(p, g, 1), 0)
                    exps(p, g, 2)
                    if not (first and g < 1):
                        copy_turned(*back(p, g, 1), 1)
                    exps(p, g, 3)
                    if not (first and g < 1):
                        copy_turned(*back(p, g, 1), 2)
                        copy_turned(*back(p, g, 1), 3)
                    if g == 5 and not last:
                        weights(p + 1)
                    if g % 2 == 0 and not (last and g == STEPS - 2):
                        queries(p if g < STEPS - 2 else p + 1, (g // 2 + 1) % BATCH)

            def prologue():
                weights(0)
                queries(0, 0)

            def epilogue():
                for i in range(QT):
                    copy_turned(PAIRS - 1, STEPS - 1, i)
            drive(act, prologue, body, epilogue)

        @block.vector
        def _(dve):
            def weights(p):
                dve.wait_ge(wvo_ready, p + 1)
                dst = WVO[:, p, :] if isinstance(p, int) else WVO[:, bass.ds(p, 1), :]
                nc.vector.tensor_copy(dst, pj_ps[1][:, 0:D]).then_inc(wvo_copied, 1)

            def queries(p, b):
                m = BATCH * p + b
                for n_, kind in enumerate(KINDS):
                    r = NK * m + n_
                    buf = n_ if layer == 0 else b % 2
                    src = pj_ps[1 - n_]
                    dve.wait_ge(rp_ready, r + 1)
                    wait(dve, rp_done, 2 * (r - 1))
                    nc.vector.tensor_tensor(RM[:, buf, :], src[:], st["cos"][:], ALU.mult).then_inc(rp_read, 1)
                    nc.vector.stream_shuffle(RS[:, buf, :], src[:], SWAP).then_inc(rp_read, 1)

            def maxes(p, g, i):
                h = STEPS * p + g
                dve.wait_ge(s_ready, QT * h + i + 1)
                wait(dve, exp_done, QT * (h - 1))
                nc.vector.tensor_reduce(NM[:, g % 2, i:i + 1], s_ps[(QT * (g % 2) + i) % 3][:, 0:(i + 1) * P], AX.X,
                                        ALU.max, negate=True).then_inc(max_done, 1)

            def invert(p, g):
                h = STEPS * p + g
                dve.wait_ge(exp_done, QT * (h + 1))
                nc.vector.reciprocal(RC[:, g % 2, :], SM[:, g % 2, :]).then_inc(inv_done, 1)

            def norm(p, g, i):
                h = STEPS * p + g
                if i == 0:
                    dve.wait_ge(inv_done, h + 1)
                sl = PR[:, g % 2, tri(i):tri(i + 1), :]
                nc.vector.tensor_scalar(sl, sl, RC[:, g % 2, i:i + 1], None, ALU.mult).then_inc(norm_done, 1)

            def copy_out(p, g):
                e, b = g % 2, g // 2
                dve.wait_ge(o_ready, STEPS * p + g + 1)
                rows = slice(e * LAT, (e + 1) * LAT)
                dst = OL[rows, p if isinstance(p, int) else bass.ds(p, 1), b * SEQ:(b + 1) * SEQ]
                nc.vector.tensor_copy(dst, o_ps[rows, :]).then_inc(o_copied, 1)

            def body(p, first, last):
                for g in range(STEPS):
                    before = not (first and g < 1)
                    maxes(p, g, 0)
                    if before:
                        invert(*back(p, g, 1))
                        norm(*back(p, g, 1), 0)
                    maxes(p, g, 1)
                    if before:
                        norm(*back(p, g, 1), 1)
                        norm(*back(p, g, 1), 2)
                    maxes(p, g, 2)
                    if before:
                        norm(*back(p, g, 1), 3)
                    maxes(p, g, 3)
                    if not (first and g < 2):
                        copy_out(*back(p, g, 2))
                    if g == 5 and not last:
                        weights(p + 1)
                    if g % 2 == 0 and not (last and g == STEPS - 2):
                        queries(p if g < STEPS - 2 else p + 1, (g // 2 + 1) % BATCH)

            def prologue():
                weights(0)
                queries(0, 0)

            def epilogue():
                invert(PAIRS - 1, STEPS - 1)
                for i in range(QT):
                    norm(PAIRS - 1, STEPS - 1, i)
                copy_out(PAIRS - 1, STEPS - 2)
                copy_out(PAIRS - 1, STEPS - 1)
            drive(dve, prologue, body, epilogue)

        @block.gpsimd
        def _(pool):
            def queries(p, b):
                m = BATCH * p + b
                for n_, kind in enumerate(KINDS):
                    r = NK * m + n_
                    buf = n_ if layer == 0 else b % 2
                    pool.wait_ge(rp_read, 2 * (r + 1))
                    wait(pool, rp_done, 2 * r)
                    nc.gpsimd.tensor_tensor(RS[:, buf, :], RS[:, buf, :], st["sin"][:], ALU.mult).then_inc(rp_mult, 1)
                    pool.wait_ge(rp_mult, r + 1)
                    for rows, q, kk in ((slice(LAT, P), QE, KE), (slice(0, LAT), QO, KO)):
                        dst = q[rows, b % 2, :] if kind == "rope" else kk[rows, b, :]
                        nc.gpsimd.tensor_tensor(dst, RM[rows, buf, :], RS[rows, buf, :], ALU.add).then_inc(rp_done, 1)
            for b in range(BATCH):
                queries(0, b)
            with pool.Fori(1, PAIRS) as p:
                for b in range(BATCH):
                    queries(p, b)


def project(nc, layer, XN, st, x_src, gate, x_dst):
    n = f"pr{layer}"
    OL, WVO = st["OL"], st["WVO"]
    with ExitStack() as k:
        def sem(x):
            return k.enter_context(nc.semaphore(f"{n}_{x}"))
        X = k.enter_context(nc.sbuf_tensor(f"{n}_x", [P, DC, SEQ], F32))
        G = k.enter_context(nc.sbuf_tensor(f"{n}_g", [P, DC, SEQ], F32))
        o_ps = k.enter_context(nc.psum_tensor(f"{n}_o_ps", [P, DC, SEQ], F32))
        x_loaded, g_loaded, o_ready, gated, added, stored = map(sem, "x_loaded g_loaded o_ready gated added stored".split())
        block = k.enter_context(nc.Block())

        @block.sync
        def _(sp):
            def batch(b):
                wait(sp, added, b)
                sp.dma_start(X[:], x_src[:, :, at(b, SEQ)]).then_inc(x_loaded, 16)
                wait(sp, stored, 16 * b)
                sp.dma_start(G[:], gate[:, :, at(b, SEQ)]).then_inc(g_loaded, 16)
            batch(0)
            with sp.Fori(1, BATCH) as b:
                batch(b)
            sp.wait_ge(stored, 16 * BATCH)

        @block.tensor
        def _(pe):
            def batch(b):
                wait(pe, gated, b)
                for m in range(DC):
                    for p in range(PAIRS):
                        mm = nc.tensor.matmul(o_ps[:, m, :], WVO[:, p, m * P:(m + 1) * P], OL[:, p, at(b, SEQ)],
                                              start=p == 0, stop=p == PAIRS - 1)
                mm.then_inc(o_ready, 1)
            batch(0)
            with pe.Fori(1, BATCH) as b:
                batch(b)

        @block.vector
        def _(dve):
            with dve.Fori(0, BATCH) as b:
                dve.wait_ge(g_loaded, 16 * (b + 1))
                dve.wait_ge(o_ready, b + 1)
                nc.vector.tensor_tensor(G[:], G[:], o_ps[:], ALU.mult).then_inc(gated, 1)
                dve.wait_ge(x_loaded, 16 * (b + 1))
                dve.wait_ge(gated, b + 1)
                if layer == 0:
                    nc.vector.tensor_tensor(XN[:, :, at(b, SEQ)], G[:], X[:], ALU.add)
                nc.vector.tensor_tensor(G[:], G[:], X[:], ALU.add).then_inc(added, 1)

        @block.scalar
        def _(act):
            with act.Fori(0, BATCH) as b:
                act.wait_ge(added, b + 1)
                act.dma_start(x_dst[:, :, at(b, SEQ)], G[:]).then_inc(stored, 16)


def rope_tables(inv_freq):
    angle = np.arange(SEQ, dtype=np.float32)[:, None] * inv_freq.astype(np.float32)[None, :]
    row = (np.arange(P) % ROPE) // 2
    sign = np.where(np.arange(P) % 2 == 0, -1.0, 1.0).astype(np.float32)[:, None]
    cos, sin = np.cos(angle).astype(np.float32).T[row], np.sin(angle).astype(np.float32).T[row] * sign
    return np.ascontiguousarray(cos), np.ascontiguousarray(sin)


def chunks(w):
    return np.ascontiguousarray(w.reshape(-1, P, w.shape[1]).transpose(1, 0, 2))


def pad_rows(w, n):
    return np.concatenate([w, np.zeros((n - w.shape[0],) + w.shape[1:], w.dtype)], 0)


def layouts(d):
    f = {}
    half = ROPE // 2
    f["xT"] = np.ascontiguousarray(d["L0_attn_x"].reshape(T, D).T)
    inv0 = (1.0 / 10000.0 ** (np.arange(half, dtype=np.float32) / np.float32(half))).astype(np.float32)
    inv1 = (1.0 / 500000.0 ** (np.arange(0, ROPE, 2, dtype=np.float32) / np.float32(ROPE))).astype(np.float32)
    f["cos0"], f["sin0"] = rope_tables(inv0)
    f["cos1"], f["sin1"] = rope_tables(inv1)
    stack = lambda r, s: np.concatenate([d[r], d[s][None]], 0)
    wide = lambda w: np.ascontiguousarray(w.reshape(EXPERTS, DC, P, D).transpose(0, 2, 1, 3))
    column = lambda v: v.reshape(EXPERTS, DC, P, 1).transpose(0, 2, 1, 3)
    beside = lambda w, v: np.concatenate([w, column(v)], 3)
    f["w_up"] = beside(wide(stack("L0_ffn_Wup", "L0_ffn_Wsu")), stack("L0_ffn_bup", "L0_ffn_bsu"))
    f["w_gate"] = beside(wide(stack("L0_ffn_Wgate", "L0_ffn_Wsg")), stack("L0_ffn_bgate", "L0_ffn_bsg"))
    f["w_down"] = wide(stack("L0_ffn_Wdown", "L0_ffn_Wsd"))
    f["b_down"] = stack("L0_ffn_bdown", "L0_ffn_bsd")
    wr = np.zeros((D, EXPERTS), np.float32)
    wr[:, :ROUTED] = d["L0_ffn_Wr"]
    f["w_route"] = chunks(wr)
    f["b_route"], f["b_select"] = d["L0_ffn_br"][None], d["L0_ffn_gate_bias"][None]
    f["lane"] = np.arange(EXPERTS, 0, -1, dtype=np.float32)[None]
    def padded(i, rows, cols):
        o = np.full((rows, cols), LUT, np.int32)
        o[:i.shape[0], :i.shape[1]] = i
        return chunks(o).reshape(P, -1)
    f["index"] = np.concatenate([padded(d["L1_ffn_gate_idx"].T, D, INTER_PAD), padded(d["L1_ffn_up_idx"].T, D, INTER_PAD),
                                 padded(d["L1_ffn_down_idx"].T, INTER_PAD, D)], 1)
    f["lut"] = d["L1_ffn_lut"][None]
    mix = np.arange(ROPE).reshape(2, half).T.ravel()
    f["wq_down0"] = chunks(d["L0_attn_Wq_down"])
    f["wkv_down0"] = chunks(np.tile(d["L0_attn_Wkv_down"], (1, 2)))
    qn = d["L0_attn_Wq_up"].reshape(QR0, PAIRS, 2 * ND0).transpose(1, 2, 0)
    ku = d["L0_attn_Wk_up"].reshape(LAT, PAIRS, 2, ND0).transpose(1, 2, 3, 0)
    kn = np.zeros((PAIRS, 2, ND0, 2, LAT), np.float32)
    for e in range(2):
        kn[:, e, :, e] = ku[:, e]
    odd_first = lambda w: w.reshape(w.shape[0], PAIRS, 2, ROPE)[:, :, ::-1][..., mix].transpose(1, 0, 2, 3).reshape(PAIRS, w.shape[0], P)
    rope = odd_first(d["L0_attn_Wq_rope"])
    key = odd_first(d["L0_attn_Wk_rope"]).reshape(PAIRS, DC, P, P).transpose(0, 2, 1, 3)
    v = d["L0_attn_Wv_up"].reshape(LAT, PAIRS, 2, HD0).transpose(1, 3, 2, 0)
    o = d["L0_attn_Wo"].reshape(PAIRS, 2, HD0, D).transpose(0, 2, 1, 3)
    join = lambda *w: np.ascontiguousarray(np.concatenate([x.reshape(PAIRS, P, -1) for x in w], 2))
    f["stage0"] = join(qn, kn.reshape(PAIRS, P, P), rope, key, v, o)
    f["wq_down1"] = chunks(pad_rows(d["L1_attn_w_q_down"], 2 * P).T)
    wkv = d["L1_attn_w_kv_down"]
    f["wkv_down1"] = chunks(np.concatenate([wkv[:LAT], wkv[:LAT], wkv[LAT:], wkv[LAT:]], 0).T)
    f["norm_w1"] = np.ascontiguousarray(np.concatenate([pad_rows(d["L1_attn_q_norm_w"], 2 * P),
                                                        d["L1_attn_kv_norm_w"], d["L1_attn_kv_norm_w"]]).reshape(3, P).T)
    wq = d["L1_attn_w_q_up"].reshape(PAIRS, 2, QK1, Q_RANK1)
    qr = np.zeros((PAIRS, 2, QK1, 2 * P), np.float32)
    qr[..., :Q_RANK1] = wq
    qn = qr[:, :, :NOPE1].transpose(0, 2, 1, 3)
    rope = qr[:, ::-1, NOPE1:].reshape(PAIRS, P, 2, P).transpose(0, 3, 2, 1)
    kvu = d["L1_attn_w_kv_up"].reshape(PAIRS, 2, NOPE1 + VD1, LAT)
    kn, v = kvu[:, :, :NOPE1].transpose(0, 2, 1, 3), kvu[:, :, NOPE1:].transpose(0, 2, 1, 3)
    o = d["L1_attn_w_o"].T.reshape(PAIRS, 2, VD1, D).transpose(0, 2, 1, 3)
    f["stage1"] = join(qn, kn, rope, v, o)
    return f


def kernel(**inputs):
    import concourse.bacc as bacc
    from concourse.bass_utils import run_bass_kernel_spmd

    laid = layouts({name: np.asarray(v) for name, v in inputs.items()})
    nc = bacc.Bacc("TRN2", target_bir_lowering=False, num_devices=1)
    arrays, args = {}, {}
    for name, v in laid.items():
        v = np.ascontiguousarray(v)
        arrays[f"in_{name}"] = v
        args[name] = nc.dram_tensor(f"in_{name}", v.shape, mybir.dt.from_np(v.dtype), kind="ExternalInput").ap()
    out = nc.dram_tensor("outT", [D, T], F32, kind="ExternalOutput").ap()
    build(nc, args, out)
    r = run_bass_kernel_spmd(nc, [arrays], core_ids=[0])
    return np.ascontiguousarray(r.results[0]["outT"].T).reshape(BATCH, SEQ, D)
```

```python
from contextlib import ExitStack

import numpy as np

import concourse.bass as bass
from concourse import mybir

F32 = mybir.dt.float32
F32R = mybir.dt.float32r
BF16 = mybir.dt.bfloat16
I32 = mybir.dt.int32
ALU = mybir.AluOpType
ACT = mybir.ActivationFunctionType
AX = mybir.AxisListType

P = 128
D = 256
DC = D // P
BATCH, SEQ = 4, 512
T = BATCH * SEQ
QT = SEQ // P
HEADS = 16
PAIRS = HEADS // 2
LAT = 64
ROPE = 64
ND0, QR0, HD0 = 64, 128, 128
Q_RANK1, QK1, NOPE1, VD1 = 192, 192, 128, 128
EXPERTS = 8
ROUTED = 7
INTER, INTER_PAD = 688, 768
IT = INTER_PAD // P
LUT = 16
NEG = -1e30
BIG = 3e38
LN_EPS, RMS_EPS = 1e-5, 1e-6
SWAP = [i ^ 1 for i in range(32)]

STAGE0 = {"qn": 128, "kn": 128, "rope": 128, "key": 256, "v": 128, "o": 512}
STAGE1 = {"qn": 512, "kn": 128, "rope": 256, "v": 128, "o": 512}
LUT_COLS = 2 * 2 * INTER_PAD + IT * D
LUT_CHUNK = LUT_COLS // EXPERTS
HITS = 4


def at(i, n):
    return bass.ds(i * n, n)


def only(i):
    return i if isinstance(i, int) else bass.ds(i, 1)


def plain(ap):
    return ap.bitcast(F32)


def matmul3(nc, out, w_hi, w_lo, x_hi, x_lo, first, last):
    nc.tensor.matmul(out, w_hi, x_hi, start=first, stop=False)
    nc.tensor.matmul(out, w_hi, x_lo, start=False, stop=False)
    return nc.tensor.matmul(out, w_lo, x_hi, start=False, stop=last)


def wait(eng, sem, value):
    if isinstance(value, int) and value <= 0:
        return
    eng.wait_ge(sem, value)


def build(nc, a, out):
    with ExitStack() as top:
        def keep(name, shape, dt=F32):
            return top.enter_context(nc.sbuf_tensor(name, shape, dt))

        XH, XL = keep("normed_hi", [P, DC, T], F32R), keep("normed_lo", [P, DC, T], F32R)
        shared = keep("shared", [P, PAIRS * T])
        ident = keep("identity", [P, P])
        ident_b = keep("identity_bf16", [P, P], BF16)
        mask_b = keep("causal_mask_bf16", [P, P], BF16)
        ones = keep("ones", [P, P])
        x1_dram = nc.dram_tensor("x_after_layer0", [D, T], F32, kind="Internal").ap()
        gate_dram = nc.dram_tensor("gate", [D, T], F32, kind="Internal").ap()
        prob_dram = nc.dram_tensor("probs", [EXPERTS, T], F32, kind="Internal").ap()
        lut_dram = nc.dram_tensor("lut_weights", [P, LUT_COLS], F32, kind="Internal").ap()
        chunked = lambda t: t.rearrange("(c p) t -> p c t", p=P)
        xT, x1, gate = chunked(a["xT"]), chunked(x1_dram), chunked(gate_dram)

        constants(nc, a, ident, ident_b, mask_b, ones)
        layernorm(nc, shared, XH, XL, ones, xT, "ln0")
        mixture(nc, a, shared, XH, XL, ident, lut_dram, prob_dram, gate)
        attention(nc, a, 0, shared, XH, XL, ident, ident_b, mask_b, ones, xT, gate, x1)
        layernorm(nc, shared, XH, XL, ones, x1, "ln1")
        lut_ffn(nc, shared, XH, XL, lut_dram, gate)
        attention(nc, a, 1, shared, XH, XL, ident, ident_b, mask_b, ones, x1, gate, chunked(out))


def constants(nc, a, ident, ident_b, mask_b, ones):
    with ExitStack() as k:
        zeroed, made = k.enter_context(nc.semaphore("const_zeroed")), k.enter_context(nc.semaphore("const_made"))
        block = k.enter_context(nc.Block())

        @block.gpsimd
        def _(pool):
            nc.gpsimd.memset(ident[:], 0.0).then_inc(zeroed, 1)
            nc.gpsimd.memset(mask_b[:], 0.0).then_inc(zeroed, 1)
            nc.gpsimd.memset(ones[:], 1.0).then_inc(zeroed, 1)
            pool.wait_ge(zeroed, 3)
            nc.gpsimd.affine_select(out=ident[:], in_=ident[:], compare_op=ALU.not_equal, fill=1.0, base=0,
                                    pattern=[[-1, P]], channel_multiplier=1).then_inc(made, 1)
            nc.gpsimd.affine_select(out=mask_b[:], in_=mask_b[:], compare_op=ALU.is_ge, fill=NEG, base=0,
                                    pattern=[[-1, P]], channel_multiplier=1).then_inc(made, 1)

        @block.vector
        def _(dve):
            dve.wait_ge(made, 2)
            nc.vector.tensor_copy(ident_b[:], ident[:]).then_inc(made, 1)


def layernorm(nc, shared, XH, XL, ones, src, name):
    XN = shared[:, 0:DC * T].rearrange("p (c t) -> p c t", c=DC)
    with ExitStack() as k:
        def sem(n):
            return k.enter_context(nc.semaphore(f"{name}_{n}"))

        def sb(n, shape):
            return k.enter_context(nc.sbuf_tensor(f"{name}_{n}", shape, F32))
        squares = sb("squares", [P, 2, DC, SEQ])
        dev, rstd, eps = sb("dev", [P, 2, SEQ]), sb("rstd", [P, 2, SEQ]), sb("eps", [P, 1])
        mean_ps = k.enter_context(nc.psum_tensor(f"{name}_mean_ps", [P, 2, SEQ], F32))
        var_ps = k.enter_context(nc.psum_tensor(f"{name}_var_ps", [P, 2, SEQ], F32))
        has_eps, mean_ready, centred, squared, var_ready, dev_ready, rstd_ready, normed, split_hi, split_lo = map(
            sem, "has_eps mean_ready centred squared var_ready dev_ready rstd_ready normed split_hi split_lo".split())
        loaded = [sem(f"loaded{b}") for b in range(BATCH)]
        of = lambda t, b: t[:, :, b * SEQ:(b + 1) * SEQ]
        block = k.enter_context(nc.Block())

        @block.sync
        def _(sp):
            for b in range(BATCH):
                sp.dma_start(of(XN, b), of(src, b)).then_inc(loaded[b], 16)

        @block.tensor
        def _(pe):
            def mean(b):
                pe.wait_ge(loaded[b], 16)
                wait(pe, centred, b - 1)
                for c in range(DC):
                    mm = nc.tensor.matmul(mean_ps[:, b % 2, :], ones[:], of(XN, b)[:, c, :], start=c == 0, stop=c == DC - 1)
                mm.then_inc(mean_ready, 1)

            def variance(b):
                pe.wait_ge(squared, b + 1)
                wait(pe, dev_ready, b - 1)
                for c in range(DC):
                    mm = nc.tensor.matmul(var_ps[:, b % 2, :], ones[:], squares[:, b % 2, c, :], start=c == 0, stop=c == DC - 1)
                mm.then_inc(var_ready, 1)
            for b in range(BATCH + 1):
                if b < BATCH:
                    mean(b)
                if b >= 1:
                    variance(b - 1)

        @block.vector
        def _(dve):
            nc.vector.memset(eps[:], LN_EPS).then_inc(has_eps, 1)

            def centre(b):
                dve.wait_ge(mean_ready, b + 1)
                for c in range(DC):
                    x = of(XN, b)[:, c, :]
                    ins = nc.vector.scalar_tensor_tensor(out=x, in0=mean_ps[:, b % 2, :], scalar=-1.0 / D, in1=x,
                                                         op0=ALU.mult, op1=ALU.add)
                ins.then_inc(centred, 1)

            def normalise(b):
                dve.wait_ge(dev_ready, b + 1)
                nc.vector.reciprocal(rstd[:, b % 2, :], dev[:, b % 2, :]).then_inc(rstd_ready, 1)
                dve.wait_ge(rstd_ready, b + 1)
                nc.vector.tensor_tensor(of(XN, b), of(XN, b), rstd[:, b % 2, :].unsqueeze(1).to_broadcast([P, DC, SEQ]),
                                        ALU.mult).then_inc(normed, 1)
                dve.wait_ge(split_hi, b + 1)
                nc.vector.tensor_tensor(of(XL, b), of(XN, b), plain(of(XH, b)), ALU.subtract).then_inc(split_lo, 1)
            for b in range(BATCH + 1):
                if b < BATCH:
                    centre(b)
                if b >= 1:
                    normalise(b - 1)

        @block.scalar
        def _(act):
            act.wait_ge(has_eps, 1)
            for b in range(BATCH + 1):
                if b < BATCH:
                    act.wait_ge(centred, b + 1)
                    wait(act, var_ready, b - 1)
                    nc.scalar.activation(squares[:, b % 2, :, :], of(XN, b), ACT.Square).then_inc(squared, 1)
                if b >= 1:
                    act.wait_ge(var_ready, b)
                    wait(act, rstd_ready, b - 2)
                    nc.scalar.activation(dev[:, (b - 1) % 2, :], var_ps[:, (b - 1) % 2, :], ACT.Sqrt, bias=eps[:, 0:1],
                                         scale=1.0 / D).then_inc(dev_ready, 1)
                    act.wait_ge(normed, b)
                    nc.scalar.activation(of(XH, b - 1), of(XN, b - 1), ACT.Copy).then_inc(split_hi, 1)


def mixture(nc, a, shared, XH, XL, ident, lut_dram, prob_dram, gate):
    TT = T // P
    at_ = np.cumsum([0, DC * T, DC * T, T, 2 * DC * SEQ, DC * SEQ, DC * SEQ, DC * SEQ]).tolist()
    XN, acc, probT, U, G, SG, UP = (shared[:, x:y] for x, y in zip(at_, at_[1:]))
    XN, acc, G, SG, UP = (t.rearrange("p (c t) -> p c t", c=DC) for t in (XN, acc, G, SG, UP))
    U = U.rearrange("p (b c t) -> p b c t", b=2, c=DC)
    with ExitStack() as k:
        sems = []

        def sem(n):
            sems.append(nc.alloc_semaphore(name=f"moe_{n}"))
            return sems[-1]

        def sb(n, shape, dt=F32):
            return k.enter_context(nc.sbuf_tensor(f"moe_{n}", shape, dt))

        def ps(n, shape):
            return k.enter_context(nc.psum_tensor(f"moe_{n}", shape, F32))
        raw = {n: sb(f"raw_{n}", [P, DC, D]) for n in ("up", "gate", "down")}
        hi = {n: sb(f"hi_{n}", [P, DC, D], F32R) for n in raw}
        lo = {n: sb(f"lo_{n}", [P, DC, D], F32R) for n in raw}
        b_up, b_gate = sb("b_up", [P, DC]), sb("b_gate", [P, DC])
        b_down = sb("b_down", [P, D])
        w_route, b_route, b_select = sb("w_route", [P, DC, EXPERTS]), sb("b_route", [P, ROUTED]), sb("b_select", [P, ROUTED])
        index, table = sb("index", [P, LUT_COLS], I32), sb("table", [P, LUT])
        hit, lut_sum = sb("hit", [P, HITS, LUT_CHUNK]), sb("lut_sum", [P, LUT_CHUNK])
        prob_b = sb("prob_b", [P, BATCH, SEQ])
        UH, UL, GH, GL = (sb(n, [P, 2, DC, SEQ], F32R) for n in ("UH", "UL", "GH", "GL"))
        rt = [sb(f"route{i}", [P, TT, EXPERTS]) for i in range(6)]
        r1 = [sb(f"route_row{i}", [P, TT]) for i in range(8)]
        lane = sb("lane", [P, EXPERTS])
        up_ps, gate_ps, down_ps = (ps(n, [P, DC, SEQ]) for n in ("up_ps", "gate_ps", "down_ps"))
        route_ps = ps("route_ps", [P, TT, EXPERTS])
        turn_ps = ps("turn_ps", [EXPERTS, SEQ])
        (loaded, zeroed, lanes, routed, chain, expd, prob_ready, turned, turn_copied, prob_stored,
         up_loaded, gate_loaded, down_loaded, bias_ready, acc_ready, up_ready, up_copied, gate_ready, silu_done,
         scaled, glu_done, down_ready, added, lut_hit, lut_added, gated, stored) = map(sem, (
             "loaded zeroed lanes routed chain expd prob_ready turned turn_copied prob_stored "
             "up_loaded gate_loaded down_loaded bias_ready acc_ready up_ready up_copied gate_ready silu_done "
             "scaled glu_done down_ready added lut_hit lut_added gated stored").split())
        up_hi, up_lo, glu_hi, glu_lo, ups_biased, gates_biased = (
            sem(n) for n in "up_hi up_lo glu_hi glu_lo ups_biased gates_biased".split())
        lut_stored = sem("lut_stored")
        w_hi = {n: sem(f"w_hi_{n}") for n in raw}
        w_lo = {n: sem(f"w_lo_{n}") for n in raw}
        prob_bcast = [sem(f"prob_bcast{b}") for b in range(BATCH)]
        LOADS = 16 * 7

        def a_row(dram, e, b):
            return dram[bass.ds(e, 1), b * SEQ:(b + 1) * SEQ].to_broadcast([P, SEQ])
        block = k.enter_context(nc.Block())

        @block.sync
        def _(sp):
            sp.dma_start(w_route[:], a["w_route"]).then_inc(loaded, 16)
            sp.dma_start(b_route[:], a["b_route"].partition_broadcast(P)).then_inc(loaded, 16)
            sp.dma_start(b_select[:], a["b_select"].partition_broadcast(P)).then_inc(loaded, 16)
            sp.dma_start(table[:], a["lut"].partition_broadcast(P)).then_inc(loaded, 16)
            sp.wait_ge(zeroed, 2)
            sp.dma_start(b_down[0:EXPERTS, :], a["b_down"]).then_inc(loaded, 16)
            sp.dma_start(index[:], a["index"]).then_inc(loaded, 16)
            sp.dma_start(lane[:], a["lane"].partition_broadcast(P)).then_inc(loaded, 16)

            arrived = {"up": up_loaded, "gate": gate_loaded, "down": down_loaded}

            def load(e):
                for n in raw:
                    wait(sp, w_lo[n], e)
                    sp.dma_start(raw[n][:], a[f"w_{n}"][e]).then_inc(arrived[n], 16)
                wait(sp, up_copied, BATCH * e)
                sp.dma_start(b_up[:], a["b_up"][e]).then_inc(ups_biased, 16)
                if isinstance(e, int):
                    sp.wait_ge(prob_stored, 16)
                for b in range(BATCH):
                    if b == 2 and not isinstance(e, int):
                        store_weights(e - 1)
                    if b == 1:
                        wait(sp, silu_done, BATCH * e)
                        sp.dma_start(b_gate[:], a["b_gate"][e]).then_inc(gates_biased, 16)
                    wait(sp, scaled, BATCH * (e - 1) + b + 1)
                    sp.dma_start(prob_b[:, b, :], a_row(prob_dram, e, b)).then_inc(prob_bcast[b], 16)

            def store_weights(chunk):
                sp.wait_ge(lut_added, (LUT - 1) * (chunk + 1))
                sp.dma_start(lut_dram[:, at(chunk, LUT_CHUNK)], lut_sum[:]).then_inc(lut_stored, 16)
            load(0)
            with sp.Fori(1, EXPERTS) as e:
                load(e)
            store_weights(EXPERTS - 1)
            for b in range(BATCH):
                sp.wait_ge(gated, b + 1)
                sp.dma_start(gate[:, :, b * SEQ:(b + 1) * SEQ], acc[:, :, b * SEQ:(b + 1) * SEQ]).then_inc(stored, 16)
            sp.wait_ge(stored, 16 * BATCH)
            sp.wait_ge(lut_stored, 16 * EXPERTS)

        @block.gpsimd
        def _(pool):
            pool.memset(probT, 0.0).then_inc(zeroed, 1)
            pool.memset(b_down[:], 0.0).then_inc(zeroed, 1)

            def low(n, e):
                pool.wait_ge(w_hi[n], e + 1)
                nc.gpsimd.tensor_tensor(lo[n][:], raw[n][:], plain(hi[n][:]), ALU.subtract).then_inc(w_lo[n], 1)

            def add_hits(chunk, b):
                for v in range(max(1, b * LUT // BATCH), (b + 1) * LUT // BATCH):
                    n = chunk * (LUT - 1) + v - 1
                    pool.wait_ge(lut_hit, LUT * chunk + v + 1)
                    wait(pool, lut_added, n)
                    if v == 1:
                        wait(pool, lut_stored, 16 * chunk)
                    before = hit[:, 0, :] if v == 1 else lut_sum[:]
                    nc.gpsimd.tensor_tensor(lut_sum[:], before, hit[:, v % HITS, :], ALU.add).then_inc(lut_added, 1)

            def steps(e, last):
                for b in range(BATCH):
                    if b == 0:
                        low("gate", e)
                    if b == 1:
                        low("down", e)
                    if b == 3 and not last:
                        low("up", e + 1)
                    add_hits(e, b)
            low("up", 0)
            pool.wait_ge(turn_copied, BATCH)
            pool.dma_start(prob_dram, probT[0:EXPERTS, :]).then_inc(prob_stored, 16)
            steps(0, False)
            with pool.Fori(1, EXPERTS - 1) as e:
                steps(e, False)
            steps(EXPERTS - 1, True)
            pool.wait_ge(prob_stored, 16)

        @block.tensor
        def _(pe):
            pe.wait_ge(loaded, LOADS)
            for t in range(TT):
                for c in range(DC):
                    mm = nc.tensor.matmul(route_ps[:, t, :], XN[:, c, t * P:(t + 1) * P], w_route[:, c, :],
                                          start=c == 0, stop=c == DC - 1)
            mm.then_inc(routed, 1)

            def product(out, n, e, b, x_hi, x_lo):
                if b == 0:
                    pe.wait_ge(w_lo[n], e + 1)
                for m in range(DC):
                    for c in range(DC):
                        cols = slice(m * P, (m + 1) * P)
                        mm = matmul3(nc, out[:, m, :], hi[n][:, c, cols], lo[n][:, c, cols], x_hi[:, c, :], x_lo[:, c, :],
                                     c == 0, c == DC - 1)
                return mm

            def up(e, b):
                wait(pe, up_copied, BATCH * e + b)
                sl = slice(b * SEQ, (b + 1) * SEQ)
                product(up_ps, "up", e, b, XH[:, :, sl], XL[:, :, sl]).then_inc(up_ready, 1)

            def gating(e, b):
                wait(pe, silu_done, BATCH * e + b)
                pe.wait_ge(up_lo, BATCH * e + b + 1)
                product(gate_ps, "gate", e, b, UH[:, b % 2], UL[:, b % 2]).then_inc(gate_ready, 1)

            def down(e, b):
                wait(pe, added, BATCH * e + b)
                pe.wait_ge(glu_lo, BATCH * e + b + 1)
                product(down_ps, "down", e, b, GH[:, b % 2], GL[:, b % 2]).then_inc(down_ready, 1)

            def steps(e, first):
                for b in range(BATCH):
                    up(e, b)
                    if b >= 1 or not first:
                        gating(*((e, b - 1) if b >= 1 else (e - 1, BATCH - 1)))
                    if b >= 2 or not first:
                        down(*((e, b - 2) if b >= 2 else (e - 1, b + BATCH - 2)))
                    if first and b == 0:
                        turn()

            def turn():
                pe.wait_ge(prob_ready, 1)
                for b in range(BATCH):
                    wait(pe, turn_copied, b)
                    for t in range(QT):
                        mm = nc.tensor.transpose(turn_ps[:, t * P:(t + 1) * P], rt[5][:, b * QT + t, :], ident[:])
                    mm.then_inc(turned, 1)
                for b in range(BATCH):
                    pe.wait_ge(turn_copied, BATCH)
                    wait(pe, acc_ready, b)
                    for m in range(DC):
                        mm = nc.tensor.matmul(down_ps[:, m, :], b_down[:, m * P:(m + 1) * P],
                                              probT[:, b * SEQ:(b + 1) * SEQ], start=True, stop=True)
                    mm.then_inc(bias_ready, 1)
                pe.wait_ge(acc_ready, BATCH)

            steps(0, True)
            with pe.Fori(1, EXPERTS) as e:
                steps(e, False)
            gating(EXPERTS - 1, BATCH - 1)
            down(EXPERTS - 1, BATCH - 2)
            down(EXPERTS - 1, BATCH - 1)

        @block.scalar
        def _(act):
            act.wait_ge(loaded, LOADS)
            for i, n in enumerate((4, 5)):
                act.wait_ge(expd, i + 1)
                nc.scalar.activation(r1[n][:], r1[n][:], ACT.Exp).then_inc(chain, 1)

            arrived = {"up": up_loaded, "gate": gate_loaded, "down": down_loaded}
            used = {"up": up_ready, "gate": gate_ready, "down": down_ready}

            def high(n, e):
                act.wait_ge(arrived[n], 16 * (e + 1))
                wait(act, used[n], BATCH * e)
                nc.scalar.activation(hi[n][:], raw[n][:], ACT.Copy).then_inc(w_hi[n], 1)

            def copy_up(e, b):
                t = BATCH * e + b
                if b == 0:
                    act.wait_ge(ups_biased, 16 * (e + 1))
                act.wait_ge(up_ready, t + 1)
                wait(act, scaled, t - 1)
                for m in range(DC):
                    ins = nc.scalar.activation(U[:, b % 2, m, :], up_ps[:, m, :], ACT.Identity, bias=b_up[:, m:m + 1])
                ins.then_inc(up_copied, 1)
                act.wait_ge(up_copied, t + 1)
                wait(act, gate_ready, t - 1)
                nc.scalar.activation(UH[:, b % 2], U[:, b % 2], ACT.Copy).then_inc(up_hi, 1)

            def silu(e, b):
                t = BATCH * e + b
                if b == 0:
                    act.wait_ge(gates_biased, 16 * (e + 1))
                act.wait_ge(gate_ready, t + 1)
                wait(act, glu_done, t)
                for m in range(DC):
                    ins = nc.scalar.activation(SG[:, m, :], gate_ps[:, m, :], ACT.Silu, bias=b_gate[:, m:m + 1])
                ins.then_inc(silu_done, 1)

            def glu_high(e, b):
                t = BATCH * e + b
                act.wait_ge(glu_done, t + 1)
                wait(act, down_ready, t - 1)
                nc.scalar.activation(GH[:, b % 2], G[:], ACT.Copy).then_inc(glu_hi, 1)

            def steps(e, first, last):
                for b in range(BATCH):
                    before = (e, b - 1) if b >= 1 else (e - 1, BATCH - 1)
                    copy_up(e, b)
                    if b >= 1 or not first:
                        silu(*before)
                    if b == 0:
                        high("gate", e)
                    if b >= 1 or not first:
                        glu_high(*before)
                    if b == 1:
                        high("down", e)
                    if b == 3 and not last:
                        high("up", e + 1)
            high("up", 0)
            steps(0, True, False)
            with act.Fori(1, EXPERTS - 1) as e:
                steps(e, False, False)
            steps(EXPERTS - 1, False, True)
            silu(EXPERTS - 1, BATCH - 1)
            glu_high(EXPERTS - 1, BATCH - 1)
            for b in range(BATCH):
                act.wait_ge(added, BATCH * (EXPERTS - 1) + b + 1)
                sl = acc[:, :, b * SEQ:(b + 1) * SEQ]
                nc.scalar.activation(sl, sl, ACT.Silu).then_inc(gated, 1)

        @block.vector
        def _(dve):
            V = nc.vector
            links = [0]

            def link(ins):
                links[0] += 1
                ins.then_inc(lanes, 1)
                dve.wait_ge(lanes, links[0])
            wide = lambda row: row[:].unsqueeze(2).to_broadcast([P, TT, EXPERTS])
            every = lambda v: v[:].unsqueeze(1).to_broadcast([P, TT, v.shape[1]])
            logits, select, pick1, pick2, tmp, probs = rt
            top, place, g1, g2, e1, e2, both, inv = r1
            dve.wait_ge(loaded, LOADS)
            dve.wait_ge(routed, 1)
            link(V.memset(select[:], -BIG))
            link(V.memset(logits[:], 0.0))
            link(V.tensor_tensor(logits[:, :, 0:ROUTED], route_ps[:, :, 0:ROUTED], every(b_route), ALU.add))
            link(V.tensor_tensor(select[:, :, 0:ROUTED], logits[:, :, 0:ROUTED], every(b_select), ALU.add))
            for pick in (pick1, pick2):
                link(V.tensor_reduce(top[:], select[:], AX.X, ALU.max))
                link(V.tensor_tensor(tmp[:], select[:], wide(top), ALU.is_equal))
                link(V.tensor_tensor(tmp[:], tmp[:], every(lane), ALU.mult))
                link(V.tensor_reduce(place[:], tmp[:], AX.X, ALU.max))
                link(V.tensor_tensor(pick[:], tmp[:], wide(place), ALU.is_equal))
                link(V.scalar_tensor_tensor(out=select[:], in0=pick[:], scalar=-BIG, in1=select[:],
                                            op0=ALU.mult, op1=ALU.add))
            for pick, g in ((pick1, g1), (pick2, g2)):
                link(V.tensor_tensor(tmp[:], pick[:], logits[:], ALU.mult))
                link(V.tensor_reduce(g[:], tmp[:], AX.X, ALU.add))
            link(V.tensor_tensor(both[:], g1[:], g2[:], ALU.max))
            V.tensor_tensor(e1[:], g1[:], both[:], ALU.subtract).then_inc(expd, 1)
            V.tensor_tensor(e2[:], g2[:], both[:], ALU.subtract).then_inc(expd, 1)
            dve.wait_ge(chain, 2)
            link(V.tensor_tensor(both[:], e1[:], e2[:], ALU.add))
            link(V.reciprocal(inv[:], both[:]))
            for pick, e in ((pick1, e1), (pick2, e2)):
                link(V.tensor_tensor(e[:], e[:], inv[:], ALU.mult))
                link(V.tensor_tensor(pick[:], pick[:], wide(e), ALU.mult))
            link(V.tensor_tensor(probs[:], pick1[:], pick2[:], ALU.add))
            V.memset(probs[:, :, ROUTED:EXPERTS], 1.0).then_inc(prob_ready, 1)
            dve.wait_ge(zeroed, 1)
            for b in range(BATCH):
                dve.wait_ge(turned, b + 1)
                V.tensor_copy(probT[0:EXPERTS, b * SEQ:(b + 1) * SEQ], turn_ps[:]).then_inc(turn_copied, 1)
            for b in range(BATCH):
                dve.wait_ge(bias_ready, b + 1)
                V.tensor_copy(acc[:, :, b * SEQ:(b + 1) * SEQ], down_ps[:]).then_inc(acc_ready, 1)

            def up_low(e, b):
                t = BATCH * e + b
                dve.wait_ge(up_hi, t + 1)
                V.tensor_tensor(UL[:, b % 2], U[:, b % 2], plain(UH[:, b % 2]), ALU.subtract).then_inc(up_lo, 1)
                dve.wait_ge(prob_bcast[b], 16 * (e + 1))
                wait(dve, glu_done, t)
                V.tensor_tensor(UP[:], U[:, b % 2], prob_b[:, b, :].unsqueeze(1).to_broadcast([P, DC, SEQ]),
                                ALU.mult).then_inc(scaled, 1)

            def glu(e, b):
                t = BATCH * e + b
                dve.wait_ge(scaled, t + 1)
                dve.wait_ge(silu_done, t + 1)
                wait(dve, glu_lo, t)
                V.tensor_tensor(G[:], UP[:], SG[:], ALU.mult).then_inc(glu_done, 1)

            def glu_low(e, b):
                t = BATCH * e + b
                dve.wait_ge(glu_hi, t + 1)
                V.tensor_tensor(GL[:, b % 2], G[:], plain(GH[:, b % 2]), ALU.subtract).then_inc(glu_lo, 1)

            def accumulate(e, b):
                dve.wait_ge(down_ready, BATCH * e + b + 1)
                wait(dve, added, BATCH * e + b - 1)
                sl = acc[:, :, b * SEQ:(b + 1) * SEQ]
                V.tensor_tensor(sl, sl, down_ps[:], ALU.add).then_inc(added, 1)

            def look_up(chunk, v):
                cols = at(chunk, LUT_CHUNK)
                wait(dve, lut_added, chunk * (LUT - 1) + (max(v - HITS, 1) if v >= HITS else v - HITS + 1))
                V.tensor_scalar(hit[:, v % HITS, :], index[:, cols], float(v), table[:, v:v + 1],
                                ALU.is_equal, ALU.mult).then_inc(lut_hit, 1)

            def steps(e, first):
                for b in range(BATCH):
                    before = (e, b - 1) if b >= 1 else (e - 1, BATCH - 1)
                    v = b * LUT // BATCH
                    if b >= 1 or not first:
                        glu(*before)
                    look_up(e, v)
                    look_up(e, v + 1)
                    up_low(e, b)
                    if b >= 1 or not first:
                        glu_low(*before)
                    look_up(e, v + 2)
                    look_up(e, v + 3)
                    if b >= 2 or not first:
                        accumulate(*((e, b - 2) if b >= 2 else (e - 1, b + BATCH - 2)))
            steps(0, True)
            with dve.Fori(1, EXPERTS) as e:
                steps(e, False)
            glu(EXPERTS - 1, BATCH - 1)
            glu_low(EXPERTS - 1, BATCH - 1)
            accumulate(EXPERTS - 1, BATCH - 2)
            accumulate(EXPERTS - 1, BATCH - 1)
    nc.clear_and_free_semaphores(sems)
    nc.all_engine_barrier()


def lut_ffn(nc, shared, XH, XL, lut_dram, gate):
    PARTS = 3
    COLS = LUT_COLS // PARTS
    with ExitStack() as k:
        def sem(n):
            return k.enter_context(nc.semaphore(f"ffn_{n}"))

        def sb(n, shape, dt=F32):
            return k.enter_context(nc.sbuf_tensor(f"ffn_{n}", shape, dt))
        raw = shared[:, 0:LUT_COLS]
        WH, WL = sb("WH", [P, LUT_COLS], F32R), sb("WL", [P, LUT_COLS], F32R)
        HF, HH, HL = sb("HF", [P, 2, SEQ]), sb("HH", [P, IT, SEQ], F32R), sb("HL", [P, IT, SEQ], F32R)
        SG, GO = sb("SG", [P, 2, SEQ]), sb("out", [P, DC, SEQ])
        g_ps = k.enter_context(nc.psum_tensor("ffn_g_ps", [P, 2, SEQ], F32))
        u_ps = k.enter_context(nc.psum_tensor("ffn_u_ps", [P, 2, SEQ], F32))
        d_ps = k.enter_context(nc.psum_tensor("ffn_d_ps", [P, DC, SEQ], F32))
        w_hi, w_lo, g_ready, u_ready, silu_done, h_done, h_hi, h_lo, d_ready, gated, stored = map(
            sem, "w_hi w_lo g_ready u_ready silu_done h_done h_hi h_lo d_ready gated stored".split())
        loaded = [sem(f"loaded{i}") for i in range(PARTS)]
        part = lambda t, i: t[:, i * COLS:(i + 1) * COLS]
        chunk = lambda t, i, n: part(t, i).rearrange("p (c n) -> p c n", c=n)
        block = k.enter_context(nc.Block())

        @block.tensor
        def _(pe):
            def up(b, m):
                i = IT * b + m
                wait(pe, h_done, i - 1)
                cols = slice(m * P, (m + 1) * P)
                for w, o, s in ((0, g_ps, g_ready), (1, u_ps, u_ready)):
                    if isinstance(b, int) and m == 0:
                        pe.wait_ge(w_lo, w + 1)
                    wh, wl = chunk(WH, w, DC), chunk(WL, w, DC)
                    for c in range(DC):
                        mm = matmul3(nc, o[:, m % 2, :], wh[:, c, cols], wl[:, c, cols], XH[:, c, at(b, SEQ)],
                                     XL[:, c, at(b, SEQ)], c == 0, c == DC - 1)
                    mm.then_inc(s, 1)

            def batch(b):
                wh, wl = chunk(WH, 2, IT), chunk(WL, 2, IT)
                for m in range(IT):
                    up(b, m)
                wait(pe, gated, b)
                if isinstance(b, int):
                    pe.wait_ge(w_lo, PARTS)
                for c in range(IT):
                    pe.wait_ge(h_lo, IT * b + c + 1)
                    for m in range(DC):
                        cols = slice(m * P, (m + 1) * P)
                        mm = matmul3(nc, d_ps[:, m, :], wh[:, c, cols], wl[:, c, cols], HH[:, c, :], HL[:, c, :],
                                     c == 0, c == IT - 1)
                mm.then_inc(d_ready, 1)
            batch(0)
            with pe.Fori(1, BATCH) as b:
                batch(b)

        @block.scalar
        def _(act):
            for i in range(PARTS):
                act.wait_ge(loaded[i], 16)
                nc.scalar.activation(part(WH, i), part(raw, i), ACT.Copy).then_inc(w_hi, 1)

            def high(b, m):
                i = IT * b + m
                act.wait_ge(h_done, i + 1)
                nc.scalar.activation(HH[:, m, :], HF[:, m % 2, :], ACT.Copy).then_inc(h_hi, 1)

            def batch(b):
                for m in range(IT):
                    i = IT * b + m
                    act.wait_ge(g_ready, i + 1)
                    wait(act, h_done, i - 1)
                    nc.scalar.activation(SG[:, m % 2, :], g_ps[:, m % 2, :], ACT.Silu).then_inc(silu_done, 1)
                    if m == 1:
                        wait(act, d_ready, b)
                    if m >= 1:
                        high(b, m - 1)
                high(b, IT - 1)
                act.wait_ge(d_ready, b + 1)
                wait(act, stored, 16 * b)
                nc.scalar.activation(GO[:], d_ps[:], ACT.Silu).then_inc(gated, 1)
            batch(0)
            with act.Fori(1, BATCH) as b:
                batch(b)

        @block.vector
        def _(dve):
            for i in range(PARTS):
                dve.wait_ge(w_hi, i + 1)
                nc.vector.tensor_tensor(part(WL, i), part(raw, i), plain(part(WH, i)), ALU.subtract).then_inc(w_lo, 1)

            def low(b, m):
                i = IT * b + m
                dve.wait_ge(h_hi, i + 1)
                nc.vector.tensor_tensor(HL[:, m, :], HF[:, m % 2, :], plain(HH[:, m, :]), ALU.subtract).then_inc(h_lo, 1)

            def batch(b):
                for m in range(IT):
                    i = IT * b + m
                    dve.wait_ge(silu_done, i + 1)
                    dve.wait_ge(u_ready, i + 1)
                    wait(dve, h_lo, i - 1)
                    nc.vector.tensor_tensor(HF[:, m % 2, :], SG[:, m % 2, :], u_ps[:, m % 2, :], ALU.mult).then_inc(h_done, 1)
                    if m >= 1:
                        low(b, m - 1)
                low(b, IT - 1)
            batch(0)
            with dve.Fori(1, BATCH) as b:
                batch(b)

        @block.sync
        def _(sp):
            for i in range(PARTS):
                sp.dma_start(part(raw, i), part(lut_dram, i)).then_inc(loaded[i], 16)
            with sp.Fori(0, BATCH) as b:
                sp.wait_ge(gated, b + 1)
                sp.dma_start(gate[:, :, at(b, SEQ)], GO[:]).then_inc(stored, 16)
            sp.wait_ge(stored, 16 * BATCH)


def attention(nc, a, layer, shared, XH, XL, ident, ident_b, mask_b, ones, x_src, gate, x_dst):
    with ExitStack() as k:
        def sb(n, shape, dt=F32):
            return k.enter_context(nc.sbuf_tensor(f"at{layer}_{n}", shape, dt))
        st = {
            "QH": XH if layer else sb("latent_q_hi", [P, 1, T], F32R), "QL": XL if layer else sb("latent_q_lo", [P, 1, T], F32R),
            "KE": sb("KE", [P, BATCH, SEQ]), "KO": sb("KO", [P, BATCH, SEQ]),
            "V": sb("V", [P, BATCH * QT, LAT]),
            "OL": shared[:].rearrange("p (k t) -> p k t", k=PAIRS),
            "WVO": sb("WVO", [P, PAIRS, D]),
            "cos": sb("cos", [P, SEQ]), "sin": sb("sin", [P, SEQ]),
        }
        latents(nc, a, layer, XH, XL, ident, ones, st)
        heads(nc, a, layer, XH, XL, ident, ident_b, mask_b, st)
        project(nc, layer, st, x_src, gate, x_dst)


def latents(nc, a, layer, XH, XL, ident, ones, st):
    n = f"lat{layer}"
    KQ = layer + 1
    with ExitStack() as k:
        def sem(x):
            return k.enter_context(nc.semaphore(f"{n}_{x}"))

        def sb(x, shape, dt=F32):
            return k.enter_context(nc.sbuf_tensor(f"{n}_{x}", shape, dt))

        def ps(x, shape):
            return k.enter_context(nc.psum_tensor(f"{n}_{x}", shape, F32))
        w = sb("w", [P, 2, DC, KQ * P])
        WH, WL = sb("WH", [P, 2, DC, KQ * P], F32R), sb("WL", [P, 2, DC, KQ * P], F32R)
        CF = sb("CF", [P, 2, SEQ])
        normw = sb("normw", [P, KQ + 1])
        KV, RM, RS = sb("KV", [P, SEQ]), sb("RM", [P, SEQ]), sb("RS", [P, SEQ])
        SQ, dev, rstd = sb("SQ", [P, 3, SEQ]), sb("dev", [P, 2, SEQ]), sb("rstd", [P, 2, SEQ])
        eps = sb("eps", [P, 2])
        q_ps, k_ps, v_ps = ps("q_ps", [P, KQ, SEQ]), ps("k_ps", [P, KQ, SEQ]), ps("v_ps", [P, SEQ])
        m_ps = ps("m_ps", [P, 2, SEQ])
        (loaded, has_eps, q_ready, k_ready, q_done, squared, sums_ready, dev_ready, rstd_ready, kv_ready, k_done,
         roped, rope_done, v_ready, v_done, w_hi, w_lo, q_hi, q_lo) = map(sem, (
             "loaded has_eps q_ready k_ready q_done squared sums_ready dev_ready rstd_ready kv_ready k_done "
             "roped rope_done v_ready v_done w_hi w_lo q_hi q_lo").split())
        KE, KO, QH, QL, V = (st[x] for x in ("KE", "KO", "QH", "QL", "V"))
        LOADS = 16 * (4 + layer)
        block = k.enter_context(nc.Block())

        @block.sync
        def _(sp):
            sp.dma_start(w[:, 0], a[f"wq_down{layer}"]).then_inc(loaded, 16)
            sp.dma_start(w[:, 1], a[f"wkv_down{layer}"]).then_inc(loaded, 16)
            sp.dma_start(st["cos"][:], a[f"cos{layer}"]).then_inc(loaded, 16)
            sp.dma_start(st["sin"][:], a[f"sin{layer}"]).then_inc(loaded, 16)
            if layer == 1:
                sp.dma_start(normw[:], a["norm_w1"]).then_inc(loaded, 16)

        @block.tensor
        def _(pe):
            pe.wait_ge(w_lo, 1)

            def product(out, n, b):
                for m in range(KQ):
                    for c in range(DC):
                        cols = slice(m * P, (m + 1) * P)
                        mm = matmul3(nc, out[:, m, :], WH[:, n, c, cols], WL[:, n, c, cols], XH[:, c, at(b, SEQ)],
                                     XL[:, c, at(b, SEQ)], c == 0, c == DC - 1)
                return mm

            def batch(b):
                wait(pe, q_done, b)
                product(q_ps, 0, b).then_inc(q_ready, 1)
                wait(pe, kv_ready, b)
                wait(pe, roped, 2 * b * layer)
                product(k_ps, 1, b).then_inc(k_ready, 1)
                if layer == 1:
                    pe.wait_ge(squared, 2 * b + 1)
                    for c in range(KQ):
                        mm = nc.tensor.matmul(m_ps[:, 0, :], ones[:], SQ[:, c, :], start=c == 0, stop=c == KQ - 1)
                    mm.then_inc(sums_ready, 1)
                    pe.wait_ge(squared, 2 * b + 2)
                    nc.tensor.matmul(m_ps[:, 1, :], ones[:], SQ[:, 2, :], start=True, stop=True).then_inc(sums_ready, 1)
                pe.wait_ge(kv_ready, b + 1)
                wait(pe, v_done, b)
                for t in range(QT):
                    mm = nc.tensor.transpose(v_ps[:, t * P:(t + 1) * P], KV[:, t * P:(t + 1) * P], ident[:])
                mm.then_inc(v_ready, 1)
            batch(0)
            with pe.Fori(1, BATCH) as b:
                batch(b)

        @block.scalar
        def _(act):
            act.wait_ge(has_eps, 1)
            act.wait_ge(loaded, LOADS)
            nc.scalar.activation(WH[:], w[:], ACT.Copy).then_inc(w_hi, 1)

            def batch(b):
                act.wait_ge(q_ready, b + 1)
                if layer == 0:
                    nc.scalar.activation(QH[:, 0, at(b, SEQ)], q_ps[:, 0, :], ACT.Copy, scale=HD0 ** -0.5).then_inc(q_hi, 1)
                else:
                    wait(act, sums_ready, 2 * b)
                    nc.scalar.activation(SQ[:, 0:KQ, :], q_ps[:], ACT.Square).then_inc(squared, 1)
                    act.wait_ge(k_ready, b + 1)
                    nc.scalar.activation(SQ[:, 2, :], k_ps[:, 0, :], ACT.Square).then_inc(squared, 1)
                    act.wait_ge(sums_ready, 2 * b + 2)
                    wait(act, rstd_ready, b)
                    nc.scalar.activation(dev[:, 0, :], m_ps[:, 0, :], ACT.Sqrt, bias=eps[:, 0:1]).then_inc(dev_ready, 1)
                    nc.scalar.activation(dev[:, 1, :], m_ps[:, 1, :], ACT.Sqrt, bias=eps[:, 1:2],
                                         scale=1.0 / P).then_inc(dev_ready, 1)
                    act.wait_ge(q_done, b + 1)
                    nc.scalar.activation(QH[:, :, at(b, SEQ)], CF[:], ACT.Copy).then_inc(q_hi, 1)
                act.wait_ge(kv_ready, b + 1)
                nc.scalar.activation(KE[0:LAT, only(b), :], KV[0:LAT, :], ACT.Copy)
                nc.scalar.activation(KO[LAT:P, only(b), :], KV[LAT:P, :], ACT.Copy).then_inc(k_done, 1)
                act.wait_ge(v_ready, b + 1)
                nc.scalar.activation(V[:, at(b, QT), :], v_ps[:].rearrange("p (t n) -> p t n", t=QT)[:, :, 0:LAT], ACT.Copy).then_inc(v_done, 1)
            batch(0)
            with act.Fori(1, BATCH) as b:
                batch(b)

        @block.vector
        def _(dve):
            nc.vector.memset(eps[:, 0:1], Q_RANK1 * RMS_EPS)
            nc.vector.memset(eps[:, 1:2], RMS_EPS).then_inc(has_eps, 1)
            dve.wait_ge(loaded, LOADS)
            dve.wait_ge(w_hi, 1)
            nc.vector.tensor_tensor(WL[:], w[:], plain(WH[:]), ALU.subtract).then_inc(w_lo, 1)

            def batch(b):
                wait(dve, v_ready, b)
                wait(dve, k_done, b)
                if layer == 0:
                    dve.wait_ge(q_hi, b + 1)
                    nc.vector.scalar_tensor_tensor(out=QL[:, 0, at(b, SEQ)], in0=q_ps[:, 0, :], scalar=HD0 ** -0.5,
                                                   in1=plain(QH[:, 0, at(b, SEQ)]), op0=ALU.mult, op1=ALU.subtract).then_inc(q_done, 1)
                    dve.wait_ge(k_ready, b + 1)
                    nc.vector.tensor_copy(KV[:], k_ps[:, 0, :]).then_inc(kv_ready, 1)
                else:
                    dve.wait_ge(dev_ready, 2 * b + 2)
                    nc.vector.reciprocal(rstd[:], dev[:]).then_inc(rstd_ready, 1)
                    dve.wait_ge(rstd_ready, b + 1)
                    wait(dve, q_lo, b)
                    for c in range(KQ):
                        ins = nc.vector.scalar_tensor_tensor(out=CF[:, c, :], in0=q_ps[:, c, :], scalar=normw[:, c:c + 1],
                                                             in1=rstd[:, 0, :], op0=ALU.mult, op1=ALU.mult)
                    ins.then_inc(q_done, 1)
                    nc.vector.scalar_tensor_tensor(out=KV[:], in0=k_ps[:, 0, :], scalar=normw[:, KQ:KQ + 1],
                                                   in1=rstd[:, 1, :], op0=ALU.mult, op1=ALU.mult).then_inc(kv_ready, 1)
                    wait(dve, rope_done, 2 * b)
                    nc.vector.tensor_tensor(RM[:], k_ps[:, 1, :], st["cos"][:], ALU.mult).then_inc(roped, 1)
                    nc.vector.stream_shuffle(RS[:], k_ps[:, 1, :], SWAP).then_inc(roped, 1)
                    dve.wait_ge(q_hi, b + 1)
                    nc.vector.tensor_tensor(QL[:, :, at(b, SEQ)], CF[:], plain(QH[:, :, at(b, SEQ)]), ALU.subtract).then_inc(q_lo, 1)
            batch(0)
            with dve.Fori(1, BATCH) as b:
                batch(b)

        if layer == 1:
            @block.gpsimd
            def _(pool):
                pool.wait_ge(loaded, LOADS)
                turned = sem("turned")

                def batch(b):
                    pool.wait_ge(roped, 2 * b + 2)
                    wait(pool, rope_done, 2 * b)
                    nc.gpsimd.tensor_tensor(RS[:], RS[:], st["sin"][:], ALU.mult).then_inc(turned, 1)
                    pool.wait_ge(turned, b + 1)
                    nc.gpsimd.tensor_tensor(KE[LAT:P, only(b), :], RM[LAT:P, :], RS[LAT:P, :], ALU.add).then_inc(rope_done, 1)
                    nc.gpsimd.tensor_tensor(KO[0:LAT, only(b), :], RM[0:LAT, :], RS[0:LAT, :], ALU.add).then_inc(rope_done, 1)
                batch(0)
                with pool.Fori(1, BATCH) as b:
                    batch(b)


def heads(nc, a, layer, XH, XL, ident, ident_b, mask_b, st):
    n = f"hd{layer}"
    KQ = layer + 1
    stage = (STAGE0, STAGE1)[layer]
    FOLD, PLAIN = ("qn", "kn", "v", "o"), ("rope", "key") if layer == 0 else ("rope",)
    offset, width = {}, {}
    for group in (FOLD, PLAIN):
        at_ = 0
        for key in group:
            offset[key], at_ = at_, at_ + stage[key]
        width[group] = at_
    STEPS = 2 * BATCH
    KINDS = ("rope", "key") if layer == 0 else ("rope",)
    NK = len(KINDS)
    KE, KO, QH, QL, V, OL, WVO = (st[x] for x in ("KE", "KO", "QH", "QL", "V", "OL", "WVO"))
    with ExitStack() as k:
        def sem(x):
            return k.enter_context(nc.semaphore(f"{n}_{x}"))

        def sb(x, shape, dt=F32):
            return k.enter_context(nc.sbuf_tensor(f"{n}_{x}", shape, dt))

        def ps(x, shape):
            return k.enter_context(nc.psum_tensor(f"{n}_{x}", shape, F32))
        SF, SP_ = sb("stage_fold", [P, width[FOLD]]), sb("stage_plain", [P, width[PLAIN]])
        SH, SL = sb("plain_hi", [P, width[PLAIN]], F32R), sb("plain_lo", [P, width[PLAIN]], F32R)
        WNH, WNL = sb("w_latent_hi", [P, KQ, P], F32R), sb("w_latent_lo", [P, KQ, P], F32R)
        QE, QO = sb("QE", [P, 2, SEQ]), sb("QO", [P, 2, SEQ])
        RM, RS = sb("RM", [P, 2, SEQ]), sb("RS", [P, 2, SEQ])
        PR = sb("probs", [P, 2, QT * (QT + 1) // 2, P])
        PT = sb("probsT", [P, 2, QT, SEQ])
        NM, SM, RC = sb("negmax", [P, 2, QT]), sb("sums", [P, 2, QT]), sb("inv_sums", [P, 2, QT])
        s_ps = [ps(f"s_ps{i}", [P, SEQ]) for i in range(3)]
        t_ps = [ps(f"t_ps{i}", [P, SEQ]) for i in range(2)]
        o_ps = ps("o_ps", [P, SEQ])
        pj_ps = [ps(f"pj_ps{i}", [P, SEQ]) for i in range(2)]
        fold_staged, plain_staged, wabs_hi, plain_hi, plain_lo = map(
            sem, "fold_staged plain_staged wabs_hi plain_hi_done plain_lo_done".split())
        (wabs_ready, wvo_ready, wabs_copied, wvo_copied, qn_ready, qn_copied, rp_ready, rp_read, rp_mult,
         rp_done, s_ready, max_done, exp_done, inv_done, norm_done, t_ready, t_copied, o_ready, o_copied) = map(sem, (
             "wabs_ready wvo_ready wabs_copied wvo_copied qn_ready qn_copied rp_ready rp_read rp_mult "
             "rp_done s_ready max_done exp_done inv_done norm_done t_ready t_copied o_ready o_copied").split())

        def part(key, parts=1, of=None):
            v = (SF if of is None else of)[:, offset[key]:offset[key] + stage[key]]
            return v.rearrange("p (k n) -> p k n", k=parts) if parts > 1 else v
        tri = lambda i: i * (i + 1) // 2

        score_bank, score_col = (0, 0, 1, 2), (0, P, 0, 0)

        def score(i):
            return s_ps[score_bank[i]][:, score_col[i]:score_col[i] + (i + 1) * P]

        def drive(eng, prologue, body, epilogue):
            prologue()
            body(0, True, False)
            with eng.Fori(1, PAIRS - 1) as p:
                body(p, False, False)
            body(PAIRS - 1, False, True)
            epilogue()

        def back(p, g, lag):
            return (p, g - lag) if g >= lag else (p - 1, g - lag + STEPS)

        def next_batch(p, g):
            return (p, g // 2 + 1) if g < STEPS - 2 else (p + 1, 0)
        block = k.enter_context(nc.Block())

        @block.sync
        def _(sp):
            for p in range(PAIRS):
                wait(sp, wvo_ready, p)
                sp.dma_start(SF[:], a[f"fold{layer}"][p]).then_inc(fold_staged, 16)
                wait(sp, plain_lo, p)
                sp.dma_start(SP_[:], a[f"plain{layer}"][p]).then_inc(plain_staged, 16)

        @block.tensor
        def _(pe):
            def weights(p):
                pe.wait_ge(fold_staged, 16 * (p + 1))
                wait(pe, qn_copied, BATCH * p)
                wait(pe, rp_read, 2 * NK * BATCH * p)
                if layer == 0:
                    mm = nc.tensor.matmul(pj_ps[0][:, 0:P], part("qn"), part("kn"), start=True, stop=True)
                else:
                    qn, kn = part("qn", 2 * KQ), part("kn", 2)
                    for c in range(KQ):
                        for e in range(2):
                            mm = nc.tensor.matmul(pj_ps[0][:, c * P + e * LAT:c * P + (e + 1) * LAT], qn[:, KQ * e + c, :],
                                                  kn[:, e, :], start=True, stop=True)
                mm.then_inc(wabs_ready, 1)
                v, o = part("v", 2), part("o", 2)
                for e in range(2):
                    mm = nc.tensor.matmul(pj_ps[1][e * LAT:(e + 1) * LAT, 0:D], v[:, e, :], o[:, e, :], start=True, stop=True)
                mm.then_inc(wvo_ready, 1)

            def queries(p, b):
                m = BATCH * p + b
                if b == 0:
                    pe.wait_ge(wabs_copied, p + 1)
                wait(pe, rp_read, 2 * NK * m)
                wait(pe, qn_copied, m)
                sl = slice(b * SEQ, (b + 1) * SEQ)
                for c in range(KQ):
                    mm = matmul3(nc, pj_ps[0][:], WNH[:, c, :], WNL[:, c, :], QH[:, c, sl], QL[:, c, sl], c == 0, c == KQ - 1)
                mm.then_inc(qn_ready, 1)
                if b == 0:
                    pe.wait_ge(wvo_copied, p + 1)
                    pe.wait_ge(plain_lo, p + 1)
                for c in range(KQ):
                    o = offset["rope"] + c * P
                    mm = matmul3(nc, pj_ps[1][:], SH[:, o:o + P], SL[:, o:o + P], QH[:, c, sl], QL[:, c, sl], c == 0, c == KQ - 1)
                mm.then_inc(rp_ready, 1)

            def keys(p, b):
                pe.wait_ge(qn_copied, BATCH * p + b + 1)
                sl = slice(b * SEQ, (b + 1) * SEQ)
                for c in range(DC):
                    o = offset["key"] + c * P
                    mm = matmul3(nc, pj_ps[0][:], SH[:, o:o + P], SL[:, o:o + P], XH[:, c, sl], XL[:, c, sl], c == 0, c == DC - 1)
                mm.then_inc(rp_ready, 1)

            def scores(p, g, i):
                b, e = g // 2, g % 2
                if i == 0 and e == 0:
                    pe.wait_ge(qn_copied, BATCH * p + b + 1)
                    pe.wait_ge(rp_done, 2 * NK * (BATCH * p + b + 1))
                if i != 1:
                    wait(pe, exp_done, QT * (STEPS * p + g - 1) + (2, 2, 3, 4)[i])
                q, kk = (QO, KO) if e else (QE, KE)
                s = score(i)
                nc.tensor.matmul(s, q[:, b % 2, i * P:(i + 1) * P], kk[:, b, 0:(i + 1) * P], start=True, stop=False)
                nc.tensor.matmul(s[:, i * P:(i + 1) * P], ident_b[:], mask_b[:], start=False, stop=True).then_inc(s_ready, 1)

            def turn(p, g, i):
                h = STEPS * p + g
                pe.wait_ge(norm_done, QT * h + i + 1)
                wait(pe, t_copied, QT * h + i - 1)
                for j in range(i + 1):
                    mm = nc.tensor.transpose(t_ps[i % 2][:, j * P:(j + 1) * P], PR[:, g % 2, tri(i) + j, :], ident[:])
                mm.then_inc(t_ready, 1)

            def values(p, b):
                m = BATCH * p + b
                pe.wait_ge(t_copied, 2 * QT * (m + 1))
                wait(pe, o_copied, m)
                for j in range(QT):
                    for e in range(2):
                        mm = nc.tensor.matmul(o_ps[e * LAT:(e + 1) * LAT, j * P:SEQ], V[:, b * QT + j, :],
                                              PT[:, e, j, j * P:SEQ], start=j == 0, stop=j == QT - 1)
                mm.then_inc(o_ready, 1)

            def body(p, first, last):
                for g in range(STEPS):
                    before = not (first and g < 1)
                    ahead = g % 2 == 0 and not (last and g == STEPS - 2)
                    for i in range(3):
                        scores(p, g, i)
                    if ahead:
                        queries(*next_batch(p, g))
                    if g % 2 == 1 and not (first and g < 2):
                        values(*((p, g // 2 - 1) if g >= 2 else (p - 1, BATCH - 1)))
                    if before:
                        turn(*back(p, g, 1), 0)
                        turn(*back(p, g, 1), 1)
                    if ahead and layer == 0:
                        keys(*next_batch(p, g))
                    scores(p, g, 3)
                    if before:
                        turn(*back(p, g, 1), 2)
                        turn(*back(p, g, 1), 3)
                    if g == 5 and not last:
                        weights(p + 1)

            def prologue():
                weights(0)
                queries(0, 0)
                if layer == 0:
                    keys(0, 0)

            def epilogue():
                for i in range(QT):
                    turn(PAIRS - 1, STEPS - 1, i)
                values(PAIRS - 1, BATCH - 1)
            drive(pe, prologue, body, epilogue)

        @block.scalar
        def _(act):
            def weights(p):
                act.wait_ge(wabs_ready, p + 1)
                nc.scalar.activation(WNH[:], pj_ps[0][:, 0:KQ * P].rearrange("p (c n) -> p c n", c=KQ), ACT.Copy).then_inc(wabs_hi, 1)
                act.wait_ge(plain_staged, 16 * (p + 1))
                wait(act, rp_ready, NK * BATCH * p)
                nc.scalar.activation(SH[:], SP_[:], ACT.Copy).then_inc(plain_hi, 1)

            def queries(p, b):
                act.wait_ge(qn_ready, BATCH * p + b + 1)
                nc.scalar.activation(QE[0:LAT, b % 2, :], pj_ps[0][0:LAT, :], ACT.Copy)
                nc.scalar.activation(QO[LAT:P, b % 2, :], pj_ps[0][LAT:P, :], ACT.Copy).then_inc(qn_copied, 1)

            def exps(p, g, i):
                h = STEPS * p + g
                act.wait_ge(max_done, QT * h + max(i, 1) + 1)
                wait(act, t_ready, QT * (h - 1))
                nc.scalar.activation(PR[:, g % 2, tri(i):tri(i + 1), :], score(i)
                                     .rearrange("p (j n) -> p j n", j=i + 1), ACT.Exp,
                                     bias=NM[:, g % 2, i:i + 1], accum_out=SM[:, g % 2, i:i + 1]).then_inc(exp_done, 1)

            def copy_turned(p, g, i):
                h = STEPS * p + g
                act.wait_ge(t_ready, QT * h + i + 1)
                wait(act, o_ready, BATCH * p + g // 2)
                nc.scalar.activation(PT[:, g % 2, 0:i + 1, i * P:(i + 1) * P],
                                     t_ps[i % 2][:, 0:(i + 1) * P].rearrange("p (j n) -> p j n", j=i + 1), ACT.Copy).then_inc(t_copied, 1)

            def body(p, first, last):
                for g in range(STEPS):
                    before = not (first and g < 1)
                    exps(p, g, 0)
                    exps(p, g, 1)
                    if g % 2 == 0 and not (last and g == STEPS - 2):
                        queries(*next_batch(p, g))
                    exps(p, g, 2)
                    if before:
                        for i in range(QT):
                            copy_turned(*back(p, g, 1), i)
                    exps(p, g, 3)
                    if g == 5 and not last:
                        weights(p + 1)

            def prologue():
                weights(0)
                queries(0, 0)

            def epilogue():
                for i in range(QT):
                    copy_turned(PAIRS - 1, STEPS - 1, i)
            drive(act, prologue, body, epilogue)

        @block.vector
        def _(dve):
            def weights(p):
                dve.wait_ge(wvo_ready, p + 1)
                dst = WVO[:, p, :] if isinstance(p, int) else WVO[:, bass.ds(p, 1), :]
                nc.vector.tensor_copy(dst, pj_ps[1][:, 0:D]).then_inc(wvo_copied, 1)
                dve.wait_ge(wabs_hi, p + 1)
                nc.vector.tensor_tensor(WNL[:], pj_ps[0][:, 0:KQ * P].rearrange("p (c n) -> p c n", c=KQ), plain(WNH[:]),
                                        ALU.subtract).then_inc(wabs_copied, 1)
                dve.wait_ge(plain_hi, p + 1)
                nc.vector.tensor_tensor(SL[:], SP_[:], plain(SH[:]), ALU.subtract).then_inc(plain_lo, 1)

            def queries(p, b):
                m = BATCH * p + b
                for n_, kind in enumerate(KINDS):
                    r = NK * m + n_
                    buf = n_ if layer == 0 else b % 2
                    src = pj_ps[1 - n_]
                    dve.wait_ge(rp_ready, r + 1)
                    wait(dve, rp_done, 2 * (r - 1))
                    nc.vector.tensor_tensor(RM[:, buf, :], src[:], st["cos"][:], ALU.mult).then_inc(rp_read, 1)
                    nc.vector.stream_shuffle(RS[:, buf, :], src[:], SWAP).then_inc(rp_read, 1)

            def maxes(p, g, i):
                h = STEPS * p + g
                dve.wait_ge(s_ready, QT * h + max(i, 1) + 1)
                wait(dve, exp_done, QT * (h - 1))
                nc.vector.tensor_reduce(NM[:, g % 2, i:i + 1], score(i), AX.X,
                                        ALU.max, negate=True).then_inc(max_done, 1)

            def normalise(p, g):
                h = STEPS * p + g
                dve.wait_ge(exp_done, QT * (h + 1))
                nc.vector.reciprocal(RC[:, g % 2, :], SM[:, g % 2, :]).then_inc(inv_done, 1)
                dve.wait_ge(inv_done, h + 1)
                for i in range(QT):
                    sl = PR[:, g % 2, tri(i):tri(i + 1), :]
                    nc.vector.tensor_scalar(sl, sl, RC[:, g % 2, i:i + 1], None, ALU.mult).then_inc(norm_done, 1)

            def copy_out(p, b):
                dve.wait_ge(o_ready, BATCH * p + b + 1)
                nc.vector.tensor_copy(OL[:, only(p), b * SEQ:(b + 1) * SEQ], o_ps[:]).then_inc(o_copied, 1)

            def body(p, first, last):
                for g in range(STEPS):
                    for i in range(3):
                        maxes(p, g, i)
                    if not (first and g < 1):
                        normalise(*back(p, g, 1))
                    if g % 2 == 0 and not (last and g == STEPS - 2):
                        queries(*next_batch(p, g))
                    maxes(p, g, 3)
                    if g % 2 == 1 and not (first and g < 2):
                        copy_out(*((p, g // 2 - 1) if g >= 2 else (p - 1, BATCH - 1)))
                    if g == 5 and not last:
                        weights(p + 1)

            def prologue():
                weights(0)
                queries(0, 0)

            def epilogue():
                normalise(PAIRS - 1, STEPS - 1)
                copy_out(PAIRS - 1, BATCH - 1)
            drive(dve, prologue, body, epilogue)

        @block.gpsimd
        def _(pool):
            def queries(p, b):
                m = BATCH * p + b
                for n_, kind in enumerate(KINDS):
                    r = NK * m + n_
                    buf = n_ if layer == 0 else b % 2
                    pool.wait_ge(rp_read, 2 * (r + 1))
                    wait(pool, rp_done, 2 * r)
                    nc.gpsimd.tensor_tensor(RS[:, buf, :], RS[:, buf, :], st["sin"][:], ALU.mult).then_inc(rp_mult, 1)
                    pool.wait_ge(rp_mult, r + 1)
                    for rows, q, kk in ((slice(LAT, P), QE, KE), (slice(0, LAT), QO, KO)):
                        dst = q[rows, b % 2, :] if kind == "rope" else kk[rows, b, :]
                        nc.gpsimd.tensor_tensor(dst, RM[rows, buf, :], RS[rows, buf, :], ALU.add).then_inc(rp_done, 1)
            for b in range(BATCH):
                queries(0, b)
            with pool.Fori(1, PAIRS) as p:
                for b in range(BATCH):
                    queries(p, b)


def project(nc, layer, st, x_src, gate, x_dst):
    n = f"pr{layer}"
    OL, WVO = st["OL"], st["WVO"]
    with ExitStack() as k:
        def sem(x):
            return k.enter_context(nc.semaphore(f"{n}_{x}"))

        def sb(x, shape, dt=F32):
            return k.enter_context(nc.sbuf_tensor(f"{n}_{x}", shape, dt))
        X, G = sb("x", [P, DC, SEQ]), sb("g", [P, DC, SEQ])
        WH, WL = sb("WH", [P, PAIRS, D], F32R), sb("WL", [P, PAIRS, D], F32R)
        OH, OLo = sb("OH", [P, PAIRS, SEQ], F32R), sb("OL", [P, PAIRS, SEQ], F32R)
        o_ps = k.enter_context(nc.psum_tensor(f"{n}_o_ps", [P, DC, SEQ], F32))
        x_loaded, g_loaded, w_hi, w_lo, o_hi, o_lo, used, o_ready, gated, added, stored = map(
            sem, "x_loaded g_loaded w_hi w_lo o_hi o_lo used o_ready gated added stored".split())
        block = k.enter_context(nc.Block())

        @block.sync
        def _(sp):
            def batch(b):
                wait(sp, added, b)
                sp.dma_start(X[:], x_src[:, :, at(b, SEQ)]).then_inc(x_loaded, 16)
                wait(sp, stored, 16 * b)
                sp.dma_start(G[:], gate[:, :, at(b, SEQ)]).then_inc(g_loaded, 16)
            batch(0)
            with sp.Fori(1, BATCH) as b:
                batch(b)
            sp.wait_ge(stored, 16 * BATCH)

        @block.tensor
        def _(pe):
            pe.wait_ge(w_lo, 1)

            def batch(b):
                wait(pe, gated, b)
                for p in range(PAIRS):
                    pe.wait_ge(o_lo, PAIRS * b + p + 1)
                    for m in range(DC):
                        cols = slice(m * P, (m + 1) * P)
                        mm = matmul3(nc, o_ps[:, m, :], WH[:, p, cols], WL[:, p, cols], OH[:, p, :], OLo[:, p, :],
                                     p == 0, p == PAIRS - 1)
                    mm.then_inc(used, 1)
            batch(0)
            with pe.Fori(1, BATCH) as b:
                batch(b)

        @block.scalar
        def _(act):
            nc.scalar.activation(WH[:], WVO[:], ACT.Copy).then_inc(w_hi, 1)

            def batch(b):
                for p in range(PAIRS):
                    wait(act, used, PAIRS * (b - 1) + p + 1)
                    nc.scalar.activation(OH[:, p, :], OL[:, p, at(b, SEQ)], ACT.Copy).then_inc(o_hi, 1)
            batch(0)
            with act.Fori(1, BATCH) as b:
                batch(b)

        @block.gpsimd
        def _(pool):
            with pool.Fori(0, BATCH) as b:
                pool.wait_ge(added, b + 1)
                pool.dma_start(x_dst[:, :, at(b, SEQ)], G[:]).then_inc(stored, 16)
            pool.wait_ge(stored, 16 * BATCH)

        @block.vector
        def _(dve):
            dve.wait_ge(w_hi, 1)
            nc.vector.tensor_tensor(WL[:], WVO[:], plain(WH[:]), ALU.subtract).then_inc(w_lo, 1)

            def split(b):
                for p in range(PAIRS):
                    dve.wait_ge(o_hi, PAIRS * b + p + 1)
                    nc.vector.tensor_tensor(OLo[:, p, :], OL[:, p, at(b, SEQ)], plain(OH[:, p, :]), ALU.subtract).then_inc(o_lo, 1)

            def combine(b):
                dve.wait_ge(g_loaded, 16 * (b + 1))
                dve.wait_ge(used, PAIRS * (b + 1))
                nc.vector.tensor_tensor(G[:], G[:], o_ps[:], ALU.mult).then_inc(gated, 1)
                dve.wait_ge(x_loaded, 16 * (b + 1))
                dve.wait_ge(gated, b + 1)
                nc.vector.tensor_tensor(G[:], G[:], X[:], ALU.add).then_inc(added, 1)
            split(0)
            combine(0)
            with dve.Fori(1, BATCH) as b:
                split(b)
                combine(b)


def rope_tables(inv_freq):
    angle = np.arange(SEQ, dtype=np.float32)[:, None] * inv_freq.astype(np.float32)[None, :]
    row = (np.arange(P) % ROPE) // 2
    sign = np.where(np.arange(P) % 2 == 0, -1.0, 1.0).astype(np.float32)[:, None]
    cos, sin = np.cos(angle).astype(np.float32).T[row], np.sin(angle).astype(np.float32).T[row] * sign
    return np.ascontiguousarray(cos), np.ascontiguousarray(sin)


def chunks(w):
    return np.ascontiguousarray(w.reshape(-1, P, w.shape[1]).transpose(1, 0, 2))


def pad_rows(w, n):
    return np.concatenate([w, np.zeros((n - w.shape[0],) + w.shape[1:], w.dtype)], 0)


def layouts(d):
    f = {}
    half = ROPE // 2
    f["xT"] = np.ascontiguousarray(d["L0_attn_x"].reshape(T, D).T)
    inv0 = (1.0 / 10000.0 ** (np.arange(half, dtype=np.float32) / np.float32(half))).astype(np.float32)
    inv1 = (1.0 / 500000.0 ** (np.arange(0, ROPE, 2, dtype=np.float32) / np.float32(ROPE))).astype(np.float32)
    f["cos0"], f["sin0"] = rope_tables(inv0)
    f["cos1"], f["sin1"] = rope_tables(inv1)
    stack = lambda r, s: np.concatenate([d[r], d[s][None]], 0)
    wide = lambda w: np.ascontiguousarray(w.reshape(EXPERTS, DC, P, D).transpose(0, 2, 1, 3))
    f["w_up"], f["w_gate"], f["w_down"] = (wide(stack(r, s)) for r, s in (
        ("L0_ffn_Wup", "L0_ffn_Wsu"), ("L0_ffn_Wgate", "L0_ffn_Wsg"), ("L0_ffn_Wdown", "L0_ffn_Wsd")))
    col = lambda v: np.ascontiguousarray(v.reshape(EXPERTS, DC, P).transpose(0, 2, 1))
    f["b_up"], f["b_gate"] = col(stack("L0_ffn_bup", "L0_ffn_bsu")), col(stack("L0_ffn_bgate", "L0_ffn_bsg"))
    f["b_down"] = stack("L0_ffn_bdown", "L0_ffn_bsd")
    wr = np.zeros((D, EXPERTS), np.float32)
    wr[:, :ROUTED] = d["L0_ffn_Wr"]
    f["w_route"] = chunks(wr)
    f["b_route"], f["b_select"] = d["L0_ffn_br"][None], d["L0_ffn_gate_bias"][None]
    f["lane"] = np.arange(EXPERTS, 0, -1, dtype=np.float32)[None]
    def padded(i, rows, cols):
        o = np.full((rows, cols), LUT, np.int32)
        o[:i.shape[0], :i.shape[1]] = i
        return chunks(o).reshape(P, -1)
    f["index"] = np.concatenate([padded(d["L1_ffn_gate_idx"].T, D, INTER_PAD), padded(d["L1_ffn_up_idx"].T, D, INTER_PAD),
                                 padded(d["L1_ffn_down_idx"].T, INTER_PAD, D)], 1)
    f["lut"] = d["L1_ffn_lut"][None]
    mix = np.arange(ROPE).reshape(2, half).T.ravel()
    f["wq_down0"] = chunks(d["L0_attn_Wq_down"])
    f["wkv_down0"] = chunks(np.tile(d["L0_attn_Wkv_down"], (1, 2)))
    qn = d["L0_attn_Wq_up"].reshape(QR0, PAIRS, 2 * ND0).transpose(1, 2, 0)
    ku = d["L0_attn_Wk_up"].reshape(LAT, PAIRS, 2, ND0).transpose(1, 2, 3, 0)
    kn = np.zeros((PAIRS, 2, ND0, 2, LAT), np.float32)
    for e in range(2):
        kn[:, e, :, e] = ku[:, e]
    odd_first = lambda w: w.reshape(w.shape[0], PAIRS, 2, ROPE)[:, :, ::-1][..., mix].transpose(1, 0, 2, 3).reshape(PAIRS, w.shape[0], P)
    rope = odd_first(d["L0_attn_Wq_rope"])
    key = odd_first(d["L0_attn_Wk_rope"]).reshape(PAIRS, DC, P, P).transpose(0, 2, 1, 3)
    v = d["L0_attn_Wv_up"].reshape(LAT, PAIRS, 2, HD0).transpose(1, 3, 2, 0)
    o = d["L0_attn_Wo"].reshape(PAIRS, 2, HD0, D).transpose(0, 2, 1, 3)
    join = lambda *w: np.ascontiguousarray(np.concatenate([x.reshape(PAIRS, P, -1) for x in w], 2))
    f["fold0"], f["plain0"] = join(qn, kn.reshape(PAIRS, P, P), v, o), join(rope, key)
    f["wq_down1"] = chunks(pad_rows(d["L1_attn_w_q_down"], 2 * P).T)
    wkv = d["L1_attn_w_kv_down"]
    f["wkv_down1"] = chunks(np.concatenate([wkv[:LAT], wkv[:LAT], wkv[LAT:], wkv[LAT:]], 0).T)
    f["norm_w1"] = np.ascontiguousarray(np.concatenate([pad_rows(d["L1_attn_q_norm_w"], 2 * P),
                                                        d["L1_attn_kv_norm_w"], d["L1_attn_kv_norm_w"]]).reshape(3, P).T)
    wq = d["L1_attn_w_q_up"].reshape(PAIRS, 2, QK1, Q_RANK1)
    qr = np.zeros((PAIRS, 2, QK1, 2 * P), np.float32)
    qr[..., :Q_RANK1] = wq
    qn = qr[:, :, :NOPE1].transpose(0, 2, 1, 3)
    rope = qr[:, ::-1, NOPE1:].reshape(PAIRS, P, 2, P).transpose(0, 3, 2, 1)
    kvu = d["L1_attn_w_kv_up"].reshape(PAIRS, 2, NOPE1 + VD1, LAT)
    kn, v = kvu[:, :, :NOPE1].transpose(0, 2, 1, 3), kvu[:, :, NOPE1:].transpose(0, 2, 1, 3)
    o = d["L1_attn_w_o"].T.reshape(PAIRS, 2, VD1, D).transpose(0, 2, 1, 3)
    f["fold1"], f["plain1"] = join(qn, kn, v, o), join(rope)
    return f


def kernel(**inputs):
    import concourse.bacc as bacc
    from concourse.bass_utils import run_bass_kernel_spmd

    laid = layouts({name: np.asarray(v) for name, v in inputs.items()})
    nc = bacc.Bacc("TRN2", target_bir_lowering=False, num_devices=1)
    arrays, args = {}, {}
    for name, v in laid.items():
        v = np.ascontiguousarray(v)
        arrays[f"in_{name}"] = v
        args[name] = nc.dram_tensor(f"in_{name}", v.shape, mybir.dt.from_np(v.dtype), kind="ExternalInput").ap()
    out = nc.dram_tensor("outT", [D, T], F32, kind="ExternalOutput").ap()
    build(nc, args, out)
    r = run_bass_kernel_spmd(nc, [arrays], core_ids=[0])
    return np.ascontiguousarray(r.results[0]["outT"].T).reshape(BATCH, SEQ, D)
```

```python
from contextlib import ExitStack

import numpy as np

import concourse.bass as bass
from concourse import mybir

F32 = mybir.dt.float32
F32R = mybir.dt.float32r
BF16 = mybir.dt.bfloat16
I32 = mybir.dt.int32
ALU = mybir.AluOpType
ACT = mybir.ActivationFunctionType
AX = mybir.AxisListType

P = 128
D = 256
DC = D // P
BATCH, SEQ = 4, 512
T = BATCH * SEQ
QT = SEQ // P
HEADS = 16
PAIRS = HEADS // 2
LAT = 64
ROPE = 64
ND0, QR0, HD0 = 64, 128, 128
Q_RANK1, QK1, NOPE1, VD1 = 192, 192, 128, 128
EXPERTS = 8
ROUTED = 7
INTER, INTER_PAD = 688, 768
IT = INTER_PAD // P
LUT = 16
NEG = -1e30
BIG = 3e38
LN_EPS, RMS_EPS = 1e-5, 1e-6
SWAP = [i ^ 1 for i in range(32)]

STAGE0 = {"qn": 128, "kn": 128, "rope": 128, "key": 256, "v": 128, "o": 512}
STAGE1 = {"qn": 512, "kn": 128, "rope": 256, "v": 128, "o": 512}
LUT_COLS = 2 * 2 * INTER_PAD + IT * D
LUT_CHUNK = LUT_COLS // EXPERTS
HITS = 4


def at(i, n):
    return bass.ds(i * n, n)


def only(i):
    return i if isinstance(i, int) else bass.ds(i, 1)


def plain(ap):
    return ap.bitcast(F32)


def matmul3(nc, out, w_hi, w_lo, x_hi, x_lo, first, last):
    nc.tensor.matmul(out, w_hi, x_hi, start=first, stop=False)
    nc.tensor.matmul(out, w_hi, x_lo, start=False, stop=False)
    return nc.tensor.matmul(out, w_lo, x_hi, start=False, stop=last)


def wait(eng, sem, value):
    if isinstance(value, int) and value <= 0:
        return
    eng.wait_ge(sem, value)


def build(nc, a, out):
    with ExitStack() as top:
        def keep(name, shape, dt=F32):
            return top.enter_context(nc.sbuf_tensor(name, shape, dt))

        XH, XL = keep("normed_hi", [P, DC, T], F32R), keep("normed_lo", [P, DC, T], F32R)
        shared = keep("shared", [P, PAIRS * T])
        ident = keep("identity", [P, P])
        ident_b = keep("identity_bf16", [P, P], BF16)
        mask_b = keep("causal_mask_bf16", [P, P], BF16)
        ones = keep("ones", [P, P])
        x1_dram = nc.dram_tensor("x_after_layer0", [D, T], F32, kind="Internal").ap()
        gate_dram = nc.dram_tensor("gate", [D, T], F32, kind="Internal").ap()
        prob_dram = nc.dram_tensor("probs", [EXPERTS, T], F32, kind="Internal").ap()
        lut_dram = nc.dram_tensor("lut_weights", [P, LUT_COLS], F32, kind="Internal").ap()
        chunked = lambda t: t.rearrange("(c p) t -> p c t", p=P)
        xT, x1, gate = chunked(a["xT"]), chunked(x1_dram), chunked(gate_dram)

        constants(nc, a, ident, ident_b, mask_b, ones)
        mixture(nc, a, shared, XH, XL, ident, ones, xT, lut_dram, prob_dram, gate)
        attention(nc, a, 0, shared, XH, XL, ident, ident_b, mask_b, ones, xT, gate, x1)
        lut_ffn(nc, shared, XH, XL, ones, x1, lut_dram, gate)
        attention(nc, a, 1, shared, XH, XL, ident, ident_b, mask_b, ones, x1, gate, chunked(out))


def constants(nc, a, ident, ident_b, mask_b, ones):
    with ExitStack() as k:
        zeroed, made = k.enter_context(nc.semaphore("const_zeroed")), k.enter_context(nc.semaphore("const_made"))
        block = k.enter_context(nc.Block())

        @block.gpsimd
        def _(pool):
            nc.gpsimd.memset(ident[:], 0.0).then_inc(zeroed, 1)
            nc.gpsimd.memset(mask_b[:], 0.0).then_inc(zeroed, 1)
            nc.gpsimd.memset(ones[:], 1.0).then_inc(zeroed, 1)
            pool.wait_ge(zeroed, 3)
            nc.gpsimd.affine_select(out=ident[:], in_=ident[:], compare_op=ALU.not_equal, fill=1.0, base=0,
                                    pattern=[[-1, P]], channel_multiplier=1).then_inc(made, 1)
            nc.gpsimd.affine_select(out=mask_b[:], in_=mask_b[:], compare_op=ALU.is_ge, fill=NEG, base=0,
                                    pattern=[[-1, P]], channel_multiplier=1).then_inc(made, 1)

        @block.vector
        def _(dve):
            dve.wait_ge(made, 2)
            nc.vector.tensor_copy(ident_b[:], ident[:]).then_inc(made, 1)


def layernorm(nc, shared, XH, XL, ones, src, name, ahead=None):
    XN = shared[:, 0:DC * T].rearrange("p (c t) -> p c t", c=DC)
    with ExitStack() as k:
        def sem(n):
            return k.enter_context(nc.semaphore(f"{name}_{n}"))

        def sb(n, shape):
            return k.enter_context(nc.sbuf_tensor(f"{name}_{n}", shape, F32))
        squares = sb("squares", [P, 2, DC, SEQ])
        logs, rstd, eps = sb("logs", [P, 2, SEQ]), sb("rstd", [P, 2, SEQ]), sb("eps", [P, 1])
        mean_ps = k.enter_context(nc.psum_tensor(f"{name}_mean_ps", [P, 2, SEQ], F32))
        var_ps = k.enter_context(nc.psum_tensor(f"{name}_var_ps", [P, 2, SEQ], F32))
        has_eps, mean_ready, centred, squared, var_ready, logs_ready, rstd_ready, normed, split_hi, split_lo = map(
            sem, "has_eps mean_ready centred squared var_ready logs_ready rstd_ready normed split_hi split_lo".split())
        loaded = [sem(f"loaded{b}") for b in range(BATCH)]
        of = lambda t, b: t[:, :, b * SEQ:(b + 1) * SEQ]
        block = k.enter_context(nc.Block())

        @block.sync
        def _(sp):
            for b in range(BATCH):
                sp.dma_start(of(XN, b), of(src, b)).then_inc(loaded[b], 16)
            if ahead:
                ahead(sp)

        @block.tensor
        def _(pe):
            def mean(b):
                pe.wait_ge(loaded[b], 16)
                wait(pe, centred, b - 1)
                for c in range(DC):
                    mm = nc.tensor.matmul(mean_ps[:, b % 2, :], ones[:], of(XN, b)[:, c, :], start=c == 0, stop=c == DC - 1)
                mm.then_inc(mean_ready, 1)

            def variance(b):
                pe.wait_ge(squared, b + 1)
                wait(pe, logs_ready, b - 1)
                for c in range(DC):
                    mm = nc.tensor.matmul(var_ps[:, b % 2, :], ones[:], squares[:, b % 2, c, :], start=c == 0, stop=c == DC - 1)
                mm.then_inc(var_ready, 1)
            for b in range(BATCH + 1):
                if b < BATCH:
                    mean(b)
                if b >= 1:
                    variance(b - 1)

        @block.vector
        def _(dve):
            nc.vector.memset(eps[:], LN_EPS).then_inc(has_eps, 1)

            def centre(b):
                dve.wait_ge(mean_ready, b + 1)
                for c in range(DC):
                    x = of(XN, b)[:, c, :]
                    ins = nc.vector.scalar_tensor_tensor(out=x, in0=mean_ps[:, b % 2, :], scalar=-1.0 / D, in1=x,
                                                         op0=ALU.mult, op1=ALU.add)
                ins.then_inc(centred, 1)

            def normalise(b):
                dve.wait_ge(rstd_ready, b + 1)
                nc.vector.tensor_tensor(of(XN, b), of(XN, b), rstd[:, b % 2, :].unsqueeze(1).to_broadcast([P, DC, SEQ]),
                                        ALU.mult).then_inc(normed, 1)

            def low(b):
                dve.wait_ge(split_hi, b + 1)
                nc.vector.tensor_tensor(of(XL, b), of(XN, b), plain(of(XH, b)), ALU.subtract).then_inc(split_lo, 1)
            centre(0)
            centre(1)
            for b in range(BATCH):
                normalise(b)
                if b + 2 < BATCH:
                    centre(b + 2)
                if b >= 1:
                    low(b - 1)
            low(BATCH - 1)

        @block.scalar
        def _(act):
            act.wait_ge(has_eps, 1)

            def square(b):
                act.wait_ge(centred, b + 1)
                wait(act, var_ready, b - 1)
                nc.scalar.activation(squares[:, b % 2, :, :], of(XN, b), ACT.Square).then_inc(squared, 1)

            def rstds(b):
                act.wait_ge(var_ready, b + 1)
                nc.scalar.activation(logs[:, b % 2, :], var_ps[:, b % 2, :], ACT.Ln, bias=eps[:, 0:1],
                                     scale=1.0 / D).then_inc(logs_ready, 1)
                act.wait_ge(logs_ready, b + 1)
                wait(act, normed, b - 1)
                nc.scalar.activation(rstd[:, b % 2, :], logs[:, b % 2, :], ACT.Exp, scale=-0.5).then_inc(rstd_ready, 1)

            def high(b):
                act.wait_ge(normed, b + 1)
                nc.scalar.activation(of(XH, b), of(XN, b), ACT.Copy).then_inc(split_hi, 1)
            square(0)
            for b in range(BATCH):
                if b + 1 < BATCH:
                    square(b + 1)
                rstds(b)
                if b >= 1:
                    high(b - 1)
            high(BATCH - 1)


def mixture(nc, a, shared, XH, XL, ident, ones, x_src, lut_dram, prob_dram, gate):
    TT = T // P
    at_ = np.cumsum([0, DC * T, DC * T, T, 2 * DC * SEQ, DC * SEQ, DC * SEQ, DC * SEQ]).tolist()
    XN, acc, probT, U, G, SG, UP = (shared[:, x:y] for x, y in zip(at_, at_[1:]))
    XN, acc, G, SG, UP = (t.rearrange("p (c t) -> p c t", c=DC) for t in (XN, acc, G, SG, UP))
    U = U.rearrange("p (b c t) -> p b c t", b=2, c=DC)
    with ExitStack() as k:
        sems = []

        def sem(n):
            sems.append(nc.alloc_semaphore(name=f"moe_{n}"))
            return sems[-1]

        def sb(n, shape, dt=F32):
            return k.enter_context(nc.sbuf_tensor(f"moe_{n}", shape, dt))

        def ps(n, shape):
            return k.enter_context(nc.psum_tensor(f"moe_{n}", shape, F32))
        raw = {n: sb(f"raw_{n}", [P, DC, D]) for n in ("up", "gate", "down")}
        hi = {n: sb(f"hi_{n}", [P, DC, D], F32R) for n in raw}
        lo = {n: sb(f"lo_{n}", [P, DC, D], F32R) for n in raw}
        b_up, b_gate = sb("b_up", [P, DC]), sb("b_gate", [P, DC])
        b_down = sb("b_down", [P, D])
        w_route, b_route, b_select = sb("w_route", [P, DC, EXPERTS]), sb("b_route", [P, ROUTED]), sb("b_select", [P, ROUTED])
        index, table = sb("index", [P, LUT_COLS], I32), sb("table", [P, LUT])
        hit, lut_sum = sb("hit", [P, HITS, LUT_CHUNK]), sb("lut_sum", [P, LUT_CHUNK])
        prob_b = sb("prob_b", [P, BATCH, SEQ])
        UH, UL, GH, GL = (sb(n, [P, 2, DC, SEQ], F32R) for n in ("UH", "UL", "GH", "GL"))
        rt = [sb(f"route{i}", [P, TT, EXPERTS]) for i in range(6)]
        r1 = [sb(f"route_row{i}", [P, TT]) for i in range(8)]
        lane = sb("lane", [P, EXPERTS])
        (loaded, zeroed, lanes, routed, chain, expd, prob_ready, turned, turn_copied, prob_stored,
         up_loaded, gate_loaded, down_loaded, up_ready, up_copied, gate_ready, silu_done,
         scaled, glu_done, down_ready, added, lut_hit, lut_added, gated, stored) = map(sem, (
             "loaded zeroed lanes routed chain expd prob_ready turned turn_copied prob_stored "
             "up_loaded gate_loaded down_loaded up_ready up_copied gate_ready silu_done "
             "scaled glu_done down_ready added lut_hit lut_added gated stored").split())
        up_hi, up_lo, glu_hi, glu_lo, ups_biased, gates_biased = (
            sem(n) for n in "up_hi up_lo glu_hi glu_lo ups_biased gates_biased".split())
        lut_stored = sem("lut_stored")
        w_hi = {n: sem(f"w_hi_{n}") for n in raw}
        w_lo = {n: sem(f"w_lo_{n}") for n in raw}
        prob_bcast = [sem(f"prob_bcast{b}") for b in range(BATCH)]
        LOADS = 16 * 7

        def a_row(dram, e, b):
            return dram[bass.ds(e, 1), b * SEQ:(b + 1) * SEQ].to_broadcast([P, SEQ])
        arrived = {"up": up_loaded, "gate": gate_loaded, "down": down_loaded}

        def load_expert(sp, e):
            for n in raw:
                wait(sp, w_lo[n], e)
                sp.dma_start(raw[n][:], a[f"w_{n}"][e]).then_inc(arrived[n], 16)
            wait(sp, up_copied, BATCH * e)
            sp.dma_start(b_up[:], a["b_up"][e]).then_inc(ups_biased, 16)

        def ahead(sp):
            sp.dma_start(w_route[:], a["w_route"]).then_inc(loaded, 16)
            sp.dma_start(b_route[:], a["b_route"].partition_broadcast(P)).then_inc(loaded, 16)
            sp.dma_start(b_select[:], a["b_select"].partition_broadcast(P)).then_inc(loaded, 16)
            sp.dma_start(table[:], a["lut"].partition_broadcast(P)).then_inc(loaded, 16)
            sp.dma_start(lane[:], a["lane"].partition_broadcast(P)).then_inc(loaded, 16)
            sp.dma_start(b_down[:], a["b_down"]).then_inc(loaded, 16)
            load_expert(sp, 0)
            sp.dma_start(index[:], a["index"]).then_inc(loaded, 16)
        layernorm(nc, shared, XH, XL, ones, x_src, "ln0", ahead)
        up_ps, gate_ps, down_ps = (ps(n, [P, DC, SEQ]) for n in ("up_ps", "gate_ps", "down_ps"))
        route_ps = ps("route_ps", [P, TT, EXPERTS])
        turn_ps = ps("turn_ps", [EXPERTS, SEQ])
        block = k.enter_context(nc.Block())

        @block.sync
        def _(sp):
            def load(e):
                if isinstance(e, int):
                    sp.wait_ge(turn_copied, BATCH)
                    sp.dma_start(prob_dram, probT[0:EXPERTS, :]).then_inc(prob_stored, 16)
                else:
                    load_expert(sp, e)
                if isinstance(e, int):
                    sp.wait_ge(prob_stored, 16)
                for b in range(BATCH):
                    if b == 2 and not isinstance(e, int):
                        store_weights(e - 1)
                    if b == 1:
                        wait(sp, silu_done, BATCH * e)
                        sp.dma_start(b_gate[:], a["b_gate"][e]).then_inc(gates_biased, 16)
                    wait(sp, scaled, BATCH * (e - 1) + b + 1)
                    sp.dma_start(prob_b[:, b, :], a_row(prob_dram, e, b)).then_inc(prob_bcast[b], 16)

            def store_weights(chunk):
                sp.wait_ge(lut_added, (LUT - 1) * (chunk + 1))
                sp.dma_start(lut_dram[:, at(chunk, LUT_CHUNK)], lut_sum[:]).then_inc(lut_stored, 16)
            load(0)
            with sp.Fori(1, EXPERTS) as e:
                load(e)
            store_weights(EXPERTS - 1)
            for b in range(BATCH):
                sp.wait_ge(gated, b + 1)
                sp.dma_start(gate[:, :, b * SEQ:(b + 1) * SEQ], acc[:, :, b * SEQ:(b + 1) * SEQ]).then_inc(stored, 16)
            sp.wait_ge(stored, 16 * BATCH)
            sp.wait_ge(lut_stored, 16 * EXPERTS)

        @block.gpsimd
        def _(pool):
            def low(n, e):
                pool.wait_ge(w_hi[n], e + 1)
                nc.gpsimd.tensor_tensor(lo[n][:], raw[n][:], plain(hi[n][:]), ALU.subtract).then_inc(w_lo[n], 1)

            def add_hits(chunk, b):
                for v in range(max(1, b * LUT // BATCH), (b + 1) * LUT // BATCH):
                    n = chunk * (LUT - 1) + v - 1
                    pool.wait_ge(lut_hit, LUT * chunk + v + 1)
                    wait(pool, lut_added, n)
                    if v == 1:
                        wait(pool, lut_stored, 16 * chunk)
                    before = hit[:, 0, :] if v == 1 else lut_sum[:]
                    nc.gpsimd.tensor_tensor(lut_sum[:], before, hit[:, v % HITS, :], ALU.add).then_inc(lut_added, 1)

            def steps(e, last):
                for b in range(BATCH):
                    if b == 0 and not isinstance(e, int) or b == 0 and last:
                        low("gate", e)
                    if b == 1:
                        low("down", e)
                    if b == 3 and not last:
                        low("up", e + 1)
                    add_hits(e, b)
            low("up", 0)
            pool.memset(probT, 0.0).then_inc(zeroed, 1)
            pool.memset(acc, 0.0).then_inc(zeroed, 1)
            low("gate", 0)
            steps(0, False)
            with pool.Fori(1, EXPERTS - 1) as e:
                steps(e, False)
            steps(EXPERTS - 1, True)

        @block.tensor
        def _(pe):
            def route():
                for t in range(TT):
                    for c in range(DC):
                        mm = nc.tensor.matmul(route_ps[:, t, :], XN[:, c, t * P:(t + 1) * P], w_route[:, c, :],
                                              start=c == 0, stop=c == DC - 1)
                mm.then_inc(routed, 1)

            def product(out, n, e, b, x_hi, x_lo, biased=False):
                if b == 0:
                    pe.wait_ge(w_lo[n], e + 1)
                for m in range(DC):
                    for c in range(DC):
                        cols = slice(m * P, (m + 1) * P)
                        mm = matmul3(nc, out[:, m, :], hi[n][:, c, cols], lo[n][:, c, cols], x_hi[:, c, :], x_lo[:, c, :],
                                     c == 0 and not biased, c == DC - 1)
                return mm

            def up(e, b):
                wait(pe, up_copied, BATCH * e + b)
                sl = slice(b * SEQ, (b + 1) * SEQ)
                product(up_ps, "up", e, b, XH[:, :, sl], XL[:, :, sl]).then_inc(up_ready, 1)

            def gating(e, b):
                wait(pe, silu_done, BATCH * e + b)
                pe.wait_ge(up_lo, BATCH * e + b + 1)
                product(gate_ps, "gate", e, b, UH[:, b % 2], UL[:, b % 2]).then_inc(gate_ready, 1)

            def down(e, b):
                wait(pe, added, BATCH * e + b)
                pe.wait_ge(glu_lo, BATCH * e + b + 1)
                last = isinstance(e, int) and e == EXPERTS - 1
                if last:
                    for m in range(DC):
                        nc.tensor.matmul(down_ps[:, m, :], b_down[:, m * P:(m + 1) * P], probT[:, b * SEQ:(b + 1) * SEQ],
                                         start=True, stop=False)
                product(down_ps, "down", e, b, GH[:, b % 2], GL[:, b % 2], last).then_inc(down_ready, 1)

            def steps(e, first):
                for b in range(BATCH):
                    if not (first and b == 1):
                        up(e, b)
                    if first and b == 0:
                        pe.wait_ge(loaded, LOADS)
                        route()
                        gating(0, 0)
                        up(0, 1)
                    if b >= 2 or not first:
                        gating(*((e, b - 1) if b >= 1 else (e - 1, BATCH - 1)))
                    if b >= 2 or not first:
                        down(*((e, b - 2) if b >= 2 else (e - 1, b + BATCH - 2)))
                    if first and b == 0:
                        turn()

            def turn():
                pe.wait_ge(prob_ready, 1)
                for b in range(BATCH):
                    wait(pe, turn_copied, b)
                    for t in range(QT):
                        mm = nc.tensor.transpose(turn_ps[:, t * P:(t + 1) * P], rt[5][:, b * QT + t, :], ident[:])
                    mm.then_inc(turned, 1)

            steps(0, True)
            with pe.Fori(1, EXPERTS - 1) as e:
                steps(e, False)
            steps(EXPERTS - 1, False)
            gating(EXPERTS - 1, BATCH - 1)
            down(EXPERTS - 1, BATCH - 2)
            down(EXPERTS - 1, BATCH - 1)

        @block.scalar
        def _(act):
            used = {"up": up_ready, "gate": gate_ready, "down": down_ready}

            def high(n, e):
                act.wait_ge(arrived[n], 16 * (e + 1))
                wait(act, used[n], BATCH * e)
                nc.scalar.activation(hi[n][:], raw[n][:], ACT.Copy).then_inc(w_hi[n], 1)

            def copy_up(e, b):
                t = BATCH * e + b
                if b == 0:
                    act.wait_ge(ups_biased, 16 * (e + 1))
                act.wait_ge(up_ready, t + 1)
                wait(act, scaled, t - 1)
                for m in range(DC):
                    ins = nc.scalar.activation(U[:, b % 2, m, :], up_ps[:, m, :], ACT.Identity, bias=b_up[:, m:m + 1])
                ins.then_inc(up_copied, 1)
                act.wait_ge(up_copied, t + 1)
                wait(act, gate_ready, t - 1)
                nc.scalar.activation(UH[:, b % 2], U[:, b % 2], ACT.Copy).then_inc(up_hi, 1)

            def silu(e, b):
                t = BATCH * e + b
                if b == 0:
                    act.wait_ge(gates_biased, 16 * (e + 1))
                act.wait_ge(gate_ready, t + 1)
                wait(act, glu_done, t)
                for m in range(DC):
                    ins = nc.scalar.activation(SG[:, m, :], gate_ps[:, m, :], ACT.Silu, bias=b_gate[:, m:m + 1])
                ins.then_inc(silu_done, 1)

            def glu_high(e, b):
                t = BATCH * e + b
                act.wait_ge(glu_done, t + 1)
                wait(act, down_ready, t - 1)
                nc.scalar.activation(GH[:, b % 2], G[:], ACT.Copy).then_inc(glu_hi, 1)

            def steps(e, first, last):
                for b in range(BATCH):
                    before = (e, b - 1) if b >= 1 else (e - 1, BATCH - 1)
                    copy_up(e, b)
                    if b == 3 and not last:
                        high("up", e + 1)
                    if b >= 1 or not first:
                        silu(*before)
                    if b == 0:
                        high("gate", e)
                        if first:
                            for i, n in enumerate((4, 5)):
                                act.wait_ge(expd, i + 1)
                                nc.scalar.activation(r1[n][:], r1[n][:], ACT.Exp).then_inc(chain, 1)
                    if b >= 1 or not first:
                        glu_high(*before)
                    if b == 1:
                        high("down", e)
            high("up", 0)
            steps(0, True, False)
            with act.Fori(1, EXPERTS - 1) as e:
                steps(e, False, False)
            steps(EXPERTS - 1, False, True)
            silu(EXPERTS - 1, BATCH - 1)
            glu_high(EXPERTS - 1, BATCH - 1)
            for b in range(BATCH):
                act.wait_ge(added, BATCH * (EXPERTS - 1) + b + 1)
                sl = acc[:, :, b * SEQ:(b + 1) * SEQ]
                nc.scalar.activation(sl, sl, ACT.Silu).then_inc(gated, 1)

        @block.vector
        def _(dve):
            V = nc.vector
            links = [0]

            def link(ins):
                links[0] += 1
                ins.then_inc(lanes, 1)
                dve.wait_ge(lanes, links[0])
            wide = lambda row: row[:].unsqueeze(2).to_broadcast([P, TT, EXPERTS])
            every = lambda v: v[:].unsqueeze(1).to_broadcast([P, TT, v.shape[1]])
            logits, select, pick1, pick2, tmp, probs = rt
            top, place, g1, g2, e1, e2, both, inv = r1
            def up_low(e, b):
                t = BATCH * e + b
                dve.wait_ge(up_hi, t + 1)
                V.tensor_tensor(UL[:, b % 2], U[:, b % 2], plain(UH[:, b % 2]), ALU.subtract).then_inc(up_lo, 1)

            def scale(e, b):
                t = BATCH * e + b
                dve.wait_ge(prob_bcast[b], 16 * (e + 1))
                wait(dve, glu_done, t)
                V.tensor_tensor(UP[:], U[:, b % 2], prob_b[:, b, :].unsqueeze(1).to_broadcast([P, DC, SEQ]),
                                ALU.mult).then_inc(scaled, 1)

            def glu(e, b):
                t = BATCH * e + b
                dve.wait_ge(scaled, t + 1)
                dve.wait_ge(silu_done, t + 1)
                wait(dve, glu_lo, t)
                V.tensor_tensor(G[:], UP[:], SG[:], ALU.mult).then_inc(glu_done, 1)

            def glu_low(e, b):
                t = BATCH * e + b
                dve.wait_ge(glu_hi, t + 1)
                V.tensor_tensor(GL[:, b % 2], G[:], plain(GH[:, b % 2]), ALU.subtract).then_inc(glu_lo, 1)

            def accumulate(e, b):
                dve.wait_ge(down_ready, BATCH * e + b + 1)
                wait(dve, added, BATCH * e + b - 1)
                sl = acc[:, :, b * SEQ:(b + 1) * SEQ]
                V.tensor_tensor(sl, sl, down_ps[:], ALU.add).then_inc(added, 1)

            def look_up(chunk, v):
                cols = at(chunk, LUT_CHUNK)
                wait(dve, lut_added, chunk * (LUT - 1) + (max(v - HITS, 1) if v >= HITS else v - HITS + 1))
                V.tensor_scalar(hit[:, v % HITS, :], index[:, cols], float(v), table[:, v:v + 1],
                                ALU.is_equal, ALU.mult).then_inc(lut_hit, 1)

            def steps(e, first):
                for b in range(BATCH):
                    before = (e, b - 1) if b >= 1 else (e - 1, BATCH - 1)
                    v = b * LUT // BATCH
                    if b >= 1 or not first:
                        up_low(e, b)
                        glu(*before)
                    scale(e, b)
                    look_up(e, v)
                    look_up(e, v + 1)
                    if b >= 2 or not first:
                        accumulate(*((e, b - 2) if b >= 2 else (e - 1, b + BATCH - 2)))
                    if b >= 1 or not first:
                        glu_low(*before)
                    look_up(e, v + 2)
                    look_up(e, v + 3)
            up_low(0, 0)
            dve.wait_ge(loaded, LOADS)
            dve.wait_ge(routed, 1)
            link(V.memset(select[:], -BIG))
            link(V.memset(logits[:], 0.0))
            link(V.tensor_tensor(logits[:, :, 0:ROUTED], route_ps[:, :, 0:ROUTED], every(b_route), ALU.add))
            link(V.tensor_tensor(select[:, :, 0:ROUTED], logits[:, :, 0:ROUTED], every(b_select), ALU.add))
            for pick in (pick1, pick2):
                link(V.tensor_reduce(top[:], select[:], AX.X, ALU.max))
                link(V.tensor_tensor(tmp[:], select[:], wide(top), ALU.is_equal))
                link(V.tensor_tensor(tmp[:], tmp[:], every(lane), ALU.mult))
                link(V.tensor_reduce(place[:], tmp[:], AX.X, ALU.max))
                link(V.tensor_tensor(pick[:], tmp[:], wide(place), ALU.is_equal))
                link(V.scalar_tensor_tensor(out=select[:], in0=pick[:], scalar=-BIG, in1=select[:],
                                            op0=ALU.mult, op1=ALU.add))
            for pick, g in ((pick1, g1), (pick2, g2)):
                link(V.tensor_tensor(tmp[:], pick[:], logits[:], ALU.mult))
                link(V.tensor_reduce(g[:], tmp[:], AX.X, ALU.add))
            link(V.tensor_tensor(both[:], g1[:], g2[:], ALU.max))
            V.tensor_tensor(e1[:], g1[:], both[:], ALU.subtract).then_inc(expd, 1)
            V.tensor_tensor(e2[:], g2[:], both[:], ALU.subtract).then_inc(expd, 1)
            dve.wait_ge(chain, 2)
            link(V.tensor_tensor(both[:], e1[:], e2[:], ALU.add))
            link(V.reciprocal(inv[:], both[:]))
            for pick, e in ((pick1, e1), (pick2, e2)):
                link(V.tensor_tensor(e[:], e[:], inv[:], ALU.mult))
                link(V.tensor_tensor(pick[:], pick[:], wide(e), ALU.mult))
            link(V.tensor_tensor(probs[:], pick1[:], pick2[:], ALU.add))
            V.memset(probs[:, :, ROUTED:EXPERTS], 1.0).then_inc(prob_ready, 1)
            dve.wait_ge(zeroed, 2)
            for b in range(BATCH):
                dve.wait_ge(turned, b + 1)
                V.tensor_copy(probT[0:EXPERTS, b * SEQ:(b + 1) * SEQ], turn_ps[:]).then_inc(turn_copied, 1)
            steps(0, True)
            with dve.Fori(1, EXPERTS) as e:
                steps(e, False)
            glu(EXPERTS - 1, BATCH - 1)
            glu_low(EXPERTS - 1, BATCH - 1)
            accumulate(EXPERTS - 1, BATCH - 2)
            accumulate(EXPERTS - 1, BATCH - 1)
    nc.clear_and_free_semaphores(sems)
    nc.all_engine_barrier()


def lut_ffn(nc, shared, XH, XL, ones, x_src, lut_dram, gate):
    PARTS = 3
    COLS = LUT_COLS // PARTS
    with ExitStack() as k:
        def sem(n):
            return k.enter_context(nc.semaphore(f"ffn_{n}"))

        def sb(n, shape, dt=F32):
            return k.enter_context(nc.sbuf_tensor(f"ffn_{n}", shape, dt))
        raw = shared[:, DC * T:DC * T + LUT_COLS]
        WH, WL = sb("WH", [P, LUT_COLS], F32R), sb("WL", [P, LUT_COLS], F32R)
        HF, HH, HL = sb("HF", [P, 2, SEQ]), sb("HH", [P, IT, SEQ], F32R), sb("HL", [P, IT, SEQ], F32R)
        SG, GO = sb("SG", [P, 2, SEQ]), sb("out", [P, DC, SEQ])
        w_hi, w_lo, g_ready, u_ready, silu_done, h_done, h_hi, h_lo, d_ready, gated, stored = map(
            sem, "w_hi w_lo g_ready u_ready silu_done h_done h_hi h_lo d_ready gated stored".split())
        loaded = [sem(f"loaded{i}") for i in range(PARTS)]
        part = lambda t, i: t[:, i * COLS:(i + 1) * COLS]
        chunk = lambda t, i, n: part(t, i).rearrange("p (c n) -> p c n", c=n)

        def ahead(sp):
            for i in range(PARTS):
                sp.dma_start(part(raw, i), part(lut_dram, i)).then_inc(loaded[i], 16)
        layernorm(nc, shared, XH, XL, ones, x_src, "ln1", ahead)
        g_ps = k.enter_context(nc.psum_tensor("ffn_g_ps", [P, 2, SEQ], F32))
        u_ps = k.enter_context(nc.psum_tensor("ffn_u_ps", [P, 2, SEQ], F32))
        d_ps = k.enter_context(nc.psum_tensor("ffn_d_ps", [P, DC, SEQ], F32))
        block = k.enter_context(nc.Block())

        @block.tensor
        def _(pe):
            def up(b, m):
                i = IT * b + m
                wait(pe, h_done, i - 1)
                cols = slice(m * P, (m + 1) * P)
                for w, o, s in ((0, g_ps, g_ready), (1, u_ps, u_ready)):
                    if isinstance(b, int) and m == 0:
                        pe.wait_ge(w_lo, w + 1)
                    wh, wl = chunk(WH, w, DC), chunk(WL, w, DC)
                    for c in range(DC):
                        mm = matmul3(nc, o[:, m % 2, :], wh[:, c, cols], wl[:, c, cols], XH[:, c, at(b, SEQ)],
                                     XL[:, c, at(b, SEQ)], c == 0, c == DC - 1)
                    mm.then_inc(s, 1)

            def batch(b):
                wh, wl = chunk(WH, 2, IT), chunk(WL, 2, IT)
                for m in range(IT):
                    up(b, m)
                wait(pe, gated, b)
                if isinstance(b, int):
                    pe.wait_ge(w_lo, PARTS)
                for c in range(IT):
                    pe.wait_ge(h_lo, IT * b + c + 1)
                    for m in range(DC):
                        cols = slice(m * P, (m + 1) * P)
                        mm = matmul3(nc, d_ps[:, m, :], wh[:, c, cols], wl[:, c, cols], HH[:, c, :], HL[:, c, :],
                                     c == 0, c == IT - 1)
                mm.then_inc(d_ready, 1)
            batch(0)
            with pe.Fori(1, BATCH) as b:
                batch(b)

        @block.scalar
        def _(act):
            for i in range(PARTS):
                act.wait_ge(loaded[i], 16)
                nc.scalar.activation(part(WH, i), part(raw, i), ACT.Copy).then_inc(w_hi, 1)

            def high(b, m):
                i = IT * b + m
                act.wait_ge(h_done, i + 1)
                nc.scalar.activation(HH[:, m, :], HF[:, m % 2, :], ACT.Copy).then_inc(h_hi, 1)

            def batch(b):
                for m in range(IT):
                    i = IT * b + m
                    act.wait_ge(g_ready, i + 1)
                    wait(act, h_done, i - 1)
                    nc.scalar.activation(SG[:, m % 2, :], g_ps[:, m % 2, :], ACT.Silu).then_inc(silu_done, 1)
                    if m == 1:
                        wait(act, d_ready, b)
                    if m >= 1:
                        high(b, m - 1)
                high(b, IT - 1)
                act.wait_ge(d_ready, b + 1)
                wait(act, stored, 16 * b)
                nc.scalar.activation(GO[:], d_ps[:], ACT.Silu).then_inc(gated, 1)
            batch(0)
            with act.Fori(1, BATCH) as b:
                batch(b)

        @block.vector
        def _(dve):
            for i in range(PARTS):
                dve.wait_ge(w_hi, i + 1)
                nc.vector.tensor_tensor(part(WL, i), part(raw, i), plain(part(WH, i)), ALU.subtract).then_inc(w_lo, 1)

            def low(b, m):
                i = IT * b + m
                dve.wait_ge(h_hi, i + 1)
                nc.vector.tensor_tensor(HL[:, m, :], HF[:, m % 2, :], plain(HH[:, m, :]), ALU.subtract).then_inc(h_lo, 1)

            def batch(b):
                for m in range(IT):
                    i = IT * b + m
                    dve.wait_ge(silu_done, i + 1)
                    dve.wait_ge(u_ready, i + 1)
                    wait(dve, h_lo, i - 1)
                    nc.vector.tensor_tensor(HF[:, m % 2, :], SG[:, m % 2, :], u_ps[:, m % 2, :], ALU.mult).then_inc(h_done, 1)
                    if m >= 1:
                        low(b, m - 1)
                low(b, IT - 1)
            batch(0)
            with dve.Fori(1, BATCH) as b:
                batch(b)

        @block.sync
        def _(sp):
            with sp.Fori(0, BATCH) as b:
                sp.wait_ge(gated, b + 1)
                sp.dma_start(gate[:, :, at(b, SEQ)], GO[:]).then_inc(stored, 16)
            sp.wait_ge(stored, 16 * BATCH)


def attention(nc, a, layer, shared, XH, XL, ident, ident_b, mask_b, ones, x_src, gate, x_dst):
    with ExitStack() as k:
        def sb(n, shape, dt=F32):
            return k.enter_context(nc.sbuf_tensor(f"at{layer}_{n}", shape, dt))
        st = {
            "QH": XH if layer else sb("latent_q_hi", [P, 1, T], F32R), "QL": XL if layer else sb("latent_q_lo", [P, 1, T], F32R),
            "KE": sb("KE", [P, BATCH, SEQ]), "KO": sb("KO", [P, BATCH, SEQ]),
            "V": sb("V", [P, BATCH * QT, LAT]),
            "OL": shared[:].rearrange("p (k t) -> p k t", k=PAIRS),
            "WVO": sb("WVO", [P, PAIRS, D]),
            "cos": sb("cos", [P, SEQ]), "sin": sb("sin", [P, SEQ]),
        }
        latents(nc, a, layer, XH, XL, ident, ones, st)
        heads(nc, a, layer, XH, XL, ident, ident_b, mask_b, st)
        project(nc, layer, st, x_src, gate, x_dst)


def latents(nc, a, layer, XH, XL, ident, ones, st):
    n = f"lat{layer}"
    KQ = layer + 1
    with ExitStack() as k:
        def sem(x):
            return k.enter_context(nc.semaphore(f"{n}_{x}"))

        def sb(x, shape, dt=F32):
            return k.enter_context(nc.sbuf_tensor(f"{n}_{x}", shape, dt))

        def ps(x, shape):
            return k.enter_context(nc.psum_tensor(f"{n}_{x}", shape, F32))
        w = sb("w", [P, 2, DC, KQ * P])
        WH, WL = sb("WH", [P, 2, DC, KQ * P], F32R), sb("WL", [P, 2, DC, KQ * P], F32R)
        CQ, CK = st["OL"][:, 0:KQ, :], st["OL"][:, KQ, :]
        normw = sb("normw", [P, KQ + 1])
        KV, RM, RS = sb("KV", [P, SEQ]), sb("RM", [P, SEQ]), sb("RS", [P, SEQ])
        SQ, logs, rstd = sb("SQ", [P, 3, SEQ]), sb("logs", [P, 2, SEQ]), sb("rstd", [P, 2, SEQ])
        eps = sb("eps", [P, 1])
        q_ps, k_ps, v_ps = ps("q_ps", [P, KQ, SEQ]), ps("k_ps", [P, KQ, SEQ]), ps("v_ps", [P, SEQ])
        m_ps = ps("m_ps", [P, 2, SEQ])
        (loaded, has_eps, q_ready, k_ready, raw_q, raw_k, q_done, squared, sums_ready, logs_ready, rstd_ready, kv_ready,
         k_done, roped, rope_done, v_ready, v_done, w_hi, w_lo, q_hi, q_lo, scaled) = map(sem, (
             "loaded has_eps q_ready k_ready raw_q raw_k q_done squared sums_ready logs_ready rstd_ready kv_ready "
             "k_done roped rope_done v_ready v_done w_hi w_lo q_hi q_lo scaled").split())
        KE, KO, QH, QL, V = (st[x] for x in ("KE", "KO", "QH", "QL", "V"))
        LOADS = 16 * (4 + layer)
        block = k.enter_context(nc.Block())

        @block.sync
        def _(sp):
            sp.dma_start(w[:, 0], a[f"wq_down{layer}"]).then_inc(loaded, 16)
            sp.dma_start(w[:, 1], a[f"wkv_down{layer}"]).then_inc(loaded, 16)
            sp.dma_start(st["cos"][:], a[f"cos{layer}"]).then_inc(loaded, 16)
            sp.dma_start(st["sin"][:], a[f"sin{layer}"]).then_inc(loaded, 16)
            if layer == 1:
                sp.dma_start(normw[:], a["norm_w1"]).then_inc(loaded, 16)

        @block.tensor
        def _(pe):
            pe.wait_ge(w_lo, 1)

            def product(out, n, b):
                for m in range(KQ):
                    for c in range(DC):
                        cols = slice(m * P, (m + 1) * P)
                        mm = matmul3(nc, out[:, m, :], WH[:, n, c, cols], WL[:, n, c, cols], XH[:, c, at(b, SEQ)],
                                     XL[:, c, at(b, SEQ)], c == 0, c == DC - 1)
                return mm

            def queries(b):
                wait(pe, raw_q if layer else q_done, b)
                product(q_ps, 0, b).then_inc(q_ready, 1)

            def keys(b):
                wait(pe, raw_k if layer else kv_ready, b)
                wait(pe, roped, 2 * b * layer)
                product(k_ps, 1, b).then_inc(k_ready, 1)

            def sums(b):
                wait(pe, logs_ready, b)
                pe.wait_ge(squared, b + 1)
                for c in range(KQ):
                    nc.tensor.matmul(m_ps[:, 0, :], ones[:], SQ[:, c, :], start=c == 0, stop=c == KQ - 1)
                nc.tensor.matmul(m_ps[:, 1, :], ones[:], SQ[:, KQ, :], start=True, stop=True).then_inc(sums_ready, 1)

            def turn(b):
                pe.wait_ge(kv_ready, b + 1)
                wait(pe, v_done, b)
                for t in range(QT):
                    mm = nc.tensor.transpose(v_ps[:, t * P:(t + 1) * P], KV[:, t * P:(t + 1) * P], ident[:])
                mm.then_inc(v_ready, 1)
            queries(0)
            keys(0)
            with pe.Fori(1, BATCH) as b:
                queries(b)
                if layer == 1:
                    sums(b - 1)
                keys(b)
                turn(b - 1)
            if layer == 1:
                sums(BATCH - 1)
            turn(BATCH - 1)

        @block.scalar
        def _(act):
            act.wait_ge(has_eps, 1)
            act.wait_ge(loaded, LOADS)
            nc.scalar.activation(WH[:], w[:], ACT.Copy).then_inc(w_hi, 1)

            def squares(b):
                act.wait_ge(raw_k, b + 1)
                wait(act, sums_ready, b)
                nc.scalar.activation(SQ[:, 0:KQ, :], CQ[:, :, at(b, SEQ)], ACT.Square)
                nc.scalar.activation(SQ[:, KQ, :], CK[:, at(b, SEQ)], ACT.Square).then_inc(squared, 1)

            def rstds(b):
                act.wait_ge(sums_ready, b + 1)
                nc.scalar.activation(logs[:, 0, :], m_ps[:, 0, :], ACT.Ln, bias=eps[:, 0:1], scale=1.0 / Q_RANK1)
                nc.scalar.activation(logs[:, 1, :], m_ps[:, 1, :], ACT.Ln, bias=eps[:, 0:1], scale=1.0 / P).then_inc(logs_ready, 1)
                act.wait_ge(logs_ready, b + 1)
                wait(act, kv_ready, b)
                nc.scalar.activation(rstd[:], logs[:], ACT.Exp, scale=-0.5).then_inc(rstd_ready, 1)

            def queries(b):
                if layer == 0:
                    act.wait_ge(q_ready, b + 1)
                    nc.scalar.activation(QH[:, 0, at(b, SEQ)], q_ps[:, 0, :], ACT.Copy, scale=HD0 ** -0.5).then_inc(q_hi, 1)
                else:
                    act.wait_ge(q_done, b + 1)
                    nc.scalar.activation(QH[:, :, at(b, SEQ)], CQ[:, :, at(b, SEQ)], ACT.Copy).then_inc(q_hi, 1)

            def keys(b):
                act.wait_ge(kv_ready, b + 1)
                nc.scalar.activation(KE[0:LAT, only(b), :], KV[0:LAT, :], ACT.Copy)
                nc.scalar.activation(KO[LAT:P, only(b), :], KV[LAT:P, :], ACT.Copy).then_inc(k_done, 1)

            def values(b):
                act.wait_ge(v_ready, b + 1)
                nc.scalar.activation(V[:, at(b, QT), :], v_ps[:].rearrange("p (t n) -> p t n", t=QT)[:, :, 0:LAT], ACT.Copy).then_inc(v_done, 1)

            def finish(b):
                if layer == 1:
                    rstds(b)
                    queries(b)
                keys(b)
            if layer == 1:
                squares(0)
            else:
                queries(0)
            with act.Fori(1, BATCH) as b:
                finish(b - 1)
                if layer == 1:
                    squares(b)
                else:
                    queries(b)
                values(b - 1)
            finish(BATCH - 1)
            values(BATCH - 1)

        @block.vector
        def _(dve):
            nc.vector.memset(eps[:], RMS_EPS).then_inc(has_eps, 1)
            dve.wait_ge(loaded, LOADS)
            if layer == 1:
                nc.vector.tensor_scalar(normw[:, 0:KQ], normw[:, 0:KQ], QK1 ** -0.5, None, ALU.mult).then_inc(scaled, 1)
            dve.wait_ge(w_hi, 1)
            nc.vector.tensor_tensor(WL[:], w[:], plain(WH[:]), ALU.subtract).then_inc(w_lo, 1)

            def batch0(b):
                wait(dve, v_ready, b)
                wait(dve, k_done, b)
                dve.wait_ge(q_hi, b + 1)
                nc.vector.scalar_tensor_tensor(out=QL[:, 0, at(b, SEQ)], in0=q_ps[:, 0, :], scalar=HD0 ** -0.5,
                                               in1=plain(QH[:, 0, at(b, SEQ)]), op0=ALU.mult, op1=ALU.subtract).then_inc(q_done, 1)
                dve.wait_ge(k_ready, b + 1)
                nc.vector.tensor_copy(KV[:], k_ps[:, 0, :]).then_inc(kv_ready, 1)

            def raw(b):
                dve.wait_ge(q_ready, b + 1)
                nc.vector.tensor_copy(CQ[:, :, at(b, SEQ)], q_ps[:]).then_inc(raw_q, 1)
                dve.wait_ge(k_ready, b + 1)
                nc.vector.tensor_copy(CK[:, at(b, SEQ)], k_ps[:, 0, :]).then_inc(raw_k, 1)
                wait(dve, rope_done, 2 * b)
                nc.vector.tensor_tensor(RM[:], k_ps[:, 1, :], st["cos"][:], ALU.mult).then_inc(roped, 1)
                nc.vector.stream_shuffle(RS[:], k_ps[:, 1, :], SWAP).then_inc(roped, 1)

            def normalise(b):
                dve.wait_ge(rstd_ready, b + 1)
                for c in range(KQ):
                    cq = CQ[:, c, at(b, SEQ)]
                    ins = nc.vector.scalar_tensor_tensor(out=cq, in0=cq, scalar=normw[:, c:c + 1],
                                                         in1=rstd[:, 0, :], op0=ALU.mult, op1=ALU.mult)
                ins.then_inc(q_done, 1)
                wait(dve, v_ready, b)
                wait(dve, k_done, b)
                nc.vector.scalar_tensor_tensor(out=KV[:], in0=CK[:, at(b, SEQ)], scalar=normw[:, KQ:KQ + 1],
                                               in1=rstd[:, 1, :], op0=ALU.mult, op1=ALU.mult).then_inc(kv_ready, 1)

            def low(b):
                dve.wait_ge(q_hi, b + 1)
                nc.vector.tensor_tensor(QL[:, :, at(b, SEQ)], CQ[:, :, at(b, SEQ)], plain(QH[:, :, at(b, SEQ)]), ALU.subtract).then_inc(q_lo, 1)
            if layer == 0:
                batch0(0)
                with dve.Fori(1, BATCH) as b:
                    batch0(b)
            else:
                raw(0)
                dve.wait_ge(scaled, 1)
                with dve.Fori(1, BATCH) as b:
                    normalise(b - 1)
                    raw(b)
                    low(b - 1)
                normalise(BATCH - 1)
                low(BATCH - 1)

        if layer == 1:
            @block.gpsimd
            def _(pool):
                pool.wait_ge(loaded, LOADS)
                turned = sem("turned")

                def batch(b):
                    pool.wait_ge(roped, 2 * b + 2)
                    wait(pool, rope_done, 2 * b)
                    nc.gpsimd.tensor_tensor(RS[:], RS[:], st["sin"][:], ALU.mult).then_inc(turned, 1)
                    pool.wait_ge(turned, b + 1)
                    nc.gpsimd.tensor_tensor(KE[LAT:P, only(b), :], RM[LAT:P, :], RS[LAT:P, :], ALU.add).then_inc(rope_done, 1)
                    nc.gpsimd.tensor_tensor(KO[0:LAT, only(b), :], RM[0:LAT, :], RS[0:LAT, :], ALU.add).then_inc(rope_done, 1)
                batch(0)
                with pool.Fori(1, BATCH) as b:
                    batch(b)


def heads(nc, a, layer, XH, XL, ident, ident_b, mask_b, st):
    n = f"hd{layer}"
    KQ = layer + 1
    stage = (STAGE0, STAGE1)[layer]
    FOLD, PLAIN = ("qn", "kn", "v", "o"), ("rope", "key") if layer == 0 else ("rope",)
    offset, width = {}, {}
    for group in (FOLD, PLAIN):
        at_ = 0
        for key in group:
            offset[key], at_ = at_, at_ + stage[key]
        width[group] = at_
    STEPS = 2 * BATCH
    KINDS = ("rope", "key") if layer == 0 else ("rope",)
    NK = len(KINDS)
    KE, KO, QH, QL, V, OL, WVO = (st[x] for x in ("KE", "KO", "QH", "QL", "V", "OL", "WVO"))
    with ExitStack() as k:
        def sem(x):
            return k.enter_context(nc.semaphore(f"{n}_{x}"))

        def sb(x, shape, dt=F32):
            return k.enter_context(nc.sbuf_tensor(f"{n}_{x}", shape, dt))

        def ps(x, shape):
            return k.enter_context(nc.psum_tensor(f"{n}_{x}", shape, F32))
        SF, SP_ = sb("stage_fold", [P, width[FOLD]]), sb("stage_plain", [P, width[PLAIN]])
        SH, SL = sb("plain_hi", [P, width[PLAIN]], F32R), sb("plain_lo", [P, width[PLAIN]], F32R)
        WNH, WNL = sb("w_latent_hi", [P, KQ, P], F32R), sb("w_latent_lo", [P, KQ, P], F32R)
        QE, QO = sb("QE", [P, 2, SEQ]), sb("QO", [P, 2, SEQ])
        RM, RS = sb("RM", [P, 2, SEQ]), sb("RS", [P, 2, SEQ])
        PR = sb("probs", [P, 2, QT * (QT + 1) // 2, P])
        PT = sb("probsT", [P, 2, QT, SEQ])
        NM, SM, RC = sb("negmax", [P, 2, QT]), sb("sums", [P, 2, QT]), sb("inv_sums", [P, 2, QT])
        s_ps = [ps(f"s_ps{i}", [P, SEQ]) for i in range(3)]
        t_ps = [ps(f"t_ps{i}", [P, SEQ]) for i in range(2)]
        o_ps = ps("o_ps", [P, SEQ])
        pj_ps = [ps(f"pj_ps{i}", [P, SEQ]) for i in range(2)]
        fold_staged, plain_staged, wabs_hi, plain_hi, plain_lo = map(
            sem, "fold_staged plain_staged wabs_hi plain_hi_done plain_lo_done".split())
        (wabs_ready, wvo_ready, wabs_copied, wvo_copied, qn_ready, qn_copied, rp_ready, rp_read, rp_mult,
         rp_done, s_ready, max_done, exp_done, inv_done, norm_done, t_ready, t_copied, o_ready, o_copied) = map(sem, (
             "wabs_ready wvo_ready wabs_copied wvo_copied qn_ready qn_copied rp_ready rp_read rp_mult "
             "rp_done s_ready max_done exp_done inv_done norm_done t_ready t_copied o_ready o_copied").split())

        def part(key, parts=1, of=None):
            v = (SF if of is None else of)[:, offset[key]:offset[key] + stage[key]]
            return v.rearrange("p (k n) -> p k n", k=parts) if parts > 1 else v
        tri = lambda i: i * (i + 1) // 2

        score_bank, score_col = (0, 0, 1, 2), (0, P, 0, 0)

        def score(i):
            return s_ps[score_bank[i]][:, score_col[i]:score_col[i] + (i + 1) * P]

        def drive(eng, prologue, body, epilogue):
            prologue()
            body(0, True, False)
            with eng.Fori(1, PAIRS - 1) as p:
                body(p, False, False)
            body(PAIRS - 1, False, True)
            epilogue()

        def back(p, g, lag):
            return (p, g - lag) if g >= lag else (p - 1, g - lag + STEPS)

        def next_batch(p, g):
            return (p, g // 2 + 1) if g < STEPS - 2 else (p + 1, 0)
        block = k.enter_context(nc.Block())

        @block.sync
        def _(sp):
            for p in range(PAIRS):
                wait(sp, wvo_ready, p)
                sp.dma_start(SF[:], a[f"fold{layer}"][p]).then_inc(fold_staged, 16)
                wait(sp, plain_lo, p)
                sp.dma_start(SP_[:], a[f"plain{layer}"][p]).then_inc(plain_staged, 16)

        @block.tensor
        def _(pe):
            def weights(p):
                pe.wait_ge(fold_staged, 16 * (p + 1))
                wait(pe, qn_copied, BATCH * p)
                wait(pe, rp_read, 2 * NK * BATCH * p)
                if layer == 0:
                    mm = nc.tensor.matmul(pj_ps[0][:, 0:P], part("qn"), part("kn"), start=True, stop=True)
                else:
                    qn, kn = part("qn", 2 * KQ), part("kn", 2)
                    for c in range(KQ):
                        for e in range(2):
                            mm = nc.tensor.matmul(pj_ps[0][:, c * P + e * LAT:c * P + (e + 1) * LAT], qn[:, KQ * e + c, :],
                                                  kn[:, e, :], start=True, stop=True)
                mm.then_inc(wabs_ready, 1)
                v, o = part("v", 2), part("o", 2)
                for e in range(2):
                    mm = nc.tensor.matmul(pj_ps[1][e * LAT:(e + 1) * LAT, 0:D], v[:, e, :], o[:, e, :], start=True, stop=True)
                mm.then_inc(wvo_ready, 1)

            def queries(p, b):
                m = BATCH * p + b
                if b == 0:
                    pe.wait_ge(wabs_copied, p + 1)
                wait(pe, rp_read, 2 * NK * m)
                wait(pe, qn_copied, m)
                sl = slice(b * SEQ, (b + 1) * SEQ)
                for c in range(KQ):
                    mm = matmul3(nc, pj_ps[0][:], WNH[:, c, :], WNL[:, c, :], QH[:, c, sl], QL[:, c, sl], c == 0, c == KQ - 1)
                mm.then_inc(qn_ready, 1)
                if b == 0:
                    pe.wait_ge(wvo_copied, p + 1)
                    pe.wait_ge(plain_lo, p + 1)
                for c in range(KQ):
                    o = offset["rope"] + c * P
                    mm = matmul3(nc, pj_ps[1][:], SH[:, o:o + P], SL[:, o:o + P], QH[:, c, sl], QL[:, c, sl], c == 0, c == KQ - 1)
                mm.then_inc(rp_ready, 1)

            def keys(p, b):
                pe.wait_ge(qn_copied, BATCH * p + b + 1)
                sl = slice(b * SEQ, (b + 1) * SEQ)
                for c in range(DC):
                    o = offset["key"] + c * P
                    mm = matmul3(nc, pj_ps[0][:], SH[:, o:o + P], SL[:, o:o + P], XH[:, c, sl], XL[:, c, sl], c == 0, c == DC - 1)
                mm.then_inc(rp_ready, 1)

            def scores(p, g, i):
                b, e = g // 2, g % 2
                if i == 0 and e == 0:
                    pe.wait_ge(qn_copied, BATCH * p + b + 1)
                    pe.wait_ge(rp_done, 2 * NK * (BATCH * p + b + 1))
                if i != 1:
                    wait(pe, exp_done, QT * (STEPS * p + g - 1) + (2, 2, 3, 4)[i])
                q, kk = (QO, KO) if e else (QE, KE)
                s = score(i)
                nc.tensor.matmul(s, q[:, b % 2, i * P:(i + 1) * P], kk[:, b, 0:(i + 1) * P], start=True, stop=False)
                nc.tensor.matmul(s[:, i * P:(i + 1) * P], ident_b[:], mask_b[:], start=False, stop=True).then_inc(s_ready, 1)

            def turn(p, g, i):
                h = STEPS * p + g
                pe.wait_ge(norm_done, QT * h + i + 1)
                wait(pe, t_copied, QT * h + i - 1)
                for j in range(i + 1):
                    mm = nc.tensor.transpose(t_ps[i % 2][:, j * P:(j + 1) * P], PR[:, g % 2, tri(i) + j, :], ident[:])
                mm.then_inc(t_ready, 1)

            def values(p, b):
                m = BATCH * p + b
                pe.wait_ge(t_copied, 2 * QT * (m + 1))
                wait(pe, o_copied, m)
                for j in range(QT):
                    for e in range(2):
                        mm = nc.tensor.matmul(o_ps[e * LAT:(e + 1) * LAT, j * P:SEQ], V[:, b * QT + j, :],
                                              PT[:, e, j, j * P:SEQ], start=j == 0, stop=j == QT - 1)
                mm.then_inc(o_ready, 1)

            def body(p, first, last):
                for g in range(STEPS):
                    before = not (first and g < 1)
                    ahead = g % 2 == 0 and not (last and g == STEPS - 2)
                    for i in range(3):
                        scores(p, g, i)
                    if ahead:
                        queries(*next_batch(p, g))
                    if g % 2 == 1 and not (first and g < 2):
                        values(*((p, g // 2 - 1) if g >= 2 else (p - 1, BATCH - 1)))
                    if before:
                        turn(*back(p, g, 1), 0)
                        turn(*back(p, g, 1), 1)
                    if ahead and layer == 0:
                        keys(*next_batch(p, g))
                    scores(p, g, 3)
                    if before:
                        turn(*back(p, g, 1), 2)
                        turn(*back(p, g, 1), 3)
                    if g == 5 and not last:
                        weights(p + 1)

            def prologue():
                weights(0)
                queries(0, 0)
                if layer == 0:
                    keys(0, 0)

            def epilogue():
                for i in range(QT):
                    turn(PAIRS - 1, STEPS - 1, i)
                values(PAIRS - 1, BATCH - 1)
            drive(pe, prologue, body, epilogue)

        @block.scalar
        def _(act):
            def weights(p):
                act.wait_ge(wabs_ready, p + 1)
                nc.scalar.activation(WNH[:], pj_ps[0][:, 0:KQ * P].rearrange("p (c n) -> p c n", c=KQ), ACT.Copy).then_inc(wabs_hi, 1)
                act.wait_ge(plain_staged, 16 * (p + 1))
                wait(act, rp_ready, NK * BATCH * p)
                nc.scalar.activation(SH[:], SP_[:], ACT.Copy).then_inc(plain_hi, 1)

            def queries(p, b):
                act.wait_ge(qn_ready, BATCH * p + b + 1)
                nc.scalar.activation(QE[0:LAT, b % 2, :], pj_ps[0][0:LAT, :], ACT.Copy)
                nc.scalar.activation(QO[LAT:P, b % 2, :], pj_ps[0][LAT:P, :], ACT.Copy).then_inc(qn_copied, 1)

            def exps(p, g, i):
                h = STEPS * p + g
                act.wait_ge(max_done, QT * h + max(i, 1) + 1)
                wait(act, t_ready, QT * (h - 1))
                nc.scalar.activation(PR[:, g % 2, tri(i):tri(i + 1), :], score(i)
                                     .rearrange("p (j n) -> p j n", j=i + 1), ACT.Exp,
                                     bias=NM[:, g % 2, i:i + 1], accum_out=SM[:, g % 2, i:i + 1]).then_inc(exp_done, 1)

            def copy_turned(p, g, i):
                h = STEPS * p + g
                act.wait_ge(t_ready, QT * h + i + 1)
                wait(act, o_ready, BATCH * p + g // 2)
                nc.scalar.activation(PT[:, g % 2, 0:i + 1, i * P:(i + 1) * P],
                                     t_ps[i % 2][:, 0:(i + 1) * P].rearrange("p (j n) -> p j n", j=i + 1), ACT.Copy).then_inc(t_copied, 1)

            def body(p, first, last):
                for g in range(STEPS):
                    before = not (first and g < 1)
                    exps(p, g, 0)
                    exps(p, g, 1)
                    if g % 2 == 0 and not (last and g == STEPS - 2):
                        queries(*next_batch(p, g))
                    exps(p, g, 2)
                    if before:
                        for i in range(QT):
                            copy_turned(*back(p, g, 1), i)
                    exps(p, g, 3)
                    if g == 5 and not last:
                        weights(p + 1)

            def prologue():
                weights(0)
                queries(0, 0)

            def epilogue():
                for i in range(QT):
                    copy_turned(PAIRS - 1, STEPS - 1, i)
            drive(act, prologue, body, epilogue)

        @block.vector
        def _(dve):
            def weights(p):
                dve.wait_ge(wvo_ready, p + 1)
                dst = WVO[:, p, :] if isinstance(p, int) else WVO[:, bass.ds(p, 1), :]
                nc.vector.tensor_copy(dst, pj_ps[1][:, 0:D]).then_inc(wvo_copied, 1)
                dve.wait_ge(wabs_hi, p + 1)
                nc.vector.tensor_tensor(WNL[:], pj_ps[0][:, 0:KQ * P].rearrange("p (c n) -> p c n", c=KQ), plain(WNH[:]),
                                        ALU.subtract).then_inc(wabs_copied, 1)
                dve.wait_ge(plain_hi, p + 1)
                nc.vector.tensor_tensor(SL[:], SP_[:], plain(SH[:]), ALU.subtract).then_inc(plain_lo, 1)

            def queries(p, b):
                m = BATCH * p + b
                for n_, kind in enumerate(KINDS):
                    r = NK * m + n_
                    buf = n_ if layer == 0 else b % 2
                    src = pj_ps[1 - n_]
                    dve.wait_ge(rp_ready, r + 1)
                    wait(dve, rp_done, 2 * (r - 1))
                    nc.vector.tensor_tensor(RM[:, buf, :], src[:], st["cos"][:], ALU.mult).then_inc(rp_read, 1)
                    nc.vector.stream_shuffle(RS[:, buf, :], src[:], SWAP).then_inc(rp_read, 1)

            def maxes(p, g, i):
                h = STEPS * p + g
                dve.wait_ge(s_ready, QT * h + max(i, 1) + 1)
                wait(dve, exp_done, QT * (h - 1))
                nc.vector.tensor_reduce(NM[:, g % 2, i:i + 1], score(i), AX.X,
                                        ALU.max, negate=True).then_inc(max_done, 1)

            def normalise(p, g):
                h = STEPS * p + g
                dve.wait_ge(exp_done, QT * (h + 1))
                nc.vector.reciprocal(RC[:, g % 2, :], SM[:, g % 2, :]).then_inc(inv_done, 1)
                dve.wait_ge(inv_done, h + 1)
                for i in range(QT):
                    sl = PR[:, g % 2, tri(i):tri(i + 1), :]
                    nc.vector.tensor_scalar(sl, sl, RC[:, g % 2, i:i + 1], None, ALU.mult).then_inc(norm_done, 1)

            def copy_out(p, b):
                dve.wait_ge(o_ready, BATCH * p + b + 1)
                nc.vector.tensor_copy(OL[:, only(p), b * SEQ:(b + 1) * SEQ], o_ps[:]).then_inc(o_copied, 1)

            def body(p, first, last):
                for g in range(STEPS):
                    for i in range(3):
                        maxes(p, g, i)
                    if not (first and g < 1):
                        normalise(*back(p, g, 1))
                    if g % 2 == 0 and not (last and g == STEPS - 2):
                        queries(*next_batch(p, g))
                    maxes(p, g, 3)
                    if g % 2 == 1 and not (first and g < 2):
                        copy_out(*((p, g // 2 - 1) if g >= 2 else (p - 1, BATCH - 1)))
                    if g == 5 and not last:
                        weights(p + 1)

            def prologue():
                weights(0)
                queries(0, 0)

            def epilogue():
                normalise(PAIRS - 1, STEPS - 1)
                copy_out(PAIRS - 1, BATCH - 1)
            drive(dve, prologue, body, epilogue)

        @block.gpsimd
        def _(pool):
            def queries(p, b):
                m = BATCH * p + b
                for n_, kind in enumerate(KINDS):
                    r = NK * m + n_
                    buf = n_ if layer == 0 else b % 2
                    pool.wait_ge(rp_read, 2 * (r + 1))
                    wait(pool, rp_done, 2 * r)
                    nc.gpsimd.tensor_tensor(RS[:, buf, :], RS[:, buf, :], st["sin"][:], ALU.mult).then_inc(rp_mult, 1)
                    pool.wait_ge(rp_mult, r + 1)
                    for rows, q, kk in ((slice(LAT, P), QE, KE), (slice(0, LAT), QO, KO)):
                        dst = q[rows, b % 2, :] if kind == "rope" else kk[rows, b, :]
                        nc.gpsimd.tensor_tensor(dst, RM[rows, buf, :], RS[rows, buf, :], ALU.add).then_inc(rp_done, 1)
            for b in range(BATCH):
                queries(0, b)
            with pool.Fori(1, PAIRS) as p:
                for b in range(BATCH):
                    queries(p, b)


def project(nc, layer, st, x_src, gate, x_dst):
    n = f"pr{layer}"
    OL, WVO = st["OL"], st["WVO"]
    with ExitStack() as k:
        def sem(x):
            return k.enter_context(nc.semaphore(f"{n}_{x}"))

        def sb(x, shape, dt=F32):
            return k.enter_context(nc.sbuf_tensor(f"{n}_{x}", shape, dt))
        X, G = sb("x", [P, DC, SEQ]), sb("g", [P, DC, SEQ])
        WH, WL = sb("WH", [P, PAIRS, D], F32R), sb("WL", [P, PAIRS, D], F32R)
        OH, OLo = sb("OH", [P, PAIRS, SEQ], F32R), sb("OL", [P, PAIRS, SEQ], F32R)
        o_ps = k.enter_context(nc.psum_tensor(f"{n}_o_ps", [P, 2, DC, SEQ], F32))
        x_loaded, g_loaded, w_hi, w_lo, o_hi, o_lo, used, gated, added, stored = map(
            sem, "x_loaded g_loaded w_hi w_lo o_hi o_lo used gated added stored".split())
        block = k.enter_context(nc.Block())

        @block.sync
        def _(sp):
            def batch(b):
                wait(sp, added, b)
                sp.dma_start(X[:], x_src[:, :, at(b, SEQ)]).then_inc(x_loaded, 16)
                wait(sp, stored, 16 * b)
                sp.dma_start(G[:], gate[:, :, at(b, SEQ)]).then_inc(g_loaded, 16)
            batch(0)
            with sp.Fori(1, BATCH) as b:
                batch(b)
            sp.wait_ge(stored, 16 * BATCH)

        def paired(eng, batch):
            batch(0, 0)
            batch(1, 1)
            with eng.Fori(1, BATCH // 2) as two:
                batch(two * 2, 0)
                batch(two * 2 + 1, 1)

        @block.tensor
        def _(pe):
            def batch(b, half):
                wait(pe, gated, b - 1)
                for p in range(PAIRS):
                    if half == 0 and isinstance(b, int):
                        pe.wait_ge(w_lo, p + 1)
                    pe.wait_ge(o_lo, PAIRS * b + p + 1)
                    for m in range(DC):
                        cols = slice(m * P, (m + 1) * P)
                        mm = matmul3(nc, o_ps[:, half, m, :], WH[:, p, cols], WL[:, p, cols], OH[:, p, :], OLo[:, p, :],
                                     p == 0, p == PAIRS - 1)
                    mm.then_inc(used, 1)
            paired(pe, batch)

        @block.scalar
        def _(act):
            def batch(b):
                for p in range(PAIRS):
                    if isinstance(b, int):
                        nc.scalar.activation(WH[:, p, :], WVO[:, p, :], ACT.Copy).then_inc(w_hi, 1)
                    wait(act, used, PAIRS * (b - 1) + p + 1)
                    nc.scalar.activation(OH[:, p, :], OL[:, p, at(b, SEQ)], ACT.Copy).then_inc(o_hi, 1)
            batch(0)
            with act.Fori(1, BATCH) as b:
                batch(b)

        @block.gpsimd
        def _(pool):
            with pool.Fori(0, BATCH) as b:
                pool.wait_ge(added, b + 1)
                pool.dma_start(x_dst[:, :, at(b, SEQ)], G[:]).then_inc(stored, 16)
            pool.wait_ge(stored, 16 * BATCH)

        @block.vector
        def _(dve):
            def split(b):
                for p in range(PAIRS):
                    if isinstance(b, int) and b == 0:
                        dve.wait_ge(w_hi, p + 1)
                        nc.vector.tensor_tensor(WL[:, p, :], WVO[:, p, :], plain(WH[:, p, :]), ALU.subtract).then_inc(w_lo, 1)
                    dve.wait_ge(o_hi, PAIRS * b + p + 1)
                    nc.vector.tensor_tensor(OLo[:, p, :], OL[:, p, at(b, SEQ)], plain(OH[:, p, :]), ALU.subtract).then_inc(o_lo, 1)

            def combine(b, half):
                dve.wait_ge(g_loaded, 16 * (b + 1))
                dve.wait_ge(used, PAIRS * (b + 1))
                nc.vector.tensor_tensor(G[:], G[:], o_ps[:, half], ALU.mult).then_inc(gated, 1)
                dve.wait_ge(x_loaded, 16 * (b + 1))
                dve.wait_ge(gated, b + 1)
                nc.vector.tensor_tensor(G[:], G[:], X[:], ALU.add).then_inc(added, 1)

            def batch(b, half):
                split(b)
                if not isinstance(b, int) or b >= 1:
                    combine(b - 1, 1 - half)
            paired(dve, batch)
            combine(BATCH - 1, 1)


def rope_tables(inv_freq):
    angle = np.arange(SEQ, dtype=np.float32)[:, None] * inv_freq.astype(np.float32)[None, :]
    row = (np.arange(P) % ROPE) // 2
    sign = np.where(np.arange(P) % 2 == 0, -1.0, 1.0).astype(np.float32)[:, None]
    cos, sin = np.cos(angle).astype(np.float32).T[row], np.sin(angle).astype(np.float32).T[row] * sign
    return np.ascontiguousarray(cos), np.ascontiguousarray(sin)


def chunks(w):
    return np.ascontiguousarray(w.reshape(-1, P, w.shape[1]).transpose(1, 0, 2))


def pad_rows(w, n):
    return np.concatenate([w, np.zeros((n - w.shape[0],) + w.shape[1:], w.dtype)], 0)


def layouts(d):
    f = {}
    half = ROPE // 2
    f["xT"] = np.ascontiguousarray(d["L0_attn_x"].reshape(T, D).T)
    inv0 = (1.0 / 10000.0 ** (np.arange(half, dtype=np.float32) / np.float32(half))).astype(np.float32)
    inv1 = (1.0 / 500000.0 ** (np.arange(0, ROPE, 2, dtype=np.float32) / np.float32(ROPE))).astype(np.float32)
    f["cos0"], f["sin0"] = rope_tables(inv0)
    f["cos1"], f["sin1"] = rope_tables(inv1)
    stack = lambda r, s: np.concatenate([d[r], d[s][None]], 0)
    wide = lambda w: np.ascontiguousarray(w.reshape(EXPERTS, DC, P, D).transpose(0, 2, 1, 3))
    f["w_up"], f["w_gate"], f["w_down"] = (wide(stack(r, s)) for r, s in (
        ("L0_ffn_Wup", "L0_ffn_Wsu"), ("L0_ffn_Wgate", "L0_ffn_Wsg"), ("L0_ffn_Wdown", "L0_ffn_Wsd")))
    col = lambda v: np.ascontiguousarray(v.reshape(EXPERTS, DC, P).transpose(0, 2, 1))
    f["b_up"], f["b_gate"] = col(stack("L0_ffn_bup", "L0_ffn_bsu")), col(stack("L0_ffn_bgate", "L0_ffn_bsg"))
    f["b_down"] = pad_rows(stack("L0_ffn_bdown", "L0_ffn_bsd"), P)
    wr = np.zeros((D, EXPERTS), np.float32)
    wr[:, :ROUTED] = d["L0_ffn_Wr"]
    f["w_route"] = chunks(wr)
    f["b_route"], f["b_select"] = d["L0_ffn_br"][None], d["L0_ffn_gate_bias"][None]
    f["lane"] = np.arange(EXPERTS, 0, -1, dtype=np.float32)[None]
    def padded(i, rows, cols):
        o = np.full((rows, cols), LUT, np.int32)
        o[:i.shape[0], :i.shape[1]] = i
        return chunks(o).reshape(P, -1)
    f["index"] = np.concatenate([padded(d["L1_ffn_gate_idx"].T, D, INTER_PAD), padded(d["L1_ffn_up_idx"].T, D, INTER_PAD),
                                 padded(d["L1_ffn_down_idx"].T, INTER_PAD, D)], 1)
    f["lut"] = d["L1_ffn_lut"][None]
    mix = np.arange(ROPE).reshape(2, half).T.ravel()
    f["wq_down0"] = chunks(d["L0_attn_Wq_down"])
    f["wkv_down0"] = chunks(np.tile(d["L0_attn_Wkv_down"], (1, 2)))
    qn = d["L0_attn_Wq_up"].reshape(QR0, PAIRS, 2 * ND0).transpose(1, 2, 0)
    ku = d["L0_attn_Wk_up"].reshape(LAT, PAIRS, 2, ND0).transpose(1, 2, 3, 0)
    kn = np.zeros((PAIRS, 2, ND0, 2, LAT), np.float32)
    for e in range(2):
        kn[:, e, :, e] = ku[:, e]
    odd_first = lambda w: w.reshape(w.shape[0], PAIRS, 2, ROPE)[:, :, ::-1][..., mix].transpose(1, 0, 2, 3).reshape(PAIRS, w.shape[0], P)
    rope = odd_first(d["L0_attn_Wq_rope"])
    key = odd_first(d["L0_attn_Wk_rope"]).reshape(PAIRS, DC, P, P).transpose(0, 2, 1, 3)
    v = d["L0_attn_Wv_up"].reshape(LAT, PAIRS, 2, HD0).transpose(1, 3, 2, 0)
    o = d["L0_attn_Wo"].reshape(PAIRS, 2, HD0, D).transpose(0, 2, 1, 3)
    join = lambda *w: np.ascontiguousarray(np.concatenate([x.reshape(PAIRS, P, -1) for x in w], 2))
    f["fold0"], f["plain0"] = join(qn, kn.reshape(PAIRS, P, P), v, o), join(rope, key)
    f["wq_down1"] = chunks(pad_rows(d["L1_attn_w_q_down"], 2 * P).T)
    wkv = d["L1_attn_w_kv_down"]
    f["wkv_down1"] = chunks(np.concatenate([wkv[:LAT], wkv[:LAT], wkv[LAT:], wkv[LAT:]], 0).T)
    f["norm_w1"] = np.ascontiguousarray(np.concatenate([pad_rows(d["L1_attn_q_norm_w"], 2 * P),
                                                        d["L1_attn_kv_norm_w"], d["L1_attn_kv_norm_w"]]).reshape(3, P).T)
    wq = d["L1_attn_w_q_up"].reshape(PAIRS, 2, QK1, Q_RANK1)
    qr = np.zeros((PAIRS, 2, QK1, 2 * P), np.float32)
    qr[..., :Q_RANK1] = wq
    qn = qr[:, :, :NOPE1].transpose(0, 2, 1, 3)
    rope = qr[:, ::-1, NOPE1:].reshape(PAIRS, P, 2, P).transpose(0, 3, 2, 1)
    kvu = d["L1_attn_w_kv_up"].reshape(PAIRS, 2, NOPE1 + VD1, LAT)
    kn, v = kvu[:, :, :NOPE1].transpose(0, 2, 1, 3), kvu[:, :, NOPE1:].transpose(0, 2, 1, 3)
    o = d["L1_attn_w_o"].T.reshape(PAIRS, 2, VD1, D).transpose(0, 2, 1, 3)
    f["fold1"], f["plain1"] = join(qn, kn, v, o), join(rope)
    return f


def kernel(**inputs):
    import concourse.bacc as bacc
    from concourse.bass_utils import run_bass_kernel_spmd

    laid = layouts({name: np.asarray(v) for name, v in inputs.items()})
    nc = bacc.Bacc("TRN2", target_bir_lowering=False, num_devices=1)
    arrays, args = {}, {}
    for name, v in laid.items():
        v = np.ascontiguousarray(v)
        arrays[f"in_{name}"] = v
        args[name] = nc.dram_tensor(f"in_{name}", v.shape, mybir.dt.from_np(v.dtype), kind="ExternalInput").ap()
    out = nc.dram_tensor("outT", [D, T], F32, kind="ExternalOutput").ap()
    build(nc, args, out)
    r = run_bass_kernel_spmd(nc, [arrays], core_ids=[0])
    return np.ascontiguousarray(r.results[0]["outT"].T).reshape(BATCH, SEQ, D)
```
